# Optimizing a Trainium2 kernel written in Bass

```python
import numpy as np
import jax
import jax.numpy as jnp

def _softmax(x, axis=-1):
    return jax.nn.softmax(x, axis=axis)

def _gelu(x):
    return jax.nn.gelu(x, approximate=True)

def _silu(x):
    return jax.nn.silu(x)

def _sigmoid(x):
    return jax.nn.sigmoid(x)

def _layernorm(x, axis=-1, eps=1e-05):
    m = jnp.mean(x, axis=axis, keepdims=True)
    v = jnp.var(x, axis=axis, keepdims=True)
    return (x - m) / jnp.sqrt(v + eps)

def _scatter_add(tgt, idx, src, axis=0):
    return tgt.at[idx].add(src)

def _segment_sum(src, seg, n):
    return jax.ops.segment_sum(src, seg, n)
kernel_name = 'mk_decoder_postln_d2_seqx_r4_b2a90a'

def setup_inputs(seed: int=0):
    np.random.seed(seed)
    _w = jnp.asarray

    def _rec_inputs():
        import jax
        import jax.numpy as jnp
        _rk = jax.random.key(seed)
        x = -0.0002928 + 1 * jax.random.normal(jax.random.fold_in(_rk, 1), (4, 512, 256), jnp.float32)
        _lenS = 512 - jax.random.randint(jax.random.fold_in(_rk, 7), (4,), 0, max(1, 512 // 4) + 1, jnp.int32)
        _lenS2 = 64 - jax.random.randint(jax.random.fold_in(_rk, 8), (4,), 0, max(1, 64 // 4) + 1, jnp.int32)
        _ctx_1024P = jax.random.normal(jax.random.fold_in(_rk, 11), (4, 16, 256), jnp.float32)
        _ctx_1024c = jax.random.dirichlet(jax.random.fold_in(_rk, 511), 0.3 * jnp.ones((16,), jnp.float32), (4, 64))
        _ctx_1024t = jnp.einsum('bsk,bkd->bsd', _ctx_1024c, _ctx_1024P)
        _ctx_1024t = _ctx_1024t * jax.lax.rsqrt(jnp.mean(jnp.square(_ctx_1024t)) + 1e-12) * 0.953939
        ctx_1024 = -1.39393e-06 + 0.999914 * (_ctx_1024t + 0.3 * jax.random.normal(jax.random.fold_in(_rk, 611), (4, 64, 256), jnp.float32))
        _validS = jnp.arange(512)[None, :] < _lenS[:, None]
        _validS2 = jnp.arange(64)[None, :] < _lenS2[:, None]
        _causal = jnp.tril(jnp.ones((512, 512), dtype=bool))
        mask_Bx1xSxS2_bf0 = jnp.logical_not(jnp.ones((4, 1, 512, 64), dtype=bool))
        return (x, ctx_1024, mask_Bx1xSxS2_bf0)
    x, ctx_1024, mask_Bx1xSxS2_bf0 = _rec_inputs()

    def _L0_attn_setup():
        import jax, jax.numpy as jnp
        import numpy as np
        B, S, E = (4, 512, 256)
        HIDDEN = 256
        HEADS = 16
        key = jax.random.key(seed)
        k0, k1, k2, k3, k4 = jax.random.split(key, 5)
        inputs = jax.random.normal(k0, (B, S, E), dtype=jnp.float32)
        W_qkv = jax.random.normal(k1, (E, 3 * HIDDEN), dtype=jnp.float32) * 0.02
        b_qkv = jnp.zeros((3 * HIDDEN,), dtype=jnp.float32)
        W_out = jax.random.normal(k2, (HIDDEN, HIDDEN), dtype=jnp.float32) * 0.02
        b_out = jnp.zeros((HIDDEN,), dtype=jnp.float32)
        return {'inputs': inputs, 'W_qkv': W_qkv, 'b_qkv': b_qkv, 'W_out': W_out, 'b_out': b_out}
    _L0_attn_all = _L0_attn_setup()
    _L0_attn_in = {k: v for k, v in _L0_attn_all.items() if k in ('W_qkv', 'b_qkv', 'W_out', 'b_out')}
    del _L0_attn_all

    def _L0_xattn_setup():
        import jax, jax.numpy as jnp
        import numpy as np
        from math import sqrt
        B, L, D, H = (2, 512, 256, 16)
        DH = D // H

        def _split(x):
            b, l, _ = x.shape
            return x.reshape(b, l, H, DH).transpose(0, 2, 1, 3)
        key = jax.random.key(seed)
        ks = jax.random.split(key, 12)
        s = 1.0 / sqrt(D)
        inp = {'q': jax.random.normal(ks[0], (B, L, D), jnp.float32), 'k': jax.random.normal(ks[1], (B, L, D), jnp.float32), 'v': jax.random.normal(ks[2], (B, L, D), jnp.float32), 'mask': jnp.zeros((B, 1, L, L), dtype=bool), 'Wq': jax.random.normal(ks[3], (D, D), jnp.float32) * s, 'bq': jnp.zeros((D,), jnp.float32), 'Wk': jax.random.normal(ks[4], (D, D), jnp.float32) * s, 'bk': jnp.zeros((D,), jnp.float32), 'Wv': jax.random.normal(ks[5], (D, D), jnp.float32) * s, 'bv': jnp.zeros((D,), jnp.float32), 'Wo': jax.random.normal(ks[6], (D, D), jnp.float32) * s, 'bo': jnp.zeros((D,), jnp.float32)}
        return inp
    _L0_xattn_all = _L0_xattn_setup()
    _L0_xattn_in = {k: v for k, v in _L0_xattn_all.items() if k in ('Wq', 'bq', 'Wk', 'bk', 'Wv', 'bv', 'Wo', 'bo')}
    del _L0_xattn_all

    def _L0_ffn_setup():
        import jax, jax.numpy as jnp
        import numpy as np
        E = 8
        K = 2
        key = jax.random.key(seed)
        ks = jax.random.split(key, 8)
        B, T, d = (4, 512, 256)
        h = 4 * d // E
        s = 0.02
        X = jax.random.normal(ks[0], (B, T, d), jnp.float32)
        routing_W = jax.random.normal(ks[1], (E, d), jnp.float32) * s
        expert_bias = jnp.zeros((E,), jnp.float32)
        sW1 = jax.random.normal(ks[2], (d, h), jnp.float32) * s
        sb1 = jnp.zeros((h,), jnp.float32)
        sW2 = jax.random.normal(ks[3], (h, d), jnp.float32) * s
        sb2 = jnp.zeros((d,), jnp.float32)
        rW1 = jax.random.normal(ks[4], (E, d, h), jnp.float32) * s
        rb1 = jnp.zeros((E, h), jnp.float32)
        rW2 = jax.random.normal(ks[5], (E, h, d), jnp.float32) * s
        rb2 = jnp.zeros((E, d), jnp.float32)
        return dict(X=X, routing_W=routing_W, expert_bias=expert_bias, sW1=sW1, sb1=sb1, sW2=sW2, sb2=sb2, rW1=rW1, rb1=rb1, rW2=rW2, rb2=rb2)
    _L0_ffn_all = _L0_ffn_setup()
    _L0_ffn_in = {k: v for k, v in _L0_ffn_all.items() if k in ('routing_W', 'expert_bias', 'sW1', 'sb1', 'sW2', 'sb2', 'rW1', 'rb1', 'rW2', 'rb2')}
    del _L0_ffn_all

    def _L1_attn_setup():
        import jax, jax.numpy as jnp
        import numpy as np
        B, S, D = (8, 512, 256)
        key = jax.random.key(seed)
        kx, kw, kb = jax.random.split(key, 3)
        x = jax.random.normal(kx, (B, S, D), dtype=jnp.float32)
        W = jax.random.normal(kw, (3 * D, D), dtype=jnp.float32) * (1.0 / np.sqrt(D))
        b = jax.random.normal(kb, (3 * D,), dtype=jnp.float32) * 0.01
        return {'x': x, 'W': W, 'b': b}
    _L1_attn_all = _L1_attn_setup()
    _L1_attn_in = {k: v for k, v in _L1_attn_all.items() if k in ('W', 'b')}
    del _L1_attn_all

    def _L1_xattn_setup():
        import jax, jax.numpy as jnp
        import numpy as np
        EMBED_DIM = 256
        NUM_HEADS = 16
        HEAD_DIM = EMBED_DIM // NUM_HEADS
        WINDOW = 64

        def apply_rope(x):
            B, H, S, d = x.shape
            half = d // 2
            pos = jnp.arange(S, dtype=x.dtype)
            freqs = 1.0 / 10000.0 ** (jnp.arange(half, dtype=x.dtype) / half)
            ang = pos[:, None] * freqs[None, :]
            cos, sin = (jnp.cos(ang), jnp.sin(ang))
            x1, x2 = (x[..., :half], x[..., half:])
            return jnp.concatenate([x1 * cos - x2 * sin, x1 * sin + x2 * cos], axis=-1)

        def _forward(query, key, value, q_w, q_b, k_w, k_b, v_w, v_b, o_w, o_b):
            B, S_q, D = query.shape
            S_k = key.shape[1]
            H, d, W = (NUM_HEADS, HEAD_DIM, WINDOW)
            q = (query @ q_w.T + q_b).reshape(B, S_q, H, d).transpose(0, 2, 1, 3)
            k = (key @ k_w.T + k_b).reshape(B, S_k, H, d).transpose(0, 2, 1, 3)
            v = (value @ v_w.T + v_b).reshape(B, S_k, H, d).transpose(0, 2, 1, 3)
            q = apply_rope(q) * d ** (-0.5)
            k = apply_rope(k)
            q_pos = jnp.arange(S_q)[:, None]
            offsets = jnp.arange(-W, 1)[None, :]
            idx = q_pos + offsets
            local_mask = (idx < 0) | (idx >= S_k)
            gidx = jnp.clip(idx, 0, S_k - 1)
            k_win = k[:, :, gidx, :]
            v_win = v[:, :, gidx, :]
            scores = jnp.einsum('bhqd,bhqwd->bhqw', q, k_win)
            mask = local_mask[None, None, :, :]
            scores = jnp.where(mask, -jnp.inf, scores)
            m = jnp.max(scores, axis=-1, keepdims=True)
            m = jnp.where(jnp.isfinite(m), m, 0.0)
            e = jnp.exp(scores - m)
            denom = jnp.sum(e, axis=-1, keepdims=True)
            probs = jnp.where(denom > 0, e / jnp.where(denom > 0, denom, 1.0), 0.0)
            ctx = jnp.einsum('bhqw,bhqwd->bhqd', probs, v_win)
            ctx = ctx.transpose(0, 2, 1, 3).reshape(B, S_q, D)
            return ctx @ o_w.T + o_b
        key = jax.random.key(seed)
        ks = jax.random.split(key, 12)
        B, S, D = (1, 512, EMBED_DIM)
        scale = 1.0 / np.sqrt(D)
        inp = {'query': jax.random.normal(ks[0], (B, S, D), jnp.float32), 'key': jax.random.normal(ks[1], (B, S, D), jnp.float32), 'value': jax.random.normal(ks[2], (B, S, D), jnp.float32), 'q_w': jax.random.normal(ks[3], (D, D), jnp.float32) * scale, 'q_b': jax.random.normal(ks[4], (D,), jnp.float32) * 0.01, 'k_w': jax.random.normal(ks[5], (D, D), jnp.float32) * scale, 'k_b': jax.random.normal(ks[6], (D,), jnp.float32) * 0.01, 'v_w': jax.random.normal(ks[7], (D, D), jnp.float32) * scale, 'v_b': jax.random.normal(ks[8], (D,), jnp.float32) * 0.01, 'o_w': jax.random.normal(ks[9], (D, D), jnp.float32) * scale, 'o_b': jax.random.normal(ks[10], (D,), jnp.float32) * 0.01}
        return inp
    _L1_xattn_all = _L1_xattn_setup()
    _L1_xattn_in = {k: v for k, v in _L1_xattn_all.items() if k in ('q_w', 'q_b', 'k_w', 'k_b', 'v_w', 'v_b', 'o_w', 'o_b')}
    del _L1_xattn_all

    def _L1_ffn_setup():
        import jax, jax.numpy as jnp
        import numpy as np
        D_MODEL = 256
        HIDDEN = 512
        N_EXPERTS = 8
        TOP_K = 2
        BATCH = 2
        SEQ = 512
        key = jax.random.key(seed)
        ks = jax.random.split(key, 9)
        s = 0.02
        return {'x': jax.random.normal(ks[0], (BATCH, SEQ, D_MODEL), dtype=jnp.float32), 'w_router': jax.random.normal(ks[1], (D_MODEL, N_EXPERTS), dtype=jnp.float32) * s, 'w1': jax.random.normal(ks[2], (N_EXPERTS, D_MODEL, HIDDEN), dtype=jnp.float32) * s, 'w3': jax.random.normal(ks[3], (N_EXPERTS, D_MODEL, HIDDEN), dtype=jnp.float32) * s, 'w2': jax.random.normal(ks[4], (N_EXPERTS, HIDDEN, D_MODEL), dtype=jnp.float32) * s, 'sw1': jax.random.normal(ks[5], (D_MODEL, HIDDEN), dtype=jnp.float32) * s, 'sw3': jax.random.normal(ks[6], (D_MODEL, HIDDEN), dtype=jnp.float32) * s, 'sw2': jax.random.normal(ks[7], (HIDDEN, D_MODEL), dtype=jnp.float32) * s}
    _L1_ffn_all = _L1_ffn_setup()
    _L1_ffn_in = {k: v for k, v in _L1_ffn_all.items() if k in ('w_router', 'w1', 'w3', 'w2', 'sw1', 'sw3', 'sw2')}
    del _L1_ffn_all
    return {'x': x, 'ctx_1024': ctx_1024, 'mask_Bx1xSxS2_bf0': mask_Bx1xSxS2_bf0, 'L0_attn_W_qkv': _L0_attn_in['W_qkv'], 'L0_attn_b_qkv': _L0_attn_in['b_qkv'], 'L0_attn_W_out': _L0_attn_in['W_out'], 'L0_attn_b_out': _L0_attn_in['b_out'], 'L0_xattn_Wq': _L0_xattn_in['Wq'], 'L0_xattn_bq': _L0_xattn_in['bq'], 'L0_xattn_Wk': _L0_xattn_in['Wk'], 'L0_xattn_bk': _L0_xattn_in['bk'], 'L0_xattn_Wv': _L0_xattn_in['Wv'], 'L0_xattn_bv': _L0_xattn_in['bv'], 'L0_xattn_Wo': _L0_xattn_in['Wo'], 'L0_xattn_bo': _L0_xattn_in['bo'], 'L0_ffn_routing_W': _L0_ffn_in['routing_W'], 'L0_ffn_expert_bias': _L0_ffn_in['expert_bias'], 'L0_ffn_sW1': _L0_ffn_in['sW1'], 'L0_ffn_sb1': _L0_ffn_in['sb1'], 'L0_ffn_sW2': _L0_ffn_in['sW2'], 'L0_ffn_sb2': _L0_ffn_in['sb2'], 'L0_ffn_rW1': _L0_ffn_in['rW1'], 'L0_ffn_rb1': _L0_ffn_in['rb1'], 'L0_ffn_rW2': _L0_ffn_in['rW2'], 'L0_ffn_rb2': _L0_ffn_in['rb2'], 'L1_attn_W': _L1_attn_in['W'], 'L1_attn_b': _L1_attn_in['b'], 'L1_xattn_q_w': _L1_xattn_in['q_w'], 'L1_xattn_q_b': _L1_xattn_in['q_b'], 'L1_xattn_k_w': _L1_xattn_in['k_w'], 'L1_xattn_k_b': _L1_xattn_in['k_b'], 'L1_xattn_v_w': _L1_xattn_in['v_w'], 'L1_xattn_v_b': _L1_xattn_in['v_b'], 'L1_xattn_o_w': _L1_xattn_in['o_w'], 'L1_xattn_o_b': _L1_xattn_in['o_b'], 'L1_ffn_w_router': _L1_ffn_in['w_router'], 'L1_ffn_w1': _L1_ffn_in['w1'], 'L1_ffn_w3': _L1_ffn_in['w3'], 'L1_ffn_w2': _L1_ffn_in['w2'], 'L1_ffn_sw1': _L1_ffn_in['sw1'], 'L1_ffn_sw3': _L1_ffn_in['sw3'], 'L1_ffn_sw2': _L1_ffn_in['sw2']}

def reference(x, ctx_1024, mask_Bx1xSxS2_bf0, L0_attn_W_qkv, L0_attn_b_qkv, L0_attn_W_out, L0_attn_b_out, L0_xattn_Wq, L0_xattn_bq, L0_xattn_Wk, L0_xattn_bk, L0_xattn_Wv, L0_xattn_bv, L0_xattn_Wo, L0_xattn_bo, L0_ffn_routing_W, L0_ffn_expert_bias, L0_ffn_sW1, L0_ffn_sb1, L0_ffn_sW2, L0_ffn_sb2, L0_ffn_rW1, L0_ffn_rb1, L0_ffn_rW2, L0_ffn_rb2, L1_attn_W, L1_attn_b, L1_xattn_q_w, L1_xattn_q_b, L1_xattn_k_w, L1_xattn_k_b, L1_xattn_v_w, L1_xattn_v_b, L1_xattn_o_w, L1_xattn_o_b, L1_ffn_w_router, L1_ffn_w1, L1_ffn_w3, L1_ffn_w2, L1_ffn_sw1, L1_ffn_sw3, L1_ffn_sw2):
    import jax
    import jax.numpy as jnp

    def _L0_attn_ref(inputs, W_qkv, b_qkv, W_out, b_out):
        import jax, jax.numpy as jnp
        import numpy as np
        B, S, E = (4, 512, 256)
        HIDDEN = 256
        HEADS = 16
        Bv, Sv, Ev = inputs.shape
        x = inputs @ W_qkv + b_qkv
        x = x.reshape(Bv, HEADS, Sv, -1)
        q, k, v = jnp.split(x, 3, axis=-1)
        scale = (2 * HIDDEN) ** (-0.5)
        qk = jnp.einsum('bhse,bhte->bhst', q, k) * scale
        mask = jnp.triu(jnp.full((Sv, Sv), -jnp.inf, dtype=qk.dtype), k=1)
        attn = jax.nn.softmax(qk + mask, axis=-1)
        sa = jnp.einsum('bhst,bhte->bhse', attn, v).reshape(Bv, Sv, -1)
        return sa @ W_out + b_out

    def _L0_xattn_ref(q, k, v, mask, Wq, bq, Wk, bk, Wv, bv, Wo, bo):
        import jax, jax.numpy as jnp
        import numpy as np
        from math import sqrt
        B, L, D, H = (2, 512, 256, 16)
        DH = D // H

        def _split(x):
            b, l, _ = x.shape
            return x.reshape(b, l, H, DH).transpose(0, 2, 1, 3)
        qh = _split(q @ Wq.T + bq)
        kh = _split(k @ Wk.T + bk)
        vh = _split(v @ Wv.T + bv)
        scores = jnp.einsum('bhqd,bhkd->bhqk', qh, kh) / sqrt(DH)
        scores = jnp.where(mask, -jnp.inf, scores)
        attn = jax.nn.softmax(scores, axis=-1)
        out = jnp.einsum('bhqk,bhkd->bhqd', attn, vh)
        out = out.transpose(0, 2, 1, 3).reshape(q.shape[0], -1, D)
        return out @ Wo.T + bo

    def _L0_ffn_ref(X, routing_W, expert_bias, sW1, sb1, sW2, sb2, rW1, rb1, rW2, rb2):
        import jax, jax.numpy as jnp
        import numpy as np
        E = 8
        K = 2
        B, T, d = X.shape
        shared = jax.nn.silu(X @ sW1 + sb1) @ sW2 + sb2
        logits = jnp.einsum('btd,ed->bte', X, routing_W) + expert_bias
        activation = jnp.sqrt(jax.nn.softplus(logits))
        top_vals, top_idx = jax.lax.top_k(activation, K)
        combine = jnp.sum(jax.nn.one_hot(top_idx, E, dtype=X.dtype) * top_vals[..., None], axis=-2)
        Xf = X.reshape(-1, d)
        cf = combine.reshape(-1, E)
        hdn = jax.nn.silu(jnp.einsum('nd,edh->enh', Xf, rW1) + rb1[:, None, :])
        y = jnp.einsum('enh,ehd->end', hdn, rW2) + rb2[:, None, :]
        routed = jnp.einsum('ne,end->nd', cf, y).reshape(B, T, d)
        return shared + routed

    def _L1_attn_ref(x, W, b):
        import jax, jax.numpy as jnp
        import numpy as np
        B, S, D = (8, 512, 256)
        qkv = jnp.einsum('bsd,fd->bsf', x, W) + b
        q, k, v = jnp.split(qkv, 3, axis=-1)
        attn = jnp.einsum('bik,bjk->bij', q, k) / k.shape[-1]
        attn = jax.nn.softmax(attn, axis=1)
        out = jnp.einsum('bij,bjk->bik', attn, v)
        return out

    def _L1_xattn_ref(query, key, value, q_w, q_b, k_w, k_b, v_w, v_b, o_w, o_b):
        import jax, jax.numpy as jnp
        import numpy as np
        EMBED_DIM = 256
        NUM_HEADS = 16
        HEAD_DIM = EMBED_DIM // NUM_HEADS
        WINDOW = 64

        def apply_rope(x):
            B, H, S, d = x.shape
            half = d // 2
            pos = jnp.arange(S, dtype=x.dtype)
            freqs = 1.0 / 10000.0 ** (jnp.arange(half, dtype=x.dtype) / half)
            ang = pos[:, None] * freqs[None, :]
            cos, sin = (jnp.cos(ang), jnp.sin(ang))
            x1, x2 = (x[..., :half], x[..., half:])
            return jnp.concatenate([x1 * cos - x2 * sin, x1 * sin + x2 * cos], axis=-1)

        def _forward(query, key, value, q_w, q_b, k_w, k_b, v_w, v_b, o_w, o_b):
            B, S_q, D = query.shape
            S_k = key.shape[1]
            H, d, W = (NUM_HEADS, HEAD_DIM, WINDOW)
            q = (query @ q_w.T + q_b).reshape(B, S_q, H, d).transpose(0, 2, 1, 3)
            k = (key @ k_w.T + k_b).reshape(B, S_k, H, d).transpose(0, 2, 1, 3)
            v = (value @ v_w.T + v_b).reshape(B, S_k, H, d).transpose(0, 2, 1, 3)
            q = apply_rope(q) * d ** (-0.5)
            k = apply_rope(k)
            q_pos = jnp.arange(S_q)[:, None]
            offsets = jnp.arange(-W, 1)[None, :]
            idx = q_pos + offsets
            local_mask = (idx < 0) | (idx >= S_k)
            gidx = jnp.clip(idx, 0, S_k - 1)
            k_win = k[:, :, gidx, :]
            v_win = v[:, :, gidx, :]
            scores = jnp.einsum('bhqd,bhqwd->bhqw', q, k_win)
            mask = local_mask[None, None, :, :]
            scores = jnp.where(mask, -jnp.inf, scores)
            m = jnp.max(scores, axis=-1, keepdims=True)
            m = jnp.where(jnp.isfinite(m), m, 0.0)
            e = jnp.exp(scores - m)
            denom = jnp.sum(e, axis=-1, keepdims=True)
            probs = jnp.where(denom > 0, e / jnp.where(denom > 0, denom, 1.0), 0.0)
            ctx = jnp.einsum('bhqw,bhqwd->bhqd', probs, v_win)
            ctx = ctx.transpose(0, 2, 1, 3).reshape(B, S_q, D)
            return ctx @ o_w.T + o_b
        return _forward(query, key, value, q_w, q_b, k_w, k_b, v_w, v_b, o_w, o_b)

    def _L1_ffn_ref(x, w_router, w1, w3, w2, sw1, sw3, sw2):
        import jax, jax.numpy as jnp
        import numpy as np
        D_MODEL = 256
        HIDDEN = 512
        N_EXPERTS = 8
        TOP_K = 2
        BATCH = 2
        SEQ = 512
        b, s, d = x.shape
        xf = x.reshape(b * s, d)
        probs = jax.nn.softmax(xf @ w_router, axis=-1)
        top_vals, top_idx = jax.lax.top_k(probs, TOP_K)
        gates = top_vals / jnp.sum(top_vals, axis=-1, keepdims=True)
        onehot = jax.nn.one_hot(top_idx, N_EXPERTS, dtype=xf.dtype)
        cw = jnp.einsum('tk,tke->te', gates, onehot)
        h1 = jnp.einsum('td,edh->eth', xf, w1)
        h3 = jnp.einsum('td,edh->eth', xf, w3)
        y = jnp.einsum('eth,ehd->etd', jax.nn.silu(h1) * h3, w2)
        out = jnp.einsum('etd,te->td', y, cw)
        out = out + jax.nn.silu(xf @ sw1) * (xf @ sw3) @ sw2
        return out.reshape(b, s, d)
    x = _layernorm(x + _L0_attn_ref(x, L0_attn_W_qkv, L0_attn_b_qkv, L0_attn_W_out, L0_attn_b_out), axis=-1)
    x = _layernorm(x + _L0_xattn_ref(x, ctx_1024, ctx_1024, mask_Bx1xSxS2_bf0, L0_xattn_Wq, L0_xattn_bq, L0_xattn_Wk, L0_xattn_bk, L0_xattn_Wv, L0_xattn_bv, L0_xattn_Wo, L0_xattn_bo), axis=-1)
    x = _layernorm(x + _L0_ffn_ref(x, L0_ffn_routing_W, L0_ffn_expert_bias, L0_ffn_sW1, L0_ffn_sb1, L0_ffn_sW2, L0_ffn_sb2, L0_ffn_rW1, L0_ffn_rb1, L0_ffn_rW2, L0_ffn_rb2), axis=-1)
    x = _layernorm(x + _L1_attn_ref(x, L1_attn_W, L1_attn_b), axis=-1)
    x = _layernorm(x + _L1_xattn_ref(x, ctx_1024, ctx_1024, L1_xattn_q_w, L1_xattn_q_b, L1_xattn_k_w, L1_xattn_k_b, L1_xattn_v_w, L1_xattn_v_b, L1_xattn_o_w, L1_xattn_o_b), axis=-1)
    x = _layernorm(x + _L1_ffn_ref(x, L1_ffn_w_router, L1_ffn_w1, L1_ffn_w3, L1_ffn_w2, L1_ffn_sw1, L1_ffn_sw3, L1_ffn_sw2), axis=-1)
    return x

_drawn_inputs = setup_inputs


def setup_inputs(seed=0):
    import zlib

    import numpy as np

    out = dict(_drawn_inputs(seed))
    spreads = {'L0_attn_b_qkv': (0.0, 0.51),
     'L0_attn_b_out': (0.0, 0.1),
     'L0_xattn_bq': (0.0, 0.1),
     'L0_xattn_bk': (0.0, 2.0),
     'L0_xattn_bv': (0.0, 0.1),
     'L0_xattn_bo': (0.0, 0.1),
     'L0_ffn_expert_bias': (0.0, 0.1),
     'L0_ffn_sb1': (0.0, 0.606),
     'L0_ffn_sb2': (0.0, 0.1),
     'L0_ffn_rb1': (0.0, 0.501),
     'L0_ffn_rb2': (0.0, 0.1)}
    factors = {'L0_attn_W_qkv': 3.963,
     'L0_attn_W_out': 3.194,
     'L1_attn_b': 5.739,
     'L1_xattn_q_b': 8.0,
     'L1_xattn_k_b': 22.071,
     'L1_xattn_v_b': 8.0,
     'L1_xattn_o_b': 5.651,
     'L1_ffn_w_router': 3.981,
     'L1_ffn_w1': 3.422,
     'L1_ffn_w3': 3.367,
     'L1_ffn_w2': 3.383,
     'L1_ffn_sw1': 3.057,
     'L1_ffn_sw3': 2.911,
     'L1_ffn_sw2': 2.994}
    for name, (base, spread) in spreads.items():
        noise = np.random.default_rng([zlib.crc32(name.encode()), seed]).standard_normal(out[name].shape)
        drawn = base * np.exp(spread * noise) if base else spread * noise
        out[name] = jnp.asarray(drawn.astype(out[name].dtype))
    for name, factor in factors.items():
        out[name] = (out[name] * factor).astype(out[name].dtype)
    return out
```

```python
from contextlib import ExitStack

import concourse.bass as bass
from concourse import mybir

F32 = mybir.dt.float32
BF16 = mybir.dt.bfloat16
U8 = mybir.dt.uint8
U32 = mybir.dt.uint32
ALU = mybir.AluOpType
ACT = mybir.ActivationFunctionType
AX = mybir.AxisListType

P = 128
B, S, D = 4, 512, 256
NT, KC = S // P, D // P
H, DH = 16, 16
SK = 64
NE = 8
HID1 = 512
HB1 = HID1 // P
EPS = 1e-5
NJ = 4
HT = S // H
TR = HT // NJ
TERMS_Q = (0, 0, 1, 1, 0, 2)
TERMS_K = (0, 1, 0, 1, 2, 0)
NTERM = len(TERMS_Q)
ROWS6 = NTERM * DH
SCALE_A = float(2 * D) ** -0.5
SCALE_X = float(DH) ** -0.5
GONE = -3e38

W_COLS = {"a_qk": 1024, "a_v": 512, "a_o": 512,
          "x0_q": 512, "x0_k": 512, "x0_v": 512, "x0_o": 512,
          "f0_r": 16, "f0_w1": 2 * 9 * 128, "f0_w2": 9 * 256,
          "d_q": 512, "d_k": 512, "d_v": 512,
          "x1_q": 512, "x1_qs": 512, "x1_k": 512, "x1_ks": 512, "x1_v": 512, "x1_o": 512,
          "f1_r": 16}
ROW_COLS = {"a_v": 256, "a_o": 256, "x0_v": 256, "x0_o": 256, "f0_o": 256, "d_v": 256,
            "x1_v": 256, "x1_o": 256, "f0_r": 8}
COL_COLS = {"a_qk": 4, "x0_q": 2, "x0_k": 2, "d_q": 2, "d_k": 2, "x1_q": 2, "x1_qs": 2,
            "x1_k": 2, "x1_ks": 2, "f0_b1": 9}
CONST_COLS = {"ident": 128, "causal": 128, "window": 64, "sel": NE * 128, "blk": 8,
              "ropeq": 256, "ropek": 128, "iota": 8, "expo": 8}


def offsets(cols):
    at, out = 0, {}
    for name, n in cols.items():
        out[name] = (at, at + n)
        at += n
    return out, at


WO, W_ALL = offsets(W_COLS)
RO, R_ALL = offsets(ROW_COLS)
CO, C_ALL = offsets(COL_COLS)
KO, K_ALL = offsets(CONST_COLS)

SEMS = """x_in ctx_in pen_in xt_ps xt_a xt_v x_bias
ln_sum ln_st ln_ag ln_ep ln_rs ln_done r_done
a_qk a_qkf a_hi a_r1 a_mid a_lo a_q6 a_v a_vt a_vd a_vre
a_qr a_s a_mx a_ex a_tp a_ptv a_pta a_pv a_ri a_on a_od a_ot
o_tp o_ta o_tv
c_tp c_ct c_k c_v c_kb0 c_ka c_kb c_kc c_kb1 c_vb pen
x_q x_qt x_qa x_qb x_s x_sm x_mx x_sub x_ex x_rs x_tp x_pt x_pv x_ri x_on
g_lg g_ls g_mx g_ix g_if g_oh g_sum g_a g_e g_b g_l g_c g_p g_cmb g_h g_m g_lo g_tp g_ct
f_h f_s f_cb f_g f_y f_w f_b2
d_qk d_ev d_v d_vt d_s d_mx d_ex d_rz d_vn out""".split()


def decoder(nc, x, ctx_in, mask, weights, rows, cols, consts, b2rows, experts, out, v_scr, o_scr):
    with ExitStack() as ctx:
        def sb(name, shape, dt=F32):
            return ctx.enter_context(nc.sbuf_tensor(name, shape, dt))

        W = sb("W", [P, W_ALL])
        BR = sb("BR", [P, R_ALL])
        BC = sb("BC", [P, C_ALL])
        K = sb("K", [P, K_ALL])
        b2 = sb("b2", [NE, D])
        identb = sb("identb", [P, P], BF16)
        causalb = sb("causalb", [P, P], BF16)
        selb = sb("selb", [3 * NE, NE, P], BF16)
        X = sb("X", [P, NT, D])
        XT = sb("XT", [P, KC, S])
        stats = sb("stats", [P, NT, 6])
        mv = sb("mv", [P, NT, 2])
        veps = sb("veps", [P, NT])
        rstd = sb("rstd", [P, NT])
        qkf = sb("qkf", [P, 4, S])
        parts = sb("parts", [P, 3, 4, S], BF16)
        shared = sb("shared", [P, 2, 4096])
        q6 = shared[:, 0, :].bitcast(BF16).rearrange("p (c s) -> p c s", c=H)
        k6 = shared[:, 1, :].bitcast(BF16).rearrange("p (c s) -> p c s", c=H)
        wbuf = shared[:, :, 0:3072]
        vtok = sb("vtok", [P, NT, D])
        vpos = sb("vpos", [P, H * NJ, DH])
        opos = sb("opos", [P, H * NJ, DH])
        otok = sb("otok", [P, NT, D])
        OT = sb("OT", [P, KC, S])
        pb = sb("pb", [P, 2, S])
        ptb = sb("ptb", [P, 2, S])
        nmax = sb("nmax", [P, H * NJ])
        rsum = sb("rsum", [P, H * NJ])
        rinv = sb("rinv", [P, H * NJ])
        qT = sb("qT", [P, KC, S])
        late = sb("late", [P, 4, 2 * S])
        kT, hs, hm, hg = (late[:, n, :].rearrange("p (a b) -> p a b", a=2) for n in range(4))
        qpos = late[:].rearrange("p a b -> p (a b)").bitcast(BF16).rearrange("p (g c r) -> p g c r", c=H, r=TR)
        ctok = sb("ctok", [SK, D])
        cT = sb("cT", [P, KC, 2, SK])
        kb = [sb(f"kb{i}", [P, KC, 8, SK]) for i in range(2)]
        kr = sb("kr", [P, 3, KC, SK])
        vb = [sb(f"vb{i}", [P, H // 2, 2, DH]) for i in range(2)]
        mask8 = sb("mask8", [P, NT, SK], U8)
        pen = sb("pen", [P, NT, SK])
        sc = sb("sc", [P, 2, 8, SK])
        lg = sb("lg", [P, NT, NE])
        top = sb("top", [P, NT, 8])
        ix = sb("ix", [P, NT, 8], U32)
        ixf = sb("ixf", [P, NT, 8])
        oh = sb("oh", [P, 2, NT, NE])
        ga = sb("ga", [P, 8, NT, NE])
        cmb = sb("cmb", [P, NT, NE])
        cmb3 = sb("cmb3", [P, NT, 3 * NE], BF16)
        cmbT = sb("cmbT", [NE, S])
        cmb3T = sb("cmb3T", [3 * NE, S], BF16)
        bank = [ctx.enter_context(nc.psum_tensor(f"bank{i}", [P, 512], F32)) for i in range(8)]
        s = {n: ctx.enter_context(nc.semaphore(n)) for n in SEMS}
        w_in = [ctx.enter_context(nc.semaphore(f"w_in{i}")) for i in range(4)]
        setup = ctx.enter_context(nc.semaphore("setup"))
        cast = ctx.enter_context(nc.semaphore("cast"))

        def w(name):
            a, b = WO[name]
            return W[:, a:b].rearrange("p (k n) -> p k n", k=KC)

        def row(name):
            a, b = RO[name]
            return BR[:, a:b]

        def col(name):
            a, b = CO[name]
            return BC[:, a:b]

        def const(name):
            a, b = KO[name]
            return K[:, a:b]

        ident = const("ident")
        a, b = WO["f0_w2"]
        f0_w2 = W[:, a:b].rearrange("p (e n) -> p e n", e=9)
        vtile = vtok[:, :, :]

        with nc.Block() as first:
            @first.sync
            def _(sp):
                sp.dma_start(K[:, :], consts).then_inc(w_in[0], 16)
                sp.dma_start(BC[:, :], cols).then_inc(w_in[0], 16)
                sp.dma_start(BR[:, :], rows.partition_broadcast(P)).then_inc(w_in[0], 16)
                sp.dma_start(b2[:, :], b2rows).then_inc(w_in[0], 16)
                cut = [0, WO["x0_q"][0], WO["d_q"][0], W_ALL]
                for i in range(3):
                    sp.dma_start(W[:, cut[i]:cut[i + 1]], weights[:, cut[i]:cut[i + 1]]).then_inc(w_in[i + 1], 16)

            @first.vector
            def _(v):
                v.memset(vb[0][:], 0.0).then_inc(setup, 1)
                v.memset(vb[1][:], 0.0).then_inc(setup, 1)
                v.wait_ge(w_in[0], 64)
                v.tensor_copy(identb[:], ident).then_inc(cast, 1)
                v.tensor_copy(causalb[:], const("causal")).then_inc(cast, 1)
                v.tensor_copy(selb[:], const("sel")[0:3 * NE].rearrange("p (e n) -> p e n", e=NE)).then_inc(cast, 1)
                v.tensor_scalar_mul(col("a_qk")[:, 0:2], col("a_qk")[:, 0:2], SCALE_A).then_inc(cast, 1)
                v.tensor_scalar_mul(col("x0_q"), col("x0_q"), SCALE_X).then_inc(cast, 1)
                v.tensor_scalar_mul(col("d_q"), col("d_q"), 1.0 / D).then_inc(cast, 1)
                v.wait_ge(cast, 6)
                v.wait_ge(setup, 2)

        with nc.Fori(0, B) as bi:
            with nc.Block() as block:
                @block.sync
                def _(sp):
                    one = bass.ds(bi, 1)
                    sp.dma_start(X[:], x[one].rearrange("a (t p) d -> (a p) t d", p=P)).then_inc(s["x_in"], 16)
                    sp.dma_start(ctok[:], ctx_in[one].rearrange("a p d -> (a p) d")).then_inc(s["ctx_in"], 16)
                    sp.dma_start(mask8[:], mask[one].rearrange("a (t p) k -> (a p) t k", p=P)).then_inc(s["pen_in"], 16)

                    for part, ready in ((0, "a_hi"), (1, "a_mid"), (2, "a_lo")):
                        sp.wait_ge(s[ready], 4)
                        for dst, base, terms in ((q6, 0, TERMS_Q), (k6, 2, TERMS_K)):
                            for n, term in enumerate(terms):
                                if term != part:
                                    continue
                                for half in range(2):
                                    for c in range(8):
                                        sp.dma_start(dst[DH * n:DH * n + DH, 8 * half + c, :],
                                                     parts[DH * c:DH * c + DH, part, base + half, :])\
                                          .then_inc(s["a_q6"], 16)
                    sp.wait_ge(s["a_vt"], 2)
                    sp.dma_start(v_scr.rearrange("(t p) f -> p t f", p=P), vtok[:]).then_inc(s["a_vd"], 16)
                    sp.wait_ge(s["a_vd"], 16)
                    v_src = v_scr.rearrange("(g r) (c e) -> r c g e", r=TR, e=DH)
                    for r in range(TR):
                        sp.dma_start(vpos[r:P:TR], v_src[r]).then_inc(s["a_vre"], 16)
                    sp.wait_ge(s["a_on"], 2)
                    o_dst = o_scr.rearrange("(g r) (c e) -> r c g e", r=TR, e=DH)
                    for r in range(TR):
                        sp.dma_start(o_dst[r], opos[r:P:TR]).then_inc(s["a_od"], 16)
                    sp.wait_ge(s["a_od"], 16 * TR)
                    sp.dma_start(otok[:], o_scr.rearrange("(t p) f -> p t f", p=P)).then_inc(s["a_ot"], 16)

                    for e in range(NE + 1):
                        if e >= 2:
                            sp.wait_ge(s["f_y"], 9 + HB1 * (e - 1))
                        sp.dma_start(wbuf[:, e % 2, :], experts[e]).then_inc(s["f_w"], 16)
                        sp.wait_ge(s["f_w"], 16 * (e + 1))
                    sp.wait_ge(s["ln_done"], 6 * NT)
                    sp.dma_start(out[one].rearrange("a (t p) d -> (a p) t d", p=P), X[:]).then_inc(s["out"], 16)
                    sp.wait_ge(s["out"], 16)

                @block.tensor
                def _(pe):
                    mm, tr = nc.tensor.matmul, nc.tensor.transpose

                    def turn_x(st):
                        for t in range(NT):
                            if st == 0:
                                pe.wait_ge(s["x_in"], 16)
                            else:
                                pe.wait_ge(s["ln_done"], NT * (st - 1) + t + 1)
                            for k in range(KC):
                                last = tr(bank[6 + k][:, t * P:(t + 1) * P], X[:, t, k * P:(k + 1) * P], ident)
                        last.then_inc(s["xt_ps"], 1)
                        pe.wait_ge(s["xt_a"], st + 1)
                        pe.wait_ge(s["xt_v"], st + 1)

                    def feature_major(dst, wt, m0, rhs):
                        for k in range(KC):
                            last = mm(dst, wt[:, k, m0:m0 + P], rhs[:, k, :], start=(k == 0), stop=(k == KC - 1))
                        return last

                    def token_major(dst, src, t, wt):
                        for k in range(KC):
                            last = mm(dst, src[:, k, t * P:(t + 1) * P], wt[:, k, :],
                                      start=(k == 0), stop=(k == KC - 1))
                        return last

                    def project(n_o, banks, wt, tiles):
                        for t in range(tiles):
                            for k in range(KC):
                                last = tr(bank[6 + k][:, t * P:(t + 1) * P], otok[:, t, k * P:(k + 1) * P], ident)
                        last.then_inc(s["o_tp"], 1)
                        pe.wait_ge(s["o_ta"], n_o + 1)
                        pe.wait_ge(s["o_tv"], n_o + 1)
                        for t in range(tiles):
                            last = token_major(bank[banks[t // 2]][:, (t % 2) * D:(t % 2 + 1) * D], OT, t, wt)
                            if t % 2 == 1 or t == tiles - 1:
                                last.then_inc(s["r_done"], 1)

                    pe.wait_ge(w_in[0], 64)
                    pe.wait_ge(w_in[1], 16)
                    turn_x(0)
                    for blk in range(4):
                        feature_major(bank[blk][:, :], w("a_qk"), blk * P, XT).then_inc(s["a_qk"], 1)
                    for t in range(NT):
                        last = token_major(bank[4 + t // 2][:, (t % 2) * D:(t % 2 + 1) * D], XT, t, w("a_v"))
                        if t % 2:
                            last.then_inc(s["a_v"], 1)

                    pe.wait_ge(s["ctx_in"], 16)
                    for k in range(KC):
                        last = tr(bank[7][:, k * SK:(k + 1) * SK], ctok[:, k * P:(k + 1) * P], ident[0:SK, 0:SK])
                    last.then_inc(s["c_tp"], 1)
                    pe.wait_ge(s["c_ct"], 1)
                    pe.wait_ge(w_in[2], 16)
                    pe.wait_ge(w_in[3], 16)
                    for n, name in enumerate(("x0_k", "x1_k", "x1_ks")):
                        for blk in range(KC):
                            at = (2 * n + blk) * SK
                            for k in range(KC):
                                last = mm(bank[6][:, at:at + SK], w(name)[:, k, blk * P:(blk + 1) * P],
                                          cT[:, k, 0, :], start=(k == 0), stop=(k == KC - 1))
                    last.then_inc(s["c_k"], 1)
                    for n in range(2):
                        for k in range(KC):
                            last = mm(bank[7][:, n * D:(n + 1) * D], cT[:, k, :, :], w(f"x{n}_v")[:, k, :],
                                      start=(k == 0), stop=(k == KC - 1))
                    last.then_inc(s["c_v"], 1)

                    pe.wait_ge(s["a_q6"], 16 * 16 * 2 * NTERM)
                    pe.wait_ge(s["a_qkf"], 4)
                    pe.wait_ge(s["a_vt"], 2)
                    n_tiles = H * NJ
                    for i in range(n_tiles + 2):
                        if i < n_tiles:
                            h, j = divmod(i, NJ)
                            if i >= 2:
                                pe.wait_ge(s["a_ex"], i - 1)
                            sc_ps = bank[i % 2]
                            tok = HT * h
                            qs = qpos[0:ROWS6, i, :, :]
                            if i % H == 0:
                                pe.wait_ge(s["a_qr"], i // H + 1)
                            ks = k6[0:ROWS6, :, tok:tok + TR * (j + 1)].rearrange("p c (j r) -> p j c r", r=TR)
                            mm(sc_ps[:, 0:P * (j + 1)], qs, ks, start=True, stop=True)
                            mm(sc_ps[:, P * j:P * (j + 1)], identb[:], causalb[:], start=False, stop=True,
                               skip_group_check=True).then_inc(s["a_s"], 1)
                        if 1 <= i <= n_tiles:
                            n = i - 1
                            j = n % NJ
                            pe.wait_ge(s["a_ex"], n + 1)
                            if n >= 2:
                                pe.wait_ge(s["a_ptv"] if n % 2 == 0 else s["a_pta"], n // 2)
                            for jj in range(j + 1):
                                last = tr(bank[2 + n % 2][:, jj * P:(jj + 1) * P], pb[:, n % 2, jj * P:(jj + 1) * P], ident)
                            last.then_inc(s["a_tp"], 1)
                        if i >= 2:
                            n = i - 2
                            h, j = divmod(n, NJ)
                            if n == 0:
                                pe.wait_ge(s["a_vre"], 16 * TR)
                            pe.wait_ge(s["a_ptv"] if n % 2 == 0 else s["a_pta"], n // 2 + 1)
                            for jj in range(j + 1):
                                last = mm(bank[4 + n // 32][:, (n % 32) * DH:(n % 32 + 1) * DH],
                                          ptb[:, n % 2, jj * P:(jj + 1) * P], vpos[:, NJ * h + jj, :],
                                          start=(jj == 0), stop=(jj == j))
                            last.then_inc(s["a_pv"], 1)
                    pe.wait_ge(s["c_kb1"], 2)
                    pe.wait_ge(s["c_vb"], 4)
                    pe.wait_ge(s["a_ot"], 16)
                    project(0, (0, 1), w("a_o"), NT)

                    def cross(n, tiles, u0, t0):
                        for u in range(2 * tiles + 1):
                            if u < 2 * tiles:
                                t, g = divmod(u, 2)
                                if u >= 2:
                                    pe.wait_ge(s["x_sm"], u0 + u - 1)
                                mm(bank[4 + u % 2][:, :], qT[:, g, t * P:(t + 1) * P], kb[n][:, g, :, :],
                                   start=True, stop=True).then_inc(s["x_s"], 1)
                            if u >= 1:
                                v_ = u - 1
                                t, g = divmod(v_, 2)
                                pe.wait_ge(s["x_ex"], u0 + v_ + 1)
                                for pr in range(4):
                                    last = tr(bank[2 + v_ % 2][:, pr * P:(pr + 1) * P],
                                              pb[:, v_ % 2, pr * P:(pr + 1) * P], ident)
                                last.then_inc(s["x_tp"], 1)
                                pe.wait_ge(s["x_pt"], u0 + v_ + 1)
                                if g == 0 and t >= 2:
                                    pe.wait_ge(s["x_on"], t0 + t - 1)
                                for pr in range(4):
                                    at = (4 * g + pr) * 2 * DH
                                    last = mm(bank[t % 2][:, at:at + 2 * DH], ptb[:, v_ % 2, pr * P:(pr + 1) * P],
                                              vb[n][:, 4 * g + pr, :, :], start=True, stop=True)
                                last.then_inc(s["x_pv"], 1)
                        pe.wait_ge(s["x_on"], t0 + tiles)

                    turn_x(1)
                    for blk in range(KC):
                        feature_major(bank[2 + blk][:, :], w("x0_q"), blk * P, XT).then_inc(s["x_q"], 1)
                    pe.wait_ge(s["x_qt"], 2)
                    cross(0, NT, 0, 0)
                    project(1, (2, 3), w("x0_o"), NT)

                    def route(n, name):
                        for t in range(NT):
                            for k in range(KC):
                                last = mm(bank[2][:, t * NE:(t + 1) * NE], XT[:, k, t * P:(t + 1) * P],
                                          w(name)[:, k, :], start=(k == 0), stop=(k == KC - 1))
                        last.then_inc(s["g_lg"], 1)

                    def turn_route(n):
                        pe.wait_ge(s["g_lo"], n + 1)
                        b6 = bank[6][:, :].bitcast(BF16)
                        for t in range(NT):
                            tr(b6[0:3 * NE, t * P:(t + 1) * P], cmb3[:, t, :], identb[:])
                            last = tr(bank[7][0:NE, t * P:(t + 1) * P], cmb[:, t, :], ident)
                        last.then_inc(s["g_tp"], 1)
                        pe.wait_ge(s["g_ct"], 2 * n + 2)

                    def add_y(n_block, e, hid_tile, w2, last_one):
                        for t in range(NT):
                            last = mm(bank[t // 2][:, (t % 2) * D:(t % 2 + 1) * D], hid_tile[:, t * P:(t + 1) * P], w2,
                                      start=(n_block == 0 and t % 2 == 0), stop=last_one, skip_group_check=True)
                        return last

                    turn_x(2)
                    route(0, "f0_r")
                    for e in range(NE + 2):
                        if e <= NE:
                            if e >= 2:
                                pe.wait_ge(s["f_s"], e - 1)
                            feature_major(bank[4 + e % 2][:, :], w("f0_w1"), e * P, XT).then_inc(s["f_h"], 1)
                            if e == 1:
                                turn_route(0)
                            if e >= 1:
                                if e >= 3:
                                    pe.wait_ge(s["f_g"], e - 2)
                                mm(bank[6 + e % 2][:, :], selb[:, e - 1, :], cmb3T[:], start=True, stop=True)\
                                    .then_inc(s["f_cb"], 1)
                        if e >= 1:
                            n = e - 1
                            if n == 0:
                                pe.wait_ge(s["f_s"], 1)
                                add_y(0, 0, hs[:, 0, :], f0_w2[:, 0, :], False).then_inc(s["f_y"], 1)
                            else:
                                pe.wait_ge(s["f_g"], n)
                                add_y(n, n, hg[:, n % 2, :], f0_w2[:, n, :], False).then_inc(s["f_y"], 1)
                    for t in range(NT):
                        last = mm(bank[t // 2][:, (t % 2) * D:(t % 2 + 1) * D], cmbT[:, t * P:(t + 1) * P], b2[:],
                                  start=False, stop=True, skip_group_check=True)
                        if t % 2:
                            last.then_inc(s["r_done"], 1)

                    turn_x(3)
                    for blk in range(KC):
                        feature_major(bank[2 + blk][:, :], w("d_q"), blk * P, XT).then_inc(s["d_qk"], 1)
                    for blk in range(KC):
                        feature_major(bank[4 + blk][:, :], w("d_k"), blk * P, XT).then_inc(s["d_qk"], 1)
                    for t in range(NT):
                        last = token_major(bank[6 + t // 2][:, (t % 2) * D:(t % 2 + 1) * D], XT, t, w("d_v"))
                        if t % 2:
                            last.then_inc(s["d_v"], 1)
                    pe.wait_ge(s["d_ev"], 4)
                    pe.wait_ge(s["x_qt"], 4)
                    for j in range(NT):
                        for k in range(KC):
                            last = mm(bank[2 + j][:, :], kT[:, k, j * P:(j + 1) * P], qT[:, k, :],
                                      start=(k == 0), stop=(k == KC - 1))
                        last.then_inc(s["d_s"], 1)
                    for j in range(NT):
                        pe.wait_ge(s["d_ex"], j + 1)
                        pe.wait_ge(s["d_vn"], j + 1)
                        for t in range(NT):
                            last = mm(bank[t // 2][:, (t % 2) * D:(t % 2 + 1) * D], qkf[:, j, t * P:(t + 1) * P],
                                      vtok[:, j, :], start=(j == 0 and t % 2 == 0), stop=(j == NT - 1),
                                      skip_group_check=True)
                            if j == NT - 1 and t % 2:
                                last.then_inc(s["r_done"], 1)

                    turn_x(4)
                    for n, name in enumerate(("x1_q", "x1_qs")):
                        for blk in range(KC):
                            for k in range(KC):
                                last = mm(bank[2][:, (2 * n + blk) * P:(2 * n + blk + 1) * P],
                                          w(name)[:, k, blk * P:(blk + 1) * P], XT[:, k, 0:P],
                                          start=(k == 0), stop=(k == KC - 1))
                    last.then_inc(s["x_q"], 1)
                    pe.wait_ge(s["x_qt"], 6)
                    cross(1, 1, 2 * NT, NT)
                    project(2, (0,), w("x1_o"), 1)

                    turn_x(5)
                    route(1, "f1_r")
                    for n in range(HB1 * (NE + 1) + 1):
                        if n < HB1 * (NE + 1):
                            e, hb = divmod(n, HB1)
                            if hb == 0:
                                pe.wait_ge(s["f_w"], 16 * (e + 1))
                            we = wbuf[:, e % 2, :]
                            w1 = we[:, 0:1024].rearrange("p (k n) -> p k n", k=KC)
                            w3 = we[:, 1024:2048].rearrange("p (k n) -> p k n", k=KC)
                            if n == 0:
                                pe.wait_ge(s["g_ls"], 2)
                            if n >= 2:
                                pe.wait_ge(s["f_s"], 9 + n - 1)
                            feature_major(bank[2 + n % 2][:, :], w1, hb * P, XT).then_inc(s["f_h"], 1)
                            if n >= 2:
                                pe.wait_ge(s["f_m"] if False else s["f_b2"], n - 1)
                            feature_major(bank[4 + n % 2][:, :], w3, hb * P, XT).then_inc(s["f_h"], 1)
                            if n == HB1 - 1:
                                turn_route(1)
                            if hb == 0 and e >= 1:
                                if e >= 3:
                                    pe.wait_ge(s["f_g"], 8 + HB1 * (e - 2))
                                mm(bank[6 + e % 2][:, :], selb[:, e - 1, :], cmb3T[:], start=True, stop=True)\
                                    .then_inc(s["f_cb"], 1)
                        if n >= 1:
                            e, hb = divmod(n - 1, HB1)
                            m = n - 1
                            w2 = wbuf[:, e % 2, 2048:3072].rearrange("p (c n) -> p c n", c=HB1)[:, hb, :]
                            last_one = m == HB1 * (NE + 1) - 1
                            if e == 0:
                                pe.wait_ge(s["f_b2"], m + 1)
                                y = add_y(m, e, hm[:, m % 2, :], w2, False)
                            else:
                                pe.wait_ge(s["f_g"], 8 + m - HB1 + 1)
                                y = add_y(m, e, hg[:, m % 2, :], w2, last_one)
                            y.then_inc(s["f_y"], 1)

                @block.scalar
                def _(act):
                    A = nc.scalar.activation

                    def xt_copy(st):
                        act.wait_ge(s["xt_ps"], st + 1)
                        A(XT[:, 0, :], bank[6][:, :], ACT.Copy).then_inc(s["xt_a"], 1)

                    def ot_copy(n, tiles):
                        act.wait_ge(s["o_tp"], n + 1)
                        A(OT[:, 0, 0:tiles * P], bank[6][:, 0:tiles * P], ACT.Copy).then_inc(s["o_ta"], 1)

                    xt_copy(0)
                    for blk in range(4):
                        act.wait_ge(s["a_qk"], blk + 1)
                        A(qkf[:, blk, :], bank[blk][:, :], ACT.Identity, bias=col("a_qk")[:, blk:blk + 1],
                          scale=SCALE_A if blk < 2 else 1.0).then_inc(s["a_qkf"], 1)
                    for blk in range(4):
                        act.wait_ge(s["a_qkf"], blk + 1)
                        A(parts[:, 0, blk, :], qkf[:, blk, :], ACT.Copy).then_inc(s["a_hi"], 1)
                    for blk in range(4):
                        act.wait_ge(s["a_r1"], blk + 1)
                        A(parts[:, 1, blk, :], qkf[:, blk, :], ACT.Copy).then_inc(s["a_mid"], 1)

                    n_tiles = H * NJ
                    for i in range(n_tiles + 1):
                        if i < n_tiles:
                            j = i % NJ
                            act.wait_ge(s["a_mx"], i + 1)
                            if i >= 2:
                                act.wait_ge(s["a_tp"], i - 1)
                            A(pb[:, i % 2, 0:P * (j + 1)], bank[i % 2][:, 0:P * (j + 1)], ACT.Exp,
                              bias=nmax[:, i:i + 1], accum_out=rsum[:, i:i + 1]).then_inc(s["a_ex"], 1)
                        if i >= 1 and (i - 1) % 2 == 1:
                            n = i - 1
                            j = n % NJ
                            act.wait_ge(s["a_tp"], n + 1)
                            if n >= 2:
                                act.wait_ge(s["a_pv"], n - 1)
                            A(ptb[:, 1, 0:P * (j + 1)], bank[3][:, 0:P * (j + 1)], ACT.Copy).then_inc(s["a_pta"], 1)
                    ot_copy(0, NT)

                    def cross(tiles, u0):
                        for u in range(2 * tiles):
                            act.wait_ge(s["x_sub"], u0 + u + 1)
                            if u >= 2:
                                act.wait_ge(s["x_tp"], u0 + u - 1)
                                act.wait_ge(s["x_rs"], u0 + u - 1)
                            A(pb[:, u % 2, :], sc[:, u % 2, :, :].rearrange("p a b -> p (a b)"), ACT.Exp)\
                                .then_inc(s["x_ex"], 1)
                            act.wait_ge(s["x_tp"], u0 + u + 1)
                            if u >= 2:
                                act.wait_ge(s["x_pv"], u0 + u - 1)
                            A(ptb[:, u % 2, :], bank[2 + u % 2][:, :], ACT.Copy).then_inc(s["x_pt"], 1)

                    xt_copy(1)
                    for blk in range(KC):
                        act.wait_ge(s["x_q"], blk + 1)
                        A(qT[:, blk, :], bank[2 + blk][:, :], ACT.Identity, bias=col("x0_q")[:, blk:blk + 1],
                          scale=SCALE_X).then_inc(s["x_qt"], 1)
                    cross(NT, 0)
                    ot_copy(1, NT)

                    xt_copy(2)
                    for e in range(NE + 1):
                        if e == 1:
                            act.wait_ge(s["g_a"], 1)
                            A(ga[:, 1], ga[:, 0], ACT.Exp).then_inc(s["g_e"], 1)
                            act.wait_ge(s["g_b"], 2)
                            A(ga[:, 4], ga[:, 2], ACT.Ln).then_inc(s["g_l"], 1)
                        act.wait_ge(s["f_h"], e + 1)
                        if e >= 2:
                            if e == 2:
                                act.wait_ge(s["f_y"], 1)
                            act.wait_ge(s["f_g"], max(e - 2, 1))
                        A(hs[:, e % 2, :], bank[4 + e % 2][:, :], ACT.Silu, bias=col("f0_b1")[:, e:e + 1])\
                            .then_inc(s["f_s"], 1)

                    xt_copy(3)
                    for blk in range(KC):
                        act.wait_ge(s["d_qk"], blk + 1)
                        A(qT[:, blk, :], bank[2 + blk][:, :], ACT.Identity, bias=col("d_q")[:, blk:blk + 1],
                          scale=1.0 / D).then_inc(s["x_qt"], 1)
                    for j in range(NT):
                        act.wait_ge(s["d_mx"], j + 1)
                        A(qkf[:, j, :], bank[2 + j][:, :], ACT.Exp, bias=nmax[:, j:j + 1],
                          accum_out=rsum[:, j:j + 1]).then_inc(s["d_ex"], 1)

                    xt_copy(4)
                    cross(1, 2 * NT)
                    ot_copy(2, 1)

                    xt_copy(5)
                    for n in range(HB1 * (NE + 1)):
                        if n == 1:
                            act.wait_ge(s["g_a"], 2)
                            A(ga[:, 1, :, 0:1], ga[:, 0, :, 0:1], ACT.Exp).then_inc(s["g_e"], 1)
                        act.wait_ge(s["f_h"], 9 + 2 * n + 1)
                        if n >= 2:
                            act.wait_ge(s["f_b2"], n - 1)
                        A(hs[:, n % 2, :], bank[2 + n % 2][:, :], ACT.Silu).then_inc(s["f_s"], 1)

                @block.gpsimd
                def _(pool):
                    expo = const("expo")
                    pool.wait_ge(w_in[0], 64)

                    def add_bias(n, st, name):
                        pool.wait_ge(s["xt_ps"], st + 1)
                        pool.tensor_tensor(X[:], X[:], row(name).unsqueeze(1).to_broadcast([P, NT, D]), ALU.add)\
                            .then_inc(s["x_bias"], 1)

                    def rsqrt(st):
                        pool.wait_ge(s["ln_ag"], NT * (st + 1))
                        pool.tensor_scalar(veps[:], mv[:, :, 1], EPS, None, ALU.add).then_inc(s["ln_ep"], 1)
                        pool.wait_ge(s["ln_ep"], st + 1)
                        pool.tensor_tensor(rstd[:], veps[:], expo[:, 0:NT], ALU.pow).then_inc(s["ln_rs"], 1)

                    add_bias(0, 0, "a_o")
                    rsqrt(0)
                    add_bias(1, 1, "x0_o")
                    rsqrt(1)
                    add_bias(2, 2, "f0_o")
                    pool.wait_ge(s["g_c"], 1)
                    pool.tensor_tensor(ga[:, 6], ga[:, 5], expo[:, 4:5].unsqueeze(1).to_broadcast([P, NT, NE]), ALU.pow)\
                        .then_inc(s["g_p"], 1)
                    rsqrt(2)
                    rsqrt(3)
                    add_bias(3, 4, "x1_o")
                    rsqrt(4)
                    rsqrt(5)

                @block.vector
                def _(v):
                    V = nc.vector

                    def xt_copy(st):
                        v.wait_ge(s["xt_ps"], st + 1)
                        V.tensor_copy(XT[:, 1, :], bank[7][:, :]).then_inc(s["xt_v"], 1)

                    def ot_copy(n, tiles):
                        v.wait_ge(s["o_tp"], n + 1)
                        V.tensor_copy(OT[:, 1, 0:tiles * P], bank[7][:, 0:tiles * P]).then_inc(s["o_tv"], 1)

                    def layernorm(st, banks, n_bias, r0, sums):
                        if n_bias is not None:
                            v.wait_ge(s["x_bias"], n_bias + 1)
                        else:
                            v.wait_ge(s["xt_ps"], st + 1)
                        if len(banks) == 2:
                            for g in range(2):
                                if r0 is not None:
                                    v.wait_ge(s["r_done"], r0 + g + 1)
                                V.tensor_tensor(X[:, 2 * g:2 * g + 2, :],
                                                bank[banks[g]][:, :].rearrange("p (t d) -> p t d", t=2),
                                                X[:, 2 * g:2 * g + 2, :], ALU.add).then_inc(s["ln_sum"], 1)
                        else:
                            v.wait_ge(s["r_done"], r0 + 1)
                            V.tensor_tensor(X[:, 0, :], bank[banks[0]][:, 0:D], X[:, 0, :], ALU.add)\
                                .then_inc(s["ln_sum"], 1)
                        for t in range(NT):
                            v.wait_ge(s["ln_sum"], sums + (t // 2 + 1 if len(banks) == 2 else 1))
                            V.bn_stats(stats[:, t, :], X[:, t, :]).then_inc(s["ln_st"], 1)
                        for t in range(NT):
                            v.wait_ge(s["ln_st"], NT * st + t + 1)
                            V.bn_aggr(mv[:, t, :], stats[:, t, :]).then_inc(s["ln_ag"], 1)
                        v.wait_ge(s["ln_rs"], st + 1)
                        for t in range(NT):
                            V.tensor_scalar(X[:, t, :], X[:, t, :], mv[:, t, 0:1], rstd[:, t:t + 1],
                                            ALU.subtract, ALU.mult).then_inc(s["ln_done"], 1)

                    v.wait_ge(s["pen_in"], 16)
                    V.tensor_scalar(pen[:], mask8[:], GONE, 10.0, ALU.mult, ALU.mult).then_inc(s["pen"], 1)
                    xt_copy(0)
                    for blk in range(4):
                        v.wait_ge(s["a_hi"], blk + 1)
                        V.tensor_tensor(qkf[:, blk, :], qkf[:, blk, :], parts[:, 0, blk, :], ALU.subtract)\
                            .then_inc(s["a_r1"], 1)
                    for g in range(2):
                        v.wait_ge(s["a_v"], g + 1)
                        V.tensor_tensor(vtok[:, 2 * g:2 * g + 2, :],
                                        bank[4 + g][:, :].rearrange("p (t d) -> p t d", t=2),
                                        row("a_v").unsqueeze(1).to_broadcast([P, 2, D]), ALU.add)\
                            .then_inc(s["a_vt"], 1)
                    for blk in range(4):
                        v.wait_ge(s["a_mid"], blk + 1)
                        V.tensor_tensor(parts[:, 2, blk, :], qkf[:, blk, :], parts[:, 1, blk, :], ALU.subtract)\
                            .then_inc(s["a_lo"], 1)

                    v.wait_ge(s["c_tp"], 1)
                    V.tensor_copy(cT[:], bank[7][:, 0:KC * SK].rearrange("p (k n) -> p k n", k=KC)
                                  .unsqueeze(2).to_broadcast([P, KC, 2, SK])).then_inc(s["c_ct"], 1)
                    v.wait_ge(s["c_k"], 1)
                    blkmask = const("blk").unsqueeze(2).to_broadcast([P, 8, SK])

                    def kbank(n, blk):
                        return bank[6][:, (2 * n + blk) * SK:(2 * n + blk + 1) * SK]

                    for blk in range(KC):
                        V.scalar_tensor_tensor(kb[0][:, blk], kbank(0, blk).unsqueeze(1).to_broadcast([P, 8, SK]),
                                               col("x0_k")[:, blk:blk + 1], blkmask, ALU.add, ALU.mult)\
                            .then_inc(s["c_kb0"], 1)
                    rk = const("ropek")
                    for blk in range(KC):
                        V.scalar_tensor_tensor(kr[:, 0, blk], kbank(1, blk), col("x1_k")[:, blk:blk + 1], rk[:, 0:SK],
                                               ALU.add, ALU.mult).then_inc(s["c_ka"], 1)
                        V.scalar_tensor_tensor(kr[:, 1, blk], kbank(2, blk), col("x1_ks")[:, blk:blk + 1],
                                               rk[:, SK:2 * SK], ALU.add, ALU.mult).then_inc(s["c_ka"], 1)
                    v.wait_ge(s["c_ka"], 4)
                    V.tensor_tensor(kr[:, 2], kr[:, 0], kr[:, 1], ALU.add).then_inc(s["c_kc"], 1)
                    v.wait_ge(s["c_kc"], 1)
                    for blk in range(KC):
                        V.tensor_tensor(kb[1][:, blk], kr[:, 2, blk].unsqueeze(1).to_broadcast([P, 8, SK]), blkmask,
                                        ALU.mult).then_inc(s["c_kb1"], 1)
                    v.wait_ge(s["c_v"], 1)
                    for n in range(2):
                        for half in range(2):
                            rows_ = slice(SK * half, SK * half + SK)
                            src = bank[7][rows_, n * D:(n + 1) * D].rearrange("p (a b e) -> p a b e", b=2, e=DH)
                            bias = row(f"x{n}_v")[rows_].rearrange("p (a b e) -> p a b e", b=2, e=DH)
                            V.tensor_tensor(vb[n][rows_, :, half, :], src[:, :, half, :], bias[:, :, half, :], ALU.add)\
                                .then_inc(s["c_vb"], 1)

                    v.wait_ge(s["a_q6"], 16 * 16 * 2 * NTERM)
                    for g in range(4):
                        V.tensor_copy(qpos[0:ROWS6, H * g:H * g + H],
                                      q6[0:ROWS6, :, P * g:P * g + P].rearrange("p c (g r) -> p g c r", r=TR))\
                            .then_inc(s["a_qr"], 1)

                    n_tiles = H * NJ
                    for i in range(n_tiles + 1):
                        if i < n_tiles:
                            j = i % NJ
                            v.wait_ge(s["a_s"], i + 1)
                            V.tensor_reduce(nmax[:, i:i + 1], bank[i % 2][:, 0:P * (j + 1)], AX.X, ALU.max,
                                            negate=True).then_inc(s["a_mx"], 1)
                        if i >= 1 and (i - 1) % 2 == 0:
                            n = i - 1
                            j = n % NJ
                            v.wait_ge(s["a_tp"], n + 1)
                            if n >= 2:
                                v.wait_ge(s["a_pv"], n - 1)
                            V.tensor_copy(ptb[:, 0, 0:P * (j + 1)], bank[2][:, 0:P * (j + 1)]).then_inc(s["a_ptv"], 1)
                    v.wait_ge(s["a_ex"], n_tiles)
                    V.reciprocal(rinv[:], rsum[:]).then_inc(s["a_ri"], 1)
                    v.wait_ge(s["a_ri"], 1)
                    for g in range(2):
                        v.wait_ge(s["a_pv"], 32 * (g + 1))
                        V.tensor_tensor(opos[:, 32 * g:32 * g + 32, :], bank[4 + g][:, :].rearrange("p (n e) -> p n e", e=DH),
                                        rinv[:, 32 * g:32 * g + 32].unsqueeze(2).to_broadcast([P, 32, DH]), ALU.mult)\
                            .then_inc(s["a_on"], 1)
                    ot_copy(0, NT)
                    layernorm(0, (0, 1), 0, 0, 0)

                    def cross(n, tiles, u0, t0, penalty):
                        for u in range(2 * tiles):
                            t, g = divmod(u, 2)
                            cur = sc[:, u % 2]
                            v.wait_ge(s["x_s"], u0 + u + 1)
                            if u >= 2:
                                v.wait_ge(s["x_ex"], u0 + u - 1)
                            V.tensor_tensor(cur, bank[4 + u % 2][:, :].rearrange("p (h k) -> p h k", k=SK),
                                            penalty(t).unsqueeze(1).to_broadcast([P, 8, SK]), ALU.add)\
                                .then_inc(s["x_sm"], 1)
                            v.wait_ge(s["x_sm"], u0 + u + 1)
                            V.tensor_reduce(nmax[:, 8 * (u % 2):8 * (u % 2) + 8], cur, AX.X, ALU.max)\
                                .then_inc(s["x_mx"], 1)
                            v.wait_ge(s["x_mx"], u0 + u + 1)
                            V.tensor_tensor(cur, cur, nmax[:, 8 * (u % 2):8 * (u % 2) + 8].unsqueeze(2)
                                            .to_broadcast([P, 8, SK]), ALU.subtract).then_inc(s["x_sub"], 1)
                            v.wait_ge(s["x_ex"], u0 + u + 1)
                            V.tensor_reduce(rsum[:, 8 * u:8 * u + 8], pb[:, u % 2, :].rearrange("p (h k) -> p h k", k=SK),
                                            AX.X, ALU.add).then_inc(s["x_rs"], 1)
                            if g == 1:
                                v.wait_ge(s["x_rs"], u0 + u + 1)
                                V.reciprocal(rinv[:, H * t:H * t + H], rsum[:, H * t:H * t + H]).then_inc(s["x_ri"], 1)
                                v.wait_ge(s["x_ri"], t0 + t + 1)
                                v.wait_ge(s["x_pv"], u0 + u + 1)
                                V.tensor_tensor(otok[:, t, :].rearrange("p (h e) -> p h e", e=DH),
                                                bank[t % 2][:, 0:D].rearrange("p (h e) -> p h e", e=DH),
                                                rinv[:, H * t:H * t + H].unsqueeze(2).to_broadcast([P, H, DH]), ALU.mult)\
                                    .then_inc(s["x_on"], 1)

                    xt_copy(1)
                    v.wait_ge(s["pen"], 1)
                    cross(0, NT, 0, 0, lambda t: pen[:, t, :])
                    ot_copy(1, NT)
                    layernorm(1, (2, 3), 1, 2, 2)

                    def pick(n, lgv):
                        for t in range(NT):
                            V.max(top[:, t, :], lgv[:, t, :]).then_inc(s["g_mx"], 1)
                        for t in range(NT):
                            v.wait_ge(s["g_mx"], NT * n + t + 1)
                            V.max_index(ix[:, t, :], top[:, t, :], lgv[:, t, :]).then_inc(s["g_ix"], 1)
                        v.wait_ge(s["g_ix"], NT * (n + 1))
                        V.tensor_copy(ixf[:], ix[:]).then_inc(s["g_if"], 1)
                        v.wait_ge(s["g_if"], n + 1)
                        for k in range(2):
                            V.tensor_tensor(oh[:, k], ixf[:, :, k:k + 1].to_broadcast([P, NT, NE]),
                                            const("iota").unsqueeze(1).to_broadcast([P, NT, NE]), ALU.is_equal)\
                                .then_inc(s["g_oh"], 1)
                        v.wait_ge(s["g_oh"], 2 * n + 2)

                    def split3(n):
                        c3 = cmb3[:].rearrange("p t (q e) -> p t q e", q=3)
                        v.wait_ge(s["g_cmb"], n + 1)
                        V.tensor_copy(c3[:, :, 0, :], cmb[:]).then_inc(s["g_h"], 1)
                        v.wait_ge(s["g_h"], 3 * n + 1)
                        V.tensor_tensor(ga[:, 7], cmb[:], c3[:, :, 0, :], ALU.subtract).then_inc(s["g_h"], 1)
                        v.wait_ge(s["g_h"], 3 * n + 2)
                        V.tensor_copy(c3[:, :, 1, :], ga[:, 7]).then_inc(s["g_h"], 1)
                        v.wait_ge(s["g_h"], 3 * n + 3)
                        V.tensor_tensor(c3[:, :, 2, :], ga[:, 7], c3[:, :, 1, :], ALU.subtract).then_inc(s["g_lo"], 1)
                        v.wait_ge(s["g_tp"], n + 1)
                        V.tensor_copy(cmb3T[:], bank[6][:, :].bitcast(BF16)[0:3 * NE, 0:S]).then_inc(s["g_ct"], 1)
                        V.tensor_copy(cmbT[:], bank[7][0:NE, :]).then_inc(s["g_ct"], 1)

                    xt_copy(2)
                    v.wait_ge(s["g_lg"], 1)
                    V.tensor_tensor(lg[:], bank[2][:, 0:NT * NE].rearrange("p (t e) -> p t e", e=NE),
                                    row("f0_r").unsqueeze(1).to_broadcast([P, NT, NE]), ALU.add).then_inc(s["g_ls"], 1)
                    v.wait_ge(s["g_ls"], 1)
                    V.scalar_tensor_tensor(ga[:, 0], lg[:], -1.0, lg[:], ALU.mult, ALU.min).then_inc(s["g_a"], 1)
                    pick(0, lg)
                    v.wait_ge(s["g_e"], 1)
                    V.tensor_scalar(ga[:, 2], ga[:, 1], 1.0, None, ALU.add).then_inc(s["g_b"], 1)
                    v.wait_ge(s["g_b"], 1)
                    V.tensor_scalar(ga[:, 3], ga[:, 2], -1.0, None, ALU.add).then_inc(s["g_b"], 1)
                    v.wait_ge(s["g_b"], 2)
                    V.tensor_scalar(ga[:, 5], ga[:, 3], 0.0, None, ALU.is_equal).then_inc(s["g_b"], 1)
                    V.tensor_scalar(ga[:, 6], ga[:, 3], 1e-30, None, ALU.max).then_inc(s["g_b"], 1)
                    v.wait_ge(s["g_b"], 4)
                    V.reciprocal(ga[:, 3], ga[:, 6]).then_inc(s["g_b"], 1)
                    V.tensor_tensor(ga[:, 7], ga[:, 5], ga[:, 1], ALU.mult).then_inc(s["g_b"], 1)
                    v.wait_ge(s["g_b"], 6)
                    V.tensor_tensor(ga[:, 5], ga[:, 3], ga[:, 1], ALU.mult).then_inc(s["g_b"], 1)
                    v.wait_ge(s["g_b"], 7)
                    v.wait_ge(s["g_l"], 1)
                    V.tensor_tensor(ga[:, 3], ga[:, 5], ga[:, 4], ALU.mult).then_inc(s["g_b"], 1)
                    v.wait_ge(s["g_b"], 8)
                    V.tensor_tensor(ga[:, 6], ga[:, 3], ga[:, 7], ALU.add).then_inc(s["g_b"], 1)
                    v.wait_ge(s["g_b"], 9)
                    V.scalar_tensor_tensor(ga[:, 5], lg[:], 0.0, ga[:, 6], ALU.max, ALU.add).then_inc(s["g_c"], 1)
                    V.tensor_tensor(ga[:, 3], oh[:, 0], oh[:, 1], ALU.add).then_inc(s["g_sum"], 1)
                    v.wait_ge(s["g_sum"], 1)
                    v.wait_ge(s["g_p"], 1)
                    V.tensor_tensor(cmb[:], ga[:, 6], ga[:, 3], ALU.mult).then_inc(s["g_cmb"], 1)
                    split3(0)
                    for e in range(1, NE + 1):
                        v.wait_ge(s["f_cb"], e)
                        v.wait_ge(s["f_s"], e + 1)
                        if e >= 3:
                            v.wait_ge(s["f_y"], e - 1)
                        V.tensor_tensor(hg[:, e % 2, :], bank[6 + e % 2][:, :], hs[:, e % 2, :], ALU.mult)\
                            .then_inc(s["f_g"], 1)
                    layernorm(2, (0, 1), 2, 4, 4)

                    xt_copy(3)
                    for blk in range(KC):
                        v.wait_ge(s["d_qk"], 3 + blk)
                        V.tensor_scalar(kT[:, blk, :], bank[4 + blk][:, :], col("d_k")[:, blk:blk + 1], None, ALU.add)\
                            .then_inc(s["d_ev"], 1)
                    for g in range(2):
                        v.wait_ge(s["d_v"], g + 1)
                        V.tensor_tensor(vtok[:, 2 * g:2 * g + 2, :],
                                        bank[6 + g][:, :].rearrange("p (t d) -> p t d", t=2),
                                        row("d_v").unsqueeze(1).to_broadcast([P, 2, D]), ALU.add)\
                            .then_inc(s["d_ev"], 1)
                    for j in range(NT):
                        v.wait_ge(s["d_s"], j + 1)
                        V.tensor_reduce(nmax[:, j:j + 1], bank[2 + j][:, :], AX.X, ALU.max, negate=True)\
                            .then_inc(s["d_mx"], 1)
                    v.wait_ge(s["d_ev"], 4)
                    for j in range(NT):
                        v.wait_ge(s["d_ex"], j + 1)
                        V.reciprocal(rinv[:, j:j + 1], rsum[:, j:j + 1]).then_inc(s["d_rz"], 1)
                        v.wait_ge(s["d_rz"], j + 1)
                        V.tensor_scalar(vtok[:, j, :], vtok[:, j, :], rinv[:, j:j + 1], None, ALU.mult)\
                            .then_inc(s["d_vn"], 1)
                    layernorm(3, (0, 1), None, 6, 6)

                    xt_copy(4)
                    v.wait_ge(s["x_q"], 3)
                    rq = const("ropeq")
                    for n, name in enumerate(("x1_q", "x1_qs")):
                        for blk in range(KC):
                            V.scalar_tensor_tensor((hs if n == 0 else hm)[:, 0, blk * P:(blk + 1) * P],
                                                   bank[2][:, (2 * n + blk) * P:(2 * n + blk + 1) * P],
                                                   col(name)[:, blk:blk + 1], rq[:, n * P:(n + 1) * P],
                                                   ALU.add, ALU.mult).then_inc(s["x_qa"], 1)
                    v.wait_ge(s["x_qa"], 4)
                    for blk in range(KC):
                        V.tensor_tensor(qT[:, blk, 0:P], hs[:, 0, blk * P:(blk + 1) * P], hm[:, 0, blk * P:(blk + 1) * P],
                                        ALU.add).then_inc(s["x_qt"], 1)
                    cross(1, 1, 2 * NT, NT, lambda t: const("window"))
                    ot_copy(2, 1)
                    layernorm(4, (0,), 3, 8, 8)

                    xt_copy(5)
                    v.wait_ge(s["g_lg"], 2)
                    V.tensor_copy(lg[:], bank[2][:, 0:NT * NE].rearrange("p (t e) -> p t e", e=NE))\
                        .then_inc(s["g_ls"], 1)
                    v.wait_ge(s["g_ls"], 2)
                    pick(1, lg)
                    V.tensor_tensor(ga[:, 0, :, 0:1], top[:, :, 1:2], top[:, :, 0:1], ALU.subtract)\
                        .then_inc(s["g_a"], 1)

                    def hidden(n):
                        v.wait_ge(s["f_s"], 9 + n + 1)
                        v.wait_ge(s["f_h"], 9 + 2 * n + 2)
                        if n >= 2:
                            e_, _ = divmod(n - 2, HB1)
                            v.wait_ge(s["f_y"], 9 + n - 1)
                        V.tensor_tensor(hm[:, n % 2, :], bank[4 + n % 2][:, :], hs[:, n % 2, :], ALU.mult)\
                            .then_inc(s["f_b2"], 1)

                    hidden(0)
                    v.wait_ge(s["g_e"], 2)
                    V.tensor_scalar(ga[:, 2, :, 0:1], ga[:, 1, :, 0:1], 1.0, None, ALU.add).then_inc(s["g_b"], 1)
                    v.wait_ge(s["g_b"], 10)
                    V.reciprocal(ga[:, 3, :, 0:1], ga[:, 2, :, 0:1]).then_inc(s["g_b"], 1)
                    v.wait_ge(s["g_b"], 11)
                    V.tensor_tensor(ga[:, 4, :, 0:1], ga[:, 3, :, 0:1], ga[:, 1, :, 0:1], ALU.mult)\
                        .then_inc(s["g_b"], 1)
                    V.tensor_tensor(ga[:, 5], oh[:, 0], ga[:, 3, :, 0:1].to_broadcast([P, NT, NE]), ALU.mult)\
                        .then_inc(s["g_b"], 1)
                    v.wait_ge(s["g_b"], 13)
                    V.tensor_tensor(ga[:, 6], oh[:, 1], ga[:, 4, :, 0:1].to_broadcast([P, NT, NE]), ALU.mult)\
                        .then_inc(s["g_b"], 1)
                    v.wait_ge(s["g_b"], 14)
                    V.tensor_tensor(cmb[:], ga[:, 5], ga[:, 6], ALU.add).then_inc(s["g_cmb"], 1)
                    hidden(1)
                    hidden(2)
                    hidden(3)
                    split3(1)
                    for n in range(HB1, HB1 * (NE + 1)):
                        hidden(n)
                        e = n // HB1
                        v.wait_ge(s["f_b2"], n + 1)
                        v.wait_ge(s["f_cb"], 8 + e)
                        V.tensor_tensor(hg[:, n % 2, :], bank[6 + e % 2][:, :], hm[:, n % 2, :], ALU.mult)\
                            .then_inc(s["f_g"], 1)
                    v.wait_ge(s["f_y"], 9 + HB1 * (NE + 1))
                    layernorm(5, (0, 1), None, None, 9)

            nc.all_engine_barrier()
            order = list(s.values())
            engines = (nc.gpsimd, nc.sync, nc.scalar, nc.vector, nc.tensor)
            for n, sem_ in enumerate(order):
                engines[n % 5].sem_clear(sem_)
            nc.all_engine_barrier()


def kernel(**inputs):
    import numpy as np
    import concourse.bacc as bacc
    from concourse.bass_utils import run_bass_kernel_spmd

    g = {k: np.asarray(v) for k, v in inputs.items()}

    def chunks(a):
        return np.ascontiguousarray(a.reshape(-1, P, a.shape[1]).transpose(1, 0, 2)).reshape(P, -1)

    e = np.arange(DH)
    third = [(np.arange(H)[:, None] * 3 * DH + n * DH + e[None, :]).ravel() for n in range(3)]
    f = np.arange(D)
    swap = (f // DH) * DH + (f % DH + DH // 2) % DH
    wqkv, bqkv = g["L0_attn_W_qkv"], g["L0_attn_b_qkv"]
    w1 = np.concatenate([g["L0_ffn_sW1"][None], g["L0_ffn_rW1"]])
    w2 = np.concatenate([g["L0_ffn_sW2"][None], g["L0_ffn_rW2"]])
    W1 = g["L1_attn_W"]
    mats = {"a_qk": np.concatenate([wqkv[:, third[0]], wqkv[:, third[1]]], 1), "a_v": wqkv[:, third[2]],
            "a_o": g["L0_attn_W_out"],
            "x0_q": g["L0_xattn_Wq"].T, "x0_k": g["L0_xattn_Wk"].T, "x0_v": g["L0_xattn_Wv"].T,
            "x0_o": g["L0_xattn_Wo"].T, "f0_r": g["L0_ffn_routing_W"].T,
            "f0_w1": w1.transpose(1, 0, 2).reshape(D, -1),
            "d_q": W1[0:D].T, "d_k": W1[D:2 * D].T, "d_v": W1[2 * D:].T,
            "x1_q": g["L1_xattn_q_w"].T, "x1_qs": g["L1_xattn_q_w"][swap].T,
            "x1_k": g["L1_xattn_k_w"].T, "x1_ks": g["L1_xattn_k_w"][swap].T,
            "x1_v": g["L1_xattn_v_w"].T, "x1_o": g["L1_xattn_o_w"].T, "f1_r": g["L1_ffn_w_router"]}
    packed = {n: chunks(a) for n, a in mats.items()}
    packed["f0_w2"] = w2.transpose(1, 0, 2).reshape(P, -1)
    weights = np.concatenate([packed[n] for n in W_COLS], 1)
    b1 = g["L1_attn_b"]
    row_of = {"a_v": bqkv[third[2]], "a_o": g["L0_attn_b_out"], "x0_v": g["L0_xattn_bv"], "x0_o": g["L0_xattn_bo"],
              "f0_o": g["L0_ffn_sb2"], "d_v": b1[2 * D:], "x1_v": g["L1_xattn_v_b"], "x1_o": g["L1_xattn_o_b"],
              "f0_r": g["L0_ffn_expert_bias"]}
    rows = np.concatenate([row_of[n] for n in ROW_COLS])
    col_of = {"a_qk": np.concatenate([bqkv[third[0]], bqkv[third[1]]]), "x0_q": g["L0_xattn_bq"],
              "x0_k": g["L0_xattn_bk"], "d_q": b1[0:D], "d_k": b1[D:2 * D],
              "x1_q": g["L1_xattn_q_b"], "x1_qs": g["L1_xattn_q_b"][swap],
              "x1_k": g["L1_xattn_k_b"], "x1_ks": g["L1_xattn_k_b"][swap],
              "f0_b1": np.concatenate([g["L0_ffn_sb1"][None], g["L0_ffn_rb1"]]).ravel()}
    cols = np.concatenate([col_of[n].reshape(-1, P).T for n in COL_COLS], 1)
    experts = np.stack([np.concatenate([chunks(a), chunks(b), chunks(c)], 1) for a, b, c in
                        [(g["L1_ffn_sw1"], g["L1_ffn_sw3"], g["L1_ffn_sw2"])] +
                        [(g["L1_ffn_w1"][i], g["L1_ffn_w3"][i], g["L1_ffn_w2"][i]) for i in range(NE)]])

    p = np.arange(P)
    pos = (p % TR) * H + p // TR
    half = DH // 2
    freqs = (1.0 / 10000.0 ** (np.arange(half, dtype=np.float32) / half)).astype(np.float32)
    ang = np.arange(P, dtype=np.float32)[None, :] * freqs[p % half][:, None]
    sign = np.where(p % DH < half, -1.0, 1.0)[:, None]
    cos, sin = np.cos(ang), np.sin(ang) * sign
    keys = np.arange(SK)[None, :]
    sel = np.zeros((P, NE, P))
    for r in range(3 * NE):
        sel[r, r % NE, :] = 1
    const_of = {"ident": np.eye(P), "causal": np.where(pos[None, :] <= pos[:, None], 0.0, -2.0 ** 100),
                "window": np.where((keys <= p[:, None]) & (keys >= p[:, None] - 64), 0.0, -2.0 ** 100),
                "sel": sel.reshape(P, -1), "blk": p[:, None] // DH == np.arange(8)[None, :],
                "ropeq": np.concatenate([cos, sin], 1) * SCALE_X,
                "ropek": np.concatenate([cos[:, 0:SK], sin[:, 0:SK]], 1),
                "iota": np.tile(np.arange(8), (P, 1)), "expo": np.tile([-0.5] * 4 + [0.5] * 4, (P, 1))}
    consts = np.concatenate([np.asarray(const_of[n], np.float32) for n in CONST_COLS], 1)

    arrays = {"x": g["x"], "ctx": g["ctx_1024"], "mask": g["mask_Bx1xSxS2_bf0"].reshape(B, S, SK),
              "weights": weights, "rows": rows, "cols": cols, "consts": consts, "b2": g["L0_ffn_rb2"],
              "experts": experts}
    nc = bacc.Bacc("TRN2", target_bir_lowering=False, num_devices=1)
    feed, args = {}, []
    for name, a in arrays.items():
        a = np.ascontiguousarray(a)
        feed[f"in_{name}"] = a
        args.append(nc.dram_tensor(f"in_{name}", a.shape, mybir.dt.from_np(a.dtype), kind="ExternalInput").ap())
    args.append(nc.dram_tensor("result", (B, S, D), F32, kind="ExternalOutput").ap())
    args.append(nc.dram_tensor("v_scr", (S, D), F32, kind="Internal").ap())
    args.append(nc.dram_tensor("o_scr", (S, D), F32, kind="Internal").ap())
    decoder(nc, *args)
    r = run_bass_kernel_spmd(nc, [feed], core_ids=[0])
    return r.results[0]["result"]
```

```python
from contextlib import ExitStack

import concourse.bass as bass
from concourse import mybir

F32 = mybir.dt.float32
BF16 = mybir.dt.bfloat16
U8 = mybir.dt.uint8
U32 = mybir.dt.uint32
ALU = mybir.AluOpType
ACT = mybir.ActivationFunctionType
AX = mybir.AxisListType

P = 128
B, S, D = 4, 512, 256
NT, KC = S // P, D // P
H, DH = 16, 16
SK = 64
NE = 8
HID1 = 512
HB1 = HID1 // P
EPS = 1e-5
NJ = 4
HT = S // H
TR = HT // NJ
TERMS_Q = (0, 0, 1, 1, 0, 2)
TERMS_K = (0, 1, 0, 1, 2, 0)
NTERM = len(TERMS_Q)
ROWS6 = NTERM * DH
SCALE_A = float(2 * D) ** -0.5
SCALE_X = float(DH) ** -0.5
GONE = -3e38

W_COLS = {"a_qk": 1024, "a_v": 512, "a_o": 512,
          "x0_q": 512, "x0_k": 512, "x0_v": 512, "x0_o": 512,
          "f0_r": 16, "f0_w1": 2 * 9 * 128, "f0_w2": 9 * 256,
          "d_q": 512, "d_k": 512, "d_v": 512,
          "x1_q": 512, "x1_qs": 512, "x1_k": 512, "x1_ks": 512, "x1_v": 512, "x1_o": 512,
          "f1_r": 16}
ROW_COLS = {"a_v": 256, "a_o": 256, "x0_v": 256, "x0_o": 256, "f0_o": 256, "d_v": 256,
            "x1_v": 256, "x1_o": 256, "f0_r": 8}
COL_COLS = {"a_qk": 4, "x0_q": 2, "x0_k": 2, "d_q": 2, "d_k": 2, "x1_q": 2, "x1_qs": 2,
            "x1_k": 2, "x1_ks": 2, "f0_b1": 9}
CONST_COLS = {"ident": 128, "causal": 128, "window": 64, "blk": 8,
              "ropeq": 256, "ropek": 128, "iota": 8, "expo": 8}


def offsets(cols):
    at, out = 0, {}
    for name, n in cols.items():
        out[name] = (at, at + n)
        at += n
    return out, at


WO, W_ALL = offsets(W_COLS)
RO, R_ALL = offsets(ROW_COLS)
CO, C_ALL = offsets(COL_COLS)
KO, K_ALL = offsets(CONST_COLS)

SEMS = """x_in ctx_in pen_in xt_ps xt_a xt_v x_bias
ln_sum ln_st ln_ag ln_ep ln_rs ln_done r_done
a_qk a_qkf a_hi a_r1 a_mid a_lo a_ps0 a_ps1 a_ps2 a_q6 a_v a_vt a_vd a_vre
a_qr a_s a_mx a_ex a_tp a_ptv a_pta a_pv a_ri a_on a_od a_ot
o_tp o_ta o_tv
c_tp c_ct c_k c_v c_kb0 c_ka c_kc c_kb1 c_vb pen
x_q x_qt x_qa x_s x_sm x_mx x_sub x_ex x_rs x_tp x_pt x_pv x_ri x_on
g_lg g_ls g_mx g_ix g_if g_oh g_sum g_a g_e g_b g_l g_c g_p g_cmb
e_h e_s e_y e_ev e_tp e_ct
d_qk d_ev d_v d_s d_mx d_ex d_rz d_vn
f_w0 f_w1 f_w2 f_w3 f_h f_s f_m f_y f_ev f_st f_ag f_ep f_rs f_ln f_out""".split()

CH = HB1 * (NE + 1)
FS = 2 * CH
SLOTS = FS + 5
HALF = S // 2
NBUF = 4




def decoder(nc, x, ctx_in, mask, weights, rows, cols, consts, b2rows, experts, out, v_scr, o_scr, p_scr):
    with ExitStack() as ctx:
        def sb(name, shape, dt=F32):
            return ctx.enter_context(nc.sbuf_tensor(name, shape, dt))

        W = sb("W", [P, W_ALL])
        BR = sb("BR", [P, R_ALL])
        BC = sb("BC", [P, C_ALL])
        K = sb("K", [P, K_ALL])
        b2 = sb("b2", [NE, D])
        identb = sb("identb", [P, P], BF16)
        causalb = sb("causalb", [P, P], BF16)
        X = sb("X", [P, NT, D])
        XT = sb("XT", [P, KC, S])
        XF = sb("XF", [P, NT, D])
        XTF = sb("XTF", [P, KC, S])
        wbuf = sb("wbuf", [P, NBUF, 768])
        hsF = sb("hsF", [P, 2, HALF])
        hmF = sb("hmF", [P, 2, HALF])
        cmbF = sb("cmbF", [P, NT, NE])
        stats = sb("stats", [P, 2, NT, 6])
        mv = sb("mv", [P, 2, NT, 2])
        veps = sb("veps", [P, 2, NT])
        rstd = sb("rstd", [P, 2, NT])

        r_q6 = sb("r_q6", [P, 4, 1024])
        q6 = r_q6[:].rearrange("p a b -> p (a b)").bitcast(BF16).rearrange("p (c s) -> p c s", c=H)
        otok = r_q6[:, 0, :].rearrange("p (t d) -> p t d", t=NT)
        OT = r_q6[:, 1, :].rearrange("p (k s) -> p k s", k=KC)
        qT = r_q6[:, 2, :].rearrange("p (k s) -> p k s", k=KC)
        sc = r_q6[:, 3, :].rearrange("p (u h k) -> p u h k", u=2, k=SK)
        r_qpos = sb("r_qpos", [P, 4, 1024])
        qpos = r_qpos[:].rearrange("p a b -> p (a b)").bitcast(BF16).rearrange("p (g c r) -> p g c r", c=H, r=TR)
        kT = r_qpos[:, 0, :].rearrange("p (k s) -> p k s", k=KC)
        hs = r_qpos[:, 1, :].rearrange("p (u s) -> p u s", u=2)
        ex = r_qpos[:, 2:4, :].rearrange("p a (b s) -> p (a b) s", b=2)
        k6 = sb("k6", [P, H, S], BF16)
        r_parts = sb("r_parts", [P, 3072])
        parts = r_parts[:].bitcast(BF16).rearrange("p (q b s) -> p q b s", q=3, b=4)
        pb = r_parts[:, 0:1024].rearrange("p (u s) -> p u s", u=2)
        ptb = r_parts[:, 1024:2048].rearrange("p (u s) -> p u s", u=2)
        qkf = sb("qkf", [P, 4, S])
        vpos = qkf[:, 0:2, :].rearrange("p a (g e) -> p (a g) e", e=DH)
        opos = qkf[:, 2:4, :].rearrange("p a (g e) -> p (a g) e", e=DH)
        vtok = sb("vtok", [P, NT, D])
        nmax = sb("nmax", [P, H * NJ])
        rsum = sb("rsum", [P, H * NJ])
        rinv = sb("rinv", [P, H * NJ])
        ctok = sb("ctok", [SK, D])
        cT = sb("cT", [P, KC, 2, SK])
        kb = [sb(f"kb{i}", [P, KC, 8, SK]) for i in range(2)]
        kr = sb("kr", [P, 3, KC, SK])
        vb = [sb(f"vb{i}", [P, H // 2, 2, DH]) for i in range(2)]
        mask8 = sb("mask8", [P, NT, SK], U8)
        pen = sb("pen", [P, NT, SK])
        lg = sb("lg", [P, NT, NE])
        top = sb("top", [P, NT, 8])
        ix = sb("ix", [P, NT, 8], U32)
        ixf = sb("ixf", [P, NT, 8])
        oh = sb("oh", [P, 2, NT, NE])
        ga = sb("ga", [P, 8, NT, NE])
        cmb = sb("cmb", [P, NT, NE])
        cmbT = sb("cmbT", [NE, S])
        bank = [ctx.enter_context(nc.psum_tensor(f"bank{i}", [P, 512], F32)) for i in range(8)]
        M = bank[0:4]
        FH, FY = bank[4:6], bank[6:8]
        s = {n: ctx.enter_context(nc.semaphore(n)) for n in SEMS}
        w_in = [ctx.enter_context(nc.semaphore(f"w_in{i}")) for i in range(4)]
        setup = ctx.enter_context(nc.semaphore("setup"))
        cast = ctx.enter_context(nc.semaphore("cast"))

        def w(name):
            a, b = WO[name]
            return W[:, a:b].rearrange("p (k n) -> p k n", k=KC)

        def row(name):
            a, b = RO[name]
            return BR[:, a:b]

        def col(name):
            a, b = CO[name]
            return BC[:, a:b]

        def const(name):
            a, b = KO[name]
            return K[:, a:b]

        ident = const("ident")
        a, b = WO["f0_w2"]
        f0_w2 = W[:, a:b].rearrange("p (e n) -> p e n", e=9)

        with nc.Block() as first:
            @first.sync
            def _(sp):
                sp.dma_start(K[:, :], consts).then_inc(w_in[0], 16)
                sp.dma_start(BC[:, :], cols).then_inc(w_in[0], 16)
                sp.dma_start(BR[:, :], rows.partition_broadcast(P)).then_inc(w_in[0], 16)
                sp.dma_start(b2[:, :], b2rows).then_inc(w_in[0], 16)
                cut = [0, WO["x0_q"][0], WO["d_q"][0], W_ALL]
                for i in range(3):
                    sp.dma_start(W[:, cut[i]:cut[i + 1]], weights[:, cut[i]:cut[i + 1]]).then_inc(w_in[i + 1], 16)

            @first.vector
            def _(v):
                v.memset(vb[0][:], 0.0).then_inc(setup, 1)
                v.memset(vb[1][:], 0.0).then_inc(setup, 1)
                v.wait_ge(w_in[0], 64)
                v.tensor_copy(identb[:], ident).then_inc(cast, 1)
                v.tensor_copy(causalb[:], const("causal")).then_inc(cast, 1)
                v.tensor_scalar_mul(col("a_qk")[:, 0:2], col("a_qk")[:, 0:2], SCALE_A).then_inc(cast, 1)
                v.tensor_scalar_mul(col("x0_q"), col("x0_q"), SCALE_X).then_inc(cast, 1)
                v.tensor_scalar_mul(col("d_q"), col("d_q"), 1.0 / D).then_inc(cast, 1)
                v.wait_ge(cast, 5)
                v.wait_ge(setup, 2)

        def step(front, back):
            with nc.Block() as block:
                def slots(slot):
                    at = [0]

                    def run(n):
                        if back is not None:
                            for k in range(at[0], min(at[0] + n, SLOTS)):
                                slot(k)
                            at[0] = min(at[0] + n, SLOTS)
                    return run

                @block.sync
                def _(sp):
                    def load_chunk(c):
                        if c >= NBUF:
                            sp.wait_ge(s["f_y"], 2 * (c - NBUF) + 2)
                        sp.dma_start(wbuf[:, c % NBUF, :], experts[c]).then_inc(s[f"f_w{c % NBUF}"], 16)

                    def slot(k):
                        if k % 2 == 0 and k // 2 + 2 < CH:
                            load_chunk(k // 2 + 2)
                        if k == SLOTS - 1:
                            sp.wait_ge(s["f_ln"], NT)
                            sp.dma_start(out[bass.ds(back, 1)].rearrange("a (t p) d -> (a p) t d", p=P), XF[:])\
                                .then_inc(s["f_out"], 16)

                    fill = slots(slot)
                    if front is not None:
                        one = bass.ds(front, 1)
                        sp.dma_start(X[:], x[one].rearrange("a (t p) d -> (a p) t d", p=P)).then_inc(s["x_in"], 16)
                        sp.dma_start(ctok[:], ctx_in[one].rearrange("a p d -> (a p) d")).then_inc(s["ctx_in"], 16)
                        sp.dma_start(mask8[:], mask[one].rearrange("a (t p) k -> (a p) t k", p=P))\
                            .then_inc(s["pen_in"], 16)
                    if back is not None:
                        load_chunk(0)
                        load_chunk(1)
                    if front is not None:
                        for part, ready in ((0, "a_hi"), (1, "a_mid"), (2, "a_lo")):
                            sp.wait_ge(s[ready], 4)
                            sp.dma_start(p_scr[part].rearrange("b p s -> p b s"), parts[:, part])\
                                .then_inc(s[f"a_ps{part}"], 16)
                        for part in range(3):
                            sp.wait_ge(s[f"a_ps{part}"], 16)
                            for dst, base, terms in ((q6, 0, TERMS_Q), (k6, 2, TERMS_K)):
                                src = p_scr[part, base:base + 2].rearrange("b (c e) s -> e (b c) s", e=DH)
                                for n, term in enumerate(terms):
                                    if term == part:
                                        sp.dma_start(dst[DH * n:DH * n + DH], src).then_inc(s["a_q6"], 16)
                        sp.wait_ge(s["a_vt"], 2)
                        sp.dma_start(v_scr.rearrange("(t p) f -> p t f", p=P), vtok[:]).then_inc(s["a_vd"], 16)
                        sp.wait_ge(s["a_vd"], 16)
                        sp.wait_ge(s["a_lo"], 4)
                        v_src = v_scr.rearrange("(g r) (c e) -> r c g e", r=TR, e=DH)
                        for r in range(TR):
                            sp.dma_start(vpos[r:P:TR], v_src[r]).then_inc(s["a_vre"], 16)
                        fill(6)
                        fill(33)
                        sp.wait_ge(s["a_on"], 2)
                        o_dst = o_scr.rearrange("(g r) (c e) -> r c g e", r=TR, e=DH)
                        for r in range(TR):
                            sp.dma_start(o_dst[r], opos[r:P:TR]).then_inc(s["a_od"], 16)
                        sp.wait_ge(s["a_od"], 16 * TR)
                        sp.dma_start(otok, o_scr.rearrange("(t p) f -> p t f", p=P)).then_inc(s["a_ot"], 16)
                    fill(SLOTS)
                    if back is not None:
                        sp.wait_ge(s["f_out"], 16)

                @block.tensor
                def _(pe):
                    mm, tr = nc.tensor.matmul, nc.tensor.transpose

                    def feature_major(dst, wt, m0, rhs):
                        for k in range(KC):
                            last = mm(dst, wt[:, k, m0:m0 + P], rhs[:, k, :], start=(k == 0), stop=(k == KC - 1))
                        return last

                    def token_major(dst, src, t, wt):
                        for k in range(KC):
                            last = mm(dst, src[:, k, t * P:(t + 1) * P], wt[:, k, :],
                                      start=(k == 0), stop=(k == KC - 1))
                        return last

                    def slot(k):
                        if k < FS:
                            c, half = divmod(k, 2)
                            wc = wbuf[:, c % NBUF]
                            if half == 0:
                                pe.wait_ge(s[f"f_w{c % NBUF}"], 16 * (c // NBUF + 1))
                            if k >= 2:
                                pe.wait_ge(s["f_m"], k - 1)
                            for n in range(2):
                                for kc in range(KC):
                                    last = mm(FH[k % 2][:, n * HALF:(n + 1) * HALF],
                                              wc[:, (2 * n + kc) * P:(2 * n + kc + 1) * P],
                                              XTF[:, kc, half * HALF:(half + 1) * HALF],
                                              start=(kc == 0), stop=(kc == KC - 1))
                            last.then_inc(s["f_h"], 1)
                        if 2 <= k < FS + 2:
                            j = k - 2
                            c, half = divmod(j, 2)
                            e, hb = divmod(c, HB1)
                            pe.wait_ge(s["f_m"], j + 1)
                            if hb == 0 and e >= 1:
                                pe.wait_ge(s["f_ev"], 2 * (e - 1) + half + 1)
                            for t in range(2):
                                last = mm(FY[half][:, t * D:(t + 1) * D], hmF[:, j % 2, t * P:(t + 1) * P],
                                          wbuf[:, c % NBUF, 512:768], start=(hb == 0 and t == 0),
                                          stop=(hb == HB1 - 1), skip_group_check=True)
                            last.then_inc(s["f_y"], 1)

                    fill = slots(slot)
                    if front is None:
                        fill(SLOTS)
                        return

                    def turn_x(st, src):
                        for t in range(NT):
                            if st == 0:
                                pe.wait_ge(s["x_in"], 16)
                            else:
                                pe.wait_ge(s["ln_done"], NT * (st - 1) + t + 1)
                            for k in range(KC):
                                last = tr(M[2 + k][:, t * P:(t + 1) * P], src[:, t, k * P:(k + 1) * P], ident)
                        last.then_inc(s["xt_ps"], 1)
                        pe.wait_ge(s["xt_a"], st + 1)
                        pe.wait_ge(s["xt_v"], st + 1)

                    def project(n_o, wt, tiles):
                        for t in range(tiles):
                            for k in range(KC):
                                last = tr(M[2 + k][:, t * P:(t + 1) * P], otok[:, t, k * P:(k + 1) * P], ident)
                        last.then_inc(s["o_tp"], 1)
                        pe.wait_ge(s["o_ta"], n_o + 1)
                        pe.wait_ge(s["o_tv"], n_o + 1)
                        for t in range(tiles):
                            last = token_major(M[t // 2][:, (t % 2) * D:(t % 2 + 1) * D], OT, t, wt)
                            if t % 2 == 1 or t == tiles - 1:
                                last.then_inc(s["r_done"], 1)

                    pe.wait_ge(w_in[0], 64)
                    pe.wait_ge(w_in[1], 16)
                    turn_x(0, X)
                    for blk in range(4):
                        feature_major(M[blk][:, :], w("a_qk"), blk * P, XT).then_inc(s["a_qk"], 1)
                    for t in range(NT):
                        if t % 2 == 0:
                            pe.wait_ge(s["a_qkf"], t // 2 + 1)
                        last = token_major(M[t // 2][:, (t % 2) * D:(t % 2 + 1) * D], XT, t, w("a_v"))
                        if t % 2:
                            last.then_inc(s["a_v"], 1)

                    pe.wait_ge(s["ctx_in"], 16)
                    pe.wait_ge(s["a_qkf"], 3)
                    for k in range(KC):
                        last = tr(M[2][:, k * SK:(k + 1) * SK], ctok[:, k * P:(k + 1) * P], ident[0:SK, 0:SK])
                    last.then_inc(s["c_tp"], 1)
                    pe.wait_ge(s["c_ct"], 1)
                    pe.wait_ge(s["a_qkf"], 4)
                    pe.wait_ge(w_in[2], 16)
                    pe.wait_ge(w_in[3], 16)
                    for n, name in enumerate(("x0_k", "x1_k", "x1_ks")):
                        for blk in range(KC):
                            at = (2 * n + blk) * SK
                            for k in range(KC):
                                last = mm(M[3][:, at:at + SK], w(name)[:, k, blk * P:(blk + 1) * P],
                                          cT[:, k, 0, :], start=(k == 0), stop=(k == KC - 1))
                    last.then_inc(s["c_k"], 1)
                    for n in range(2):
                        for k in range(KC):
                            last = mm(M[2][:, n * D:(n + 1) * D], cT[:, k, :, :], w(f"x{n}_v")[:, k, :],
                                      start=(k == 0), stop=(k == KC - 1))
                    last.then_inc(s["c_v"], 1)
                    fill(6)

                    n_tiles = H * NJ
                    for i in range(n_tiles + 2):
                        if i < n_tiles:
                            h, j = divmod(i, NJ)
                            if i < 2:
                                pe.wait_ge(s["a_vt"], i + 1)
                            else:
                                pe.wait_ge(s["a_ex"], i - 1)
                            if i % H == 0:
                                pe.wait_ge(s["a_qr"], i // H + 1)
                            tok = HT * h
                            ks = k6[0:ROWS6, :, tok:tok + TR * (j + 1)].rearrange("p c (j r) -> p j c r", r=TR)
                            mm(M[i % 2][:, 0:P * (j + 1)], qpos[0:ROWS6, i, :, :], ks, start=True, stop=True)
                            mm(M[i % 2][:, P * j:P * (j + 1)], identb[:], causalb[:], start=False, stop=True,
                               skip_group_check=True).then_inc(s["a_s"], 1)
                        if 1 <= i <= n_tiles:
                            n = i - 1
                            j = n % NJ
                            pe.wait_ge(s["a_ex"], n + 1)
                            if n == 0:
                                pe.wait_ge(s["c_vb"], 4)
                            else:
                                pe.wait_ge(s["a_ptv"] if n % 2 else s["a_pta"], (n + 1) // 2)
                            for jj in range(j + 1):
                                last = tr(M[2][:, jj * P:(jj + 1) * P], pb[:, n % 2, jj * P:(jj + 1) * P], ident)
                            last.then_inc(s["a_tp"], 1)
                        if i >= 2:
                            n = i - 2
                            h, j = divmod(n, NJ)
                            if n == 0:
                                pe.wait_ge(s["a_vre"], 16 * TR)
                                pe.wait_ge(s["c_kb1"], 2)
                            if n == 32:
                                pe.wait_ge(s["a_on"], 1)
                            pe.wait_ge(s["a_ptv"] if n % 2 == 0 else s["a_pta"], n // 2 + 1)
                            for jj in range(j + 1):
                                last = mm(M[3][:, (n % 32) * DH:(n % 32 + 1) * DH],
                                          ptb[:, n % 2, jj * P:(jj + 1) * P], vpos[:, NJ * h + jj, :],
                                          start=(jj == 0), stop=(jj == j))
                            last.then_inc(s["a_pv"], 1)
                        if i % 2:
                            fill(1)
                    fill(3)
                    pe.wait_ge(s["a_ot"], 16)
                    project(0, w("a_o"), NT)
                    fill(3)

                    def cross(n, tiles, u0, t0, extra):
                        for u in range(2 * tiles + 2):
                            if u < 2 * tiles:
                                t, g = divmod(u, 2)
                                if u >= 2:
                                    pe.wait_ge(s["x_sm"], u0 + u - 1)
                                mm(M[u % 2][:, :], qT[:, g, t * P:(t + 1) * P], kb[n][:, g, :, :],
                                   start=True, stop=True).then_inc(s["x_s"], 1)
                            if 1 <= u <= 2 * tiles:
                                v_ = u - 1
                                pe.wait_ge(s["x_ex"], u0 + v_ + 1)
                                if u0 + v_:
                                    pe.wait_ge(s["x_pt"], u0 + v_)
                                for pr in range(4):
                                    last = tr(M[2][:, pr * P:(pr + 1) * P], pb[:, v_ % 2, pr * P:(pr + 1) * P], ident)
                                last.then_inc(s["x_tp"], 1)
                            if u >= 2:
                                v_ = u - 2
                                t, g = divmod(v_, 2)
                                pe.wait_ge(s["x_pt"], u0 + v_ + 1)
                                if g == 0 and t >= 1:
                                    pe.wait_ge(s["x_on"], t0 + t)
                                for pr in range(4):
                                    at = (4 * g + pr) * 2 * DH
                                    last = mm(M[3][:, at:at + 2 * DH], ptb[:, v_ % 2, pr * P:(pr + 1) * P],
                                              vb[n][:, 4 * g + pr, :, :], start=True, stop=True)
                                last.then_inc(s["x_pv"], 1)
                            if u < 2 * tiles:
                                fill(extra + 1 - u % 2)
                        pe.wait_ge(s["x_on"], t0 + tiles)

                    turn_x(1, X)
                    for blk in range(KC):
                        feature_major(M[blk][:, :], w("x0_q"), blk * P, XT).then_inc(s["x_q"], 1)
                    pe.wait_ge(s["x_qt"], 2)
                    cross(0, NT, 0, 0, 1)
                    project(1, w("x0_o"), NT)
                    fill(3)

                    def route(name, xt):
                        for t in range(NT):
                            for k in range(KC):
                                last = mm(M[0][:, t * NE:(t + 1) * NE], xt[:, k, t * P:(t + 1) * P],
                                          w(name)[:, k, :], start=(k == 0), stop=(k == KC - 1))
                        last.then_inc(s["g_lg"], 1)

                    turn_x(2, X)
                    route("f0_r", XT)
                    for e in range(NE + 2):
                        if e <= NE:
                            if e == 0:
                                pe.wait_ge(s["g_ls"], 1)
                            if e >= 2:
                                pe.wait_ge(s["e_s"], e - 1)
                            feature_major(M[e % 2][:, :], w("f0_w1"), e * P, XT).then_inc(s["e_h"], 1)
                        if e >= 1:
                            n = e - 1
                            pe.wait_ge(s["e_s"], n + 1)
                            for t in range(NT):
                                if n >= 1 and t % 2 == 0:
                                    pe.wait_ge(s["e_ev"], 2 * (n - 1) + t // 2 + 1)
                                last = mm(M[2 + t // 2][:, (t % 2) * D:(t % 2 + 1) * D], hs[:, n % 2, t * P:(t + 1) * P],
                                          f0_w2[:, n, :], start=True, stop=True)
                                if t % 2:
                                    last.then_inc(s["e_y"], 1)
                        if e % 2 and e <= NE:
                            fill(1)
                    pe.wait_ge(s["g_cmb"], 1)
                    for t in range(NT):
                        last = tr(M[1][0:NE, t * P:(t + 1) * P], cmb[:, t, :], ident)
                    last.then_inc(s["e_tp"], 1)
                    pe.wait_ge(s["e_ct"], 1)
                    for t in range(NT):
                        if t % 2 == 0:
                            pe.wait_ge(s["e_ev"], 2 * NE + t // 2 + 1)
                        last = mm(M[2 + t // 2][:, (t % 2) * D:(t % 2 + 1) * D], cmbT[:, t * P:(t + 1) * P], b2[:],
                                  start=True, stop=True)
                        if t % 2:
                            last.then_inc(s["e_y"], 1)
                    fill(3)

                    turn_x(3, X)
                    for blk in range(KC):
                        feature_major(M[blk][:, :], w("d_q"), blk * P, XT).then_inc(s["d_qk"], 1)
                    for blk in range(KC):
                        feature_major(M[2 + blk][:, :], w("d_k"), blk * P, XT).then_inc(s["d_qk"], 1)
                    for t in range(NT):
                        if t % 2 == 0:
                            pe.wait_ge(s["x_qt"], 3 + t // 2)
                        last = token_major(M[t // 2][:, (t % 2) * D:(t % 2 + 1) * D], XT, t, w("d_v"))
                        if t % 2:
                            last.then_inc(s["d_v"], 1)
                    pe.wait_ge(s["d_ev"], 2)
                    for j in range(NT):
                        if j >= 2:
                            pe.wait_ge(s["d_ev"], j + 1)
                        for k in range(KC):
                            last = mm(M[(2 + j) % 4][:, :], kT[:, k, j * P:(j + 1) * P], qT[:, k, :],
                                      start=(k == 0), stop=(k == KC - 1))
                        last.then_inc(s["d_s"], 1)
                    fill(4)
                    pe.wait_ge(s["d_ex"], 2)
                    for j in range(NT):
                        pe.wait_ge(s["d_ex"], j + 1)
                        pe.wait_ge(s["d_vn"], j + 1)
                        for t in range(NT):
                            last = mm(M[2 + t // 2][:, (t % 2) * D:(t % 2 + 1) * D], ex[:, j, t * P:(t + 1) * P],
                                      vtok[:, j, :], start=(j == 0 and t % 2 == 0), stop=(j == NT - 1),
                                      skip_group_check=True)
                            if j == NT - 1 and t % 2:
                                last.then_inc(s["r_done"], 1)
                    fill(3)

                    turn_x(4, X)
                    for n, name in enumerate(("x1_q", "x1_qs")):
                        for blk in range(KC):
                            for k in range(KC):
                                last = mm(M[0][:, (2 * n + blk) * P:(2 * n + blk + 1) * P],
                                          w(name)[:, k, blk * P:(blk + 1) * P], XT[:, k, 0:P],
                                          start=(k == 0), stop=(k == KC - 1))
                    last.then_inc(s["x_q"], 1)
                    fill(SLOTS)
                    pe.wait_ge(s["x_qt"], 6)
                    cross(1, 1, 2 * NT, NT, 0)
                    project(2, w("x1_o"), 1)
                    turn_x(5, XF)
                    route("f1_r", XTF)

                @block.scalar
                def _(act):
                    A = nc.scalar.activation

                    def slot(k):
                        if 1 <= k <= FS:
                            j = k - 1
                            act.wait_ge(s["f_h"], j + 1)
                            if j >= 2:
                                act.wait_ge(s["f_m"], j - 1)
                            A(hsF[:, j % 2, :], FH[j % 2][:, 0:HALF], ACT.Silu).then_inc(s["f_s"], 1)

                    fill = slots(slot)
                    if front is None:
                        fill(SLOTS)
                        return

                    def xt_copy(st, dst):
                        act.wait_ge(s["xt_ps"], st + 1)
                        A(dst[:, 0, :], M[2][:, :], ACT.Copy).then_inc(s["xt_a"], 1)

                    def ot_copy(n, tiles):
                        act.wait_ge(s["o_tp"], n + 1)
                        A(OT[:, 0, 0:tiles * P], M[2][:, 0:tiles * P], ACT.Copy).then_inc(s["o_ta"], 1)

                    xt_copy(0, XT)
                    for blk in range(4):
                        act.wait_ge(s["a_qk"], blk + 1)
                        A(qkf[:, blk, :], M[blk][:, :], ACT.Identity, bias=col("a_qk")[:, blk:blk + 1],
                          scale=SCALE_A if blk < 2 else 1.0).then_inc(s["a_qkf"], 1)
                    for blk in range(4):
                        act.wait_ge(s["a_qkf"], blk + 1)
                        A(parts[:, 0, blk, :], qkf[:, blk, :], ACT.Copy).then_inc(s["a_hi"], 1)
                    for blk in range(4):
                        act.wait_ge(s["a_r1"], blk + 1)
                        A(parts[:, 1, blk, :], qkf[:, blk, :], ACT.Copy).then_inc(s["a_mid"], 1)
                    fill(6)

                    n_tiles = H * NJ
                    for i in range(n_tiles + 2):
                        if i < n_tiles:
                            j = i % NJ
                            act.wait_ge(s["a_mx"], i + 1)
                            if i >= 2:
                                act.wait_ge(s["a_tp"], i - 1)
                            A(pb[:, i % 2, 0:P * (j + 1)], M[i % 2][:, 0:P * (j + 1)], ACT.Exp,
                              bias=nmax[:, i:i + 1], accum_out=rsum[:, i:i + 1]).then_inc(s["a_ex"], 1)
                        if 1 <= i <= n_tiles and (i - 1) % 2 == 1:
                            n = i - 1
                            j = n % NJ
                            act.wait_ge(s["a_tp"], n + 1)
                            if n >= 2:
                                act.wait_ge(s["a_pv"], n - 1)
                            A(ptb[:, 1, 0:P * (j + 1)], M[2][:, 0:P * (j + 1)], ACT.Copy).then_inc(s["a_pta"], 1)
                        if i % 2:
                            fill(1)
                    fill(3)
                    ot_copy(0, NT)
                    fill(3)

                    def cross(tiles, u0, extra):
                        for u in range(2 * tiles + 1):
                            if u < 2 * tiles:
                                act.wait_ge(s["x_sub"], u0 + u + 1)
                                if u >= 2:
                                    act.wait_ge(s["x_tp"], u0 + u - 1)
                                    act.wait_ge(s["x_rs"], u0 + u - 1)
                                A(pb[:, u % 2, :], sc[:, u % 2, :, :].rearrange("p a b -> p (a b)"), ACT.Exp)\
                                    .then_inc(s["x_ex"], 1)
                            if u >= 1:
                                v_ = u - 1
                                act.wait_ge(s["x_tp"], u0 + v_ + 1)
                                if v_ >= 2:
                                    act.wait_ge(s["x_pv"], u0 + v_ - 1)
                                A(ptb[:, v_ % 2, :], M[2][:, :], ACT.Copy).then_inc(s["x_pt"], 1)
                            if u < 2 * tiles:
                                fill(extra + 1 - u % 2)

                    xt_copy(1, XT)
                    for blk in range(KC):
                        act.wait_ge(s["x_q"], blk + 1)
                        A(qT[:, blk, :], M[blk][:, :], ACT.Identity, bias=col("x0_q")[:, blk:blk + 1],
                          scale=SCALE_X).then_inc(s["x_qt"], 1)
                    cross(NT, 0, 1)
                    ot_copy(1, NT)
                    fill(3)

                    xt_copy(2, XT)
                    for e in range(NE + 1):
                        if e == 1:
                            act.wait_ge(s["g_a"], 1)
                            A(ga[:, 1], ga[:, 0], ACT.Exp).then_inc(s["g_e"], 1)
                            act.wait_ge(s["g_b"], 1)
                            A(ga[:, 4], ga[:, 2], ACT.Ln).then_inc(s["g_l"], 1)
                        act.wait_ge(s["e_h"], e + 1)
                        if e >= 2:
                            act.wait_ge(s["e_y"], 2 * (e - 1))
                        A(hs[:, e % 2, :], M[e % 2][:, :], ACT.Silu, bias=col("f0_b1")[:, e:e + 1])\
                            .then_inc(s["e_s"], 1)
                        if e % 2:
                            fill(1)
                    fill(3)

                    xt_copy(3, XT)
                    for blk in range(KC):
                        act.wait_ge(s["d_qk"], blk + 1)
                        A(qT[:, blk, :], M[blk][:, :], ACT.Identity, bias=col("d_q")[:, blk:blk + 1],
                          scale=1.0 / D).then_inc(s["x_qt"], 1)
                    for j in range(NT):
                        act.wait_ge(s["d_mx"], j + 1)
                        A(ex[:, j, :], M[(2 + j) % 4][:, :], ACT.Exp, bias=nmax[:, j:j + 1],
                          accum_out=rsum[:, j:j + 1]).then_inc(s["d_ex"], 1)
                    fill(4)
                    fill(3)

                    xt_copy(4, XT)
                    fill(SLOTS)
                    cross(1, 2 * NT, 0)
                    ot_copy(2, 1)
                    xt_copy(5, XTF)
                    act.wait_ge(s["g_a"], 2)
                    A(ga[:, 1, :, 0:1], ga[:, 0, :, 0:1], ACT.Exp).then_inc(s["g_e"], 1)

                @block.gpsimd
                def _(pool):
                    expo = const("expo")

                    def rsqrt(n, want, count, eps_done, rs_done, turn):
                        pool.wait_ge(s[want], count)
                        pool.tensor_scalar(veps[:, n], mv[:, n, :, 1], EPS, None, ALU.add).then_inc(s[eps_done], 1)
                        pool.wait_ge(s[eps_done], turn)
                        pool.tensor_tensor(rstd[:, n], veps[:, n], expo[:, 0:NT], ALU.pow).then_inc(s[rs_done], 1)

                    def slot(k):
                        if k == SLOTS - 2:
                            rsqrt(1, "f_ag", NT, "f_ep", "f_rs", 1)

                    fill = slots(slot)
                    pool.wait_ge(w_in[0], 64)
                    if front is None:
                        fill(SLOTS)
                        return

                    def add_bias(st, name):
                        pool.wait_ge(s["xt_ps"], st + 1)
                        pool.tensor_tensor(X[:], X[:], row(name).unsqueeze(1).to_broadcast([P, NT, D]), ALU.add)\
                            .then_inc(s["x_bias"], 1)

                    def main_rsqrt(st):
                        rsqrt(0, "ln_ag", NT * (st + 1), "ln_ep", "ln_rs", st + 1)

                    add_bias(0, "a_o")
                    fill(6 + 33 + 3)
                    main_rsqrt(0)
                    fill(3)
                    add_bias(1, "x0_o")
                    fill(3 * NT)
                    main_rsqrt(1)
                    fill(3)
                    add_bias(2, "f0_o")
                    pool.wait_ge(s["g_c"], 1)
                    pool.tensor_tensor(ga[:, 6], ga[:, 5], expo[:, 4:5].unsqueeze(1).to_broadcast([P, NT, NE]),
                                       ALU.pow).then_inc(s["g_p"], 1)
                    fill(4)
                    main_rsqrt(2)
                    fill(3)
                    fill(4)
                    main_rsqrt(3)
                    fill(3)
                    add_bias(4, "x1_o")
                    fill(SLOTS)
                    main_rsqrt(4)

                @block.vector
                def _(v):
                    V = nc.vector

                    def evacuate(e, half):
                        v.wait_ge(s["f_y"], 2 * (HB1 * e + HB1 - 1) + half + 1)
                        if e >= 1:
                            v.wait_ge(s["f_ev"], 2 * (e - 1) + half + 1)
                        if e == 0:
                            last = V.tensor_tensor(XF[:, 2 * half:2 * half + 2, :],
                                                   FY[half][:, :].rearrange("p (t d) -> p t d", t=2),
                                                   XF[:, 2 * half:2 * half + 2, :], ALU.add)
                        else:
                            for t in (2 * half, 2 * half + 1):
                                last = V.scalar_tensor_tensor(XF[:, t, :], FY[half][:, (t % 2) * D:(t % 2 + 1) * D],
                                                              cmbF[:, t, e - 1:e], XF[:, t, :], ALU.mult, ALU.add)
                        last.then_inc(s["f_ev"], 1)

                    def statistics(n, src, ready, count, st_done, ag_done, base):
                        v.wait_ge(s[ready], count)
                        for t in range(NT):
                            V.bn_stats(stats[:, n, t, :], src[:, t, :]).then_inc(s[st_done], 1)
                        for t in range(NT):
                            v.wait_ge(s[st_done], base + t + 1)
                            V.bn_aggr(mv[:, n, t, :], stats[:, n, t, :]).then_inc(s[ag_done], 1)

                    def normalise(n, src, dst, rs_done, count, done):
                        v.wait_ge(s[rs_done], count)
                        for t in range(NT):
                            V.tensor_scalar(dst[:, t, :], src[:, t, :], mv[:, n, t, 0:1], rstd[:, n, t:t + 1],
                                            ALU.subtract, ALU.mult).then_inc(s[done], 1)

                    def slot(k):
                        if 1 <= k <= FS:
                            j = k - 1
                            v.wait_ge(s["f_s"], j + 1)
                            if j >= 2:
                                v.wait_ge(s["f_y"], j - 1)
                            V.tensor_tensor(hmF[:, j % 2, :], FH[j % 2][:, HALF:S], hsF[:, j % 2, :], ALU.mult)\
                                .then_inc(s["f_m"], 1)
                        per = 2 * HB1
                        if k > per and (k - per - 1) % per == 0:
                            evacuate((k - per - 1) // per, 0)
                        if k > per + 1 and (k - per - 2) % per == 0:
                            evacuate((k - per - 2) // per, 1)
                        if k == SLOTS - 3:
                            statistics(1, XF, "f_ev", 2 * (NE + 1), "f_st", "f_ag", 0)
                        if k == SLOTS - 2:
                            normalise(1, XF, XF, "f_rs", 1, "f_ln")

                    fill = slots(slot)
                    if front is None:
                        fill(SLOTS)
                        return

                    def xt_copy(st, dst):
                        v.wait_ge(s["xt_ps"], st + 1)
                        V.tensor_copy(dst[:, 1, :], M[3][:, :]).then_inc(s["xt_v"], 1)

                    def ot_copy(n, tiles):
                        v.wait_ge(s["o_tp"], n + 1)
                        V.tensor_copy(OT[:, 1, 0:tiles * P], M[3][:, 0:tiles * P]).then_inc(s["o_tv"], 1)

                    def add_result(banks, r0, sums):
                        for g, b in enumerate(banks):
                            v.wait_ge(s["r_done"], r0 + g + 1)
                            n = 2 if len(banks) == 2 else 1
                            V.tensor_tensor(X[:, 2 * g:2 * g + n, :],
                                            M[b][:, 0:n * D].rearrange("p (t d) -> p t d", t=n),
                                            X[:, 2 * g:2 * g + n, :], ALU.add).then_inc(s["ln_sum"], 1)

                    def layernorm(st, ready, count, dst):
                        statistics(0, X, ready, count, "ln_st", "ln_ag", NT * st)
                        if st < 4:
                            fill(2)
                        normalise(0, X, dst, "ln_rs", st + 1, "ln_done")
                        if st < 4:
                            fill(1)

                    v.wait_ge(s["pen_in"], 16)
                    V.tensor_scalar(pen[:], mask8[:], GONE, 10.0, ALU.mult, ALU.mult).then_inc(s["pen"], 1)
                    xt_copy(0, XT)
                    for blk in range(4):
                        v.wait_ge(s["a_hi"], blk + 1)
                        V.tensor_tensor(qkf[:, blk, :], qkf[:, blk, :], parts[:, 0, blk, :], ALU.subtract)\
                            .then_inc(s["a_r1"], 1)
                    for g in range(2):
                        v.wait_ge(s["a_v"], g + 1)
                        V.tensor_tensor(vtok[:, 2 * g:2 * g + 2, :],
                                        M[g][:, :].rearrange("p (t d) -> p t d", t=2),
                                        row("a_v").unsqueeze(1).to_broadcast([P, 2, D]), ALU.add)\
                            .then_inc(s["a_vt"], 1)
                    for blk in range(4):
                        v.wait_ge(s["a_mid"], blk + 1)
                        V.tensor_tensor(parts[:, 2, blk, :], qkf[:, blk, :], parts[:, 1, blk, :], ALU.subtract)\
                            .then_inc(s["a_lo"], 1)

                    v.wait_ge(s["c_tp"], 1)
                    V.tensor_copy(cT[:], M[2][:, 0:KC * SK].rearrange("p (k n) -> p k n", k=KC)
                                  .unsqueeze(2).to_broadcast([P, KC, 2, SK])).then_inc(s["c_ct"], 1)
                    v.wait_ge(s["c_k"], 1)
                    blkmask = const("blk").unsqueeze(2).to_broadcast([P, 8, SK])

                    def kbank(n, blk):
                        return M[3][:, (2 * n + blk) * SK:(2 * n + blk + 1) * SK]

                    for blk in range(KC):
                        V.scalar_tensor_tensor(kb[0][:, blk], kbank(0, blk).unsqueeze(1).to_broadcast([P, 8, SK]),
                                               col("x0_k")[:, blk:blk + 1], blkmask, ALU.add, ALU.mult)\
                            .then_inc(s["c_kb0"], 1)
                    rk = const("ropek")
                    for blk in range(KC):
                        V.scalar_tensor_tensor(kr[:, 0, blk], kbank(1, blk), col("x1_k")[:, blk:blk + 1], rk[:, 0:SK],
                                               ALU.add, ALU.mult).then_inc(s["c_ka"], 1)
                        V.scalar_tensor_tensor(kr[:, 1, blk], kbank(2, blk), col("x1_ks")[:, blk:blk + 1],
                                               rk[:, SK:2 * SK], ALU.add, ALU.mult).then_inc(s["c_ka"], 1)
                    v.wait_ge(s["c_ka"], 4)
                    V.tensor_tensor(kr[:, 2], kr[:, 0], kr[:, 1], ALU.add).then_inc(s["c_kc"], 1)
                    v.wait_ge(s["c_kc"], 1)
                    for blk in range(KC):
                        V.tensor_tensor(kb[1][:, blk], kr[:, 2, blk].unsqueeze(1).to_broadcast([P, 8, SK]), blkmask,
                                        ALU.mult).then_inc(s["c_kb1"], 1)
                    v.wait_ge(s["c_v"], 1)
                    for n in range(2):
                        for half in range(2):
                            rows_ = slice(SK * half, SK * half + SK)
                            src = M[2][rows_, n * D:(n + 1) * D].rearrange("p (a b e) -> p a b e", b=2, e=DH)
                            bias = row(f"x{n}_v")[rows_].rearrange("p (a b e) -> p a b e", b=2, e=DH)
                            V.tensor_tensor(vb[n][rows_, :, half, :], src[:, :, half, :], bias[:, :, half, :], ALU.add)\
                                .then_inc(s["c_vb"], 1)
                    fill(6)

                    v.wait_ge(s["a_q6"], 16 * 2 * NTERM)
                    for g in range(4):
                        V.tensor_copy(qpos[0:ROWS6, H * g:H * g + H],
                                      q6[0:ROWS6, :, P * g:P * g + P].rearrange("p c (g r) -> p g c r", r=TR))\
                            .then_inc(s["a_qr"], 1)

                    def heads_out(g):
                        v.wait_ge(s["a_ex"], 32 * (g + 1))
                        V.reciprocal(rinv[:, 32 * g:32 * g + 32], rsum[:, 32 * g:32 * g + 32]).then_inc(s["a_ri"], 1)
                        v.wait_ge(s["a_ri"], g + 1)
                        v.wait_ge(s["a_pv"], 32 * (g + 1))
                        V.tensor_tensor(opos[:, 32 * g:32 * g + 32, :], M[3][:, :].rearrange("p (n e) -> p n e", e=DH),
                                        rinv[:, 32 * g:32 * g + 32].unsqueeze(2).to_broadcast([P, 32, DH]), ALU.mult)\
                            .then_inc(s["a_on"], 1)

                    n_tiles = H * NJ
                    for i in range(n_tiles + 2):
                        if i < n_tiles:
                            j = i % NJ
                            v.wait_ge(s["a_s"], i + 1)
                            V.tensor_reduce(nmax[:, i:i + 1], M[i % 2][:, 0:P * (j + 1)], AX.X, ALU.max,
                                            negate=True).then_inc(s["a_mx"], 1)
                        if 1 <= i <= n_tiles and (i - 1) % 2 == 0:
                            n = i - 1
                            j = n % NJ
                            v.wait_ge(s["a_tp"], n + 1)
                            if n >= 2:
                                v.wait_ge(s["a_pv"], n - 1)
                            V.tensor_copy(ptb[:, 0, 0:P * (j + 1)], M[2][:, 0:P * (j + 1)]).then_inc(s["a_ptv"], 1)
                        if i in (33, 65):
                            heads_out(i // 64)
                        if i % 2:
                            fill(1)
                    fill(3)
                    ot_copy(0, NT)
                    v.wait_ge(s["x_bias"], 1)
                    add_result((0, 1), 0, 0)
                    layernorm(0, "ln_sum", 2, X)

                    def cross(n, tiles, u0, t0, penalty, extra):
                        for u in range(2 * tiles + 2):
                            if u < 2 * tiles:
                                t, g = divmod(u, 2)
                                cur = sc[:, u % 2]
                                mx = nmax[:, 8 * (u % 2):8 * (u % 2) + 8]
                                v.wait_ge(s["x_s"], u0 + u + 1)
                                if u >= 2:
                                    v.wait_ge(s["x_ex"], u0 + u - 1)
                                V.tensor_tensor(cur, M[u % 2][:, :].rearrange("p (h k) -> p h k", k=SK),
                                                penalty(t).unsqueeze(1).to_broadcast([P, 8, SK]), ALU.add)\
                                    .then_inc(s["x_sm"], 1)
                                v.wait_ge(s["x_sm"], u0 + u + 1)
                                V.tensor_reduce(mx, cur, AX.X, ALU.max).then_inc(s["x_mx"], 1)
                                v.wait_ge(s["x_mx"], u0 + u + 1)
                                V.tensor_tensor(cur, cur, mx.unsqueeze(2).to_broadcast([P, 8, SK]), ALU.subtract)\
                                    .then_inc(s["x_sub"], 1)
                            if 1 <= u <= 2 * tiles:
                                v_ = u - 1
                                v.wait_ge(s["x_ex"], u0 + v_ + 1)
                                V.tensor_reduce(rsum[:, 8 * v_:8 * v_ + 8],
                                                pb[:, v_ % 2, :].rearrange("p (h k) -> p h k", k=SK),
                                                AX.X, ALU.add).then_inc(s["x_rs"], 1)
                            if u >= 2 and u % 2 == 1:
                                t = (u - 2) // 2
                                v.wait_ge(s["x_rs"], u0 + 2 * t + 2)
                                V.reciprocal(rinv[:, H * t:H * t + H], rsum[:, H * t:H * t + H]).then_inc(s["x_ri"], 1)
                                v.wait_ge(s["x_ri"], t0 + t + 1)
                                v.wait_ge(s["x_pv"], u0 + 2 * t + 2)
                                V.tensor_tensor(otok[:, t, :].rearrange("p (h e) -> p h e", e=DH),
                                                M[3][:, 0:D].rearrange("p (h e) -> p h e", e=DH),
                                                rinv[:, H * t:H * t + H].unsqueeze(2).to_broadcast([P, H, DH]), ALU.mult)\
                                    .then_inc(s["x_on"], 1)
                            if u < 2 * tiles:
                                fill(extra + 1 - u % 2)

                    xt_copy(1, XT)
                    v.wait_ge(s["pen"], 1)
                    cross(0, NT, 0, 0, lambda t: pen[:, t, :], 1)
                    ot_copy(1, NT)
                    v.wait_ge(s["x_bias"], 2)
                    add_result((0, 1), 2, 2)
                    layernorm(1, "ln_sum", 4, X)

                    def pick(n):
                        for t in range(NT):
                            V.max(top[:, t, :], lg[:, t, :]).then_inc(s["g_mx"], 1)
                        for t in range(NT):
                            v.wait_ge(s["g_mx"], NT * n + t + 1)
                            V.max_index(ix[:, t, :], top[:, t, :], lg[:, t, :]).then_inc(s["g_ix"], 1)
                        v.wait_ge(s["g_ix"], NT * (n + 1))
                        V.tensor_copy(ixf[:], ix[:]).then_inc(s["g_if"], 1)
                        v.wait_ge(s["g_if"], n + 1)
                        for k in range(2):
                            V.tensor_tensor(oh[:, k], ixf[:, :, k:k + 1].to_broadcast([P, NT, NE]),
                                            const("iota").unsqueeze(1).to_broadcast([P, NT, NE]), ALU.is_equal)\
                                .then_inc(s["g_oh"], 1)
                        v.wait_ge(s["g_oh"], 2 * n + 2)

                    xt_copy(2, XT)
                    v.wait_ge(s["g_lg"], 1)
                    V.tensor_tensor(lg[:], M[0][:, 0:NT * NE].rearrange("p (t e) -> p t e", e=NE),
                                    row("f0_r").unsqueeze(1).to_broadcast([P, NT, NE]), ALU.add).then_inc(s["g_ls"], 1)
                    v.wait_ge(s["g_ls"], 1)
                    V.scalar_tensor_tensor(ga[:, 0], lg[:], -1.0, lg[:], ALU.mult, ALU.min).then_inc(s["g_a"], 1)
                    pick(0)

                    def leave(n):
                        for half in range(2):
                            v.wait_ge(s["e_y"], 2 * n + half + 1)
                            if n >= 1:
                                v.wait_ge(s["e_ev"], 2 * (n - 1) + half + 1)
                            if n in (0, NE + 1):
                                last = V.tensor_tensor(X[:, 2 * half:2 * half + 2, :],
                                                       M[2 + half][:, :].rearrange("p (t d) -> p t d", t=2),
                                                       X[:, 2 * half:2 * half + 2, :], ALU.add)
                            else:
                                for t in (2 * half, 2 * half + 1):
                                    last = V.scalar_tensor_tensor(
                                        X[:, t, :], M[2 + half][:, (t % 2) * D:(t % 2 + 1) * D],
                                        cmb[:, t, n - 1:n], X[:, t, :], ALU.mult, ALU.add)
                            last.then_inc(s["e_ev"], 1)

                    for e in range(1, NE + 2):
                        if e == 1:
                            v.wait_ge(s["x_bias"], 3)
                            leave(0)
                            v.wait_ge(s["g_e"], 1)
                            V.tensor_scalar(ga[:, 2], ga[:, 1], 1.0, None, ALU.add).then_inc(s["g_b"], 1)
                            v.wait_ge(s["g_b"], 1)
                            V.tensor_scalar(ga[:, 3], ga[:, 2], -1.0, None, ALU.add).then_inc(s["g_b"], 1)
                            v.wait_ge(s["g_b"], 2)
                            V.tensor_scalar(ga[:, 5], ga[:, 3], 0.0, None, ALU.is_equal).then_inc(s["g_b"], 1)
                            V.tensor_scalar(ga[:, 6], ga[:, 3], 1e-30, None, ALU.max).then_inc(s["g_b"], 1)
                            v.wait_ge(s["g_b"], 4)
                            V.reciprocal(ga[:, 3], ga[:, 6]).then_inc(s["g_b"], 1)
                            V.tensor_tensor(ga[:, 7], ga[:, 5], ga[:, 1], ALU.mult).then_inc(s["g_b"], 1)
                            v.wait_ge(s["g_b"], 6)
                            V.tensor_tensor(ga[:, 5], ga[:, 3], ga[:, 1], ALU.mult).then_inc(s["g_b"], 1)
                            v.wait_ge(s["g_b"], 7)
                            v.wait_ge(s["g_l"], 1)
                            V.tensor_tensor(ga[:, 3], ga[:, 5], ga[:, 4], ALU.mult).then_inc(s["g_b"], 1)
                            v.wait_ge(s["g_b"], 8)
                            V.tensor_tensor(ga[:, 6], ga[:, 3], ga[:, 7], ALU.add).then_inc(s["g_b"], 1)
                            v.wait_ge(s["g_b"], 9)
                            V.scalar_tensor_tensor(ga[:, 5], lg[:], 0.0, ga[:, 6], ALU.max, ALU.add)\
                                .then_inc(s["g_c"], 1)
                            V.tensor_tensor(ga[:, 3], oh[:, 0], oh[:, 1], ALU.add).then_inc(s["g_sum"], 1)
                            v.wait_ge(s["g_sum"], 1)
                            v.wait_ge(s["g_p"], 1)
                            V.tensor_tensor(cmb[:], ga[:, 6], ga[:, 3], ALU.mult).then_inc(s["g_cmb"], 1)
                            v.wait_ge(s["g_cmb"], 1)
                        else:
                            leave(e - 1)
                        if e % 2 and e <= NE:
                            fill(1)
                    v.wait_ge(s["e_tp"], 1)
                    V.tensor_copy(cmbT[:], M[1][0:NE, :]).then_inc(s["e_ct"], 1)
                    leave(NE + 1)
                    layernorm(2, "e_ev", 2 * (NE + 2), X)

                    xt_copy(3, XT)
                    for blk in range(KC):
                        v.wait_ge(s["d_qk"], 3 + blk)
                        V.tensor_scalar(kT[:, blk, :], M[2 + blk][:, :], col("d_k")[:, blk:blk + 1], None, ALU.add)\
                            .then_inc(s["d_ev"], 1)
                    for g in range(2):
                        v.wait_ge(s["d_v"], g + 1)
                        V.tensor_tensor(vtok[:, 2 * g:2 * g + 2, :],
                                        M[g][:, :].rearrange("p (t d) -> p t d", t=2),
                                        row("d_v").unsqueeze(1).to_broadcast([P, 2, D]), ALU.add)\
                            .then_inc(s["d_ev"], 1)
                    for j in range(NT):
                        v.wait_ge(s["d_s"], j + 1)
                        V.tensor_reduce(nmax[:, j:j + 1], M[(2 + j) % 4][:, :], AX.X, ALU.max, negate=True)\
                            .then_inc(s["d_mx"], 1)
                    v.wait_ge(s["d_ev"], 4)
                    for j in range(NT):
                        v.wait_ge(s["d_ex"], j + 1)
                        V.reciprocal(rinv[:, j:j + 1], rsum[:, j:j + 1]).then_inc(s["d_rz"], 1)
                        v.wait_ge(s["d_rz"], j + 1)
                        V.tensor_scalar(vtok[:, j, :], vtok[:, j, :], rinv[:, j:j + 1], None, ALU.mult)\
                            .then_inc(s["d_vn"], 1)
                    fill(4)
                    v.wait_ge(s["xt_ps"], 4)
                    add_result((2, 3), 4, 4)
                    layernorm(3, "ln_sum", 6, X)

                    xt_copy(4, XT)
                    v.wait_ge(s["x_q"], 3)
                    rq = const("ropeq")
                    for n, name in enumerate(("x1_q", "x1_qs")):
                        for blk in range(KC):
                            V.scalar_tensor_tensor(hs[:, n, blk * P:(blk + 1) * P],
                                                   M[0][:, (2 * n + blk) * P:(2 * n + blk + 1) * P],
                                                   col(name)[:, blk:blk + 1], rq[:, n * P:(n + 1) * P],
                                                   ALU.add, ALU.mult).then_inc(s["x_qa"], 1)
                    v.wait_ge(s["x_qa"], 4)
                    for blk in range(KC):
                        V.tensor_tensor(qT[:, blk, 0:P], hs[:, 0, blk * P:(blk + 1) * P], hs[:, 1, blk * P:(blk + 1) * P],
                                        ALU.add).then_inc(s["x_qt"], 1)
                    fill(SLOTS)
                    cross(1, 1, 2 * NT, NT, lambda t: const("window"), 0)
                    ot_copy(2, 1)
                    v.wait_ge(s["x_bias"], 4)
                    add_result((0,), 6, 6)
                    if back is not None:
                        v.wait_ge(s["f_out"], 16)
                    layernorm(4, "ln_sum", 7, XF)
                    xt_copy(5, XTF)
                    v.wait_ge(s["g_lg"], 2)
                    V.tensor_copy(lg[:], M[0][:, 0:NT * NE].rearrange("p (t e) -> p t e", e=NE))\
                        .then_inc(s["g_ls"], 1)
                    v.wait_ge(s["g_ls"], 2)
                    pick(1)
                    V.tensor_tensor(ga[:, 0, :, 0:1], top[:, :, 1:2], top[:, :, 0:1], ALU.subtract)\
                        .then_inc(s["g_a"], 1)
                    v.wait_ge(s["g_e"], 2)
                    V.tensor_scalar(ga[:, 2, :, 0:1], ga[:, 1, :, 0:1], 1.0, None, ALU.add).then_inc(s["g_b"], 1)
                    v.wait_ge(s["g_b"], 10)
                    V.reciprocal(ga[:, 3, :, 0:1], ga[:, 2, :, 0:1]).then_inc(s["g_b"], 1)
                    v.wait_ge(s["g_b"], 11)
                    V.tensor_tensor(ga[:, 4, :, 0:1], ga[:, 3, :, 0:1], ga[:, 1, :, 0:1], ALU.mult)\
                        .then_inc(s["g_b"], 1)
                    V.tensor_tensor(ga[:, 5], oh[:, 0], ga[:, 3, :, 0:1].to_broadcast([P, NT, NE]), ALU.mult)\
                        .then_inc(s["g_b"], 1)
                    v.wait_ge(s["g_b"], 13)
                    V.tensor_tensor(ga[:, 6], oh[:, 1], ga[:, 4, :, 0:1].to_broadcast([P, NT, NE]), ALU.mult)\
                        .then_inc(s["g_b"], 1)
                    v.wait_ge(s["g_b"], 14)
                    V.tensor_tensor(cmbF[:], ga[:, 5], ga[:, 6], ALU.add).then_inc(s["g_cmb"], 1)

            nc.all_engine_barrier()
            engines = (nc.gpsimd, nc.sync, nc.scalar, nc.vector, nc.tensor)
            for n, each in enumerate(s.values()):
                engines[n % 5].sem_clear(each)
            nc.all_engine_barrier()

        step(0, None)
        with nc.Fori(0, B - 1) as bi:
            step(bi + 1, bi)
        step(None, B - 1)


def kernel(**inputs):
    import numpy as np
    import concourse.bacc as bacc
    from concourse.bass_utils import run_bass_kernel_spmd

    g = {k: np.asarray(v) for k, v in inputs.items()}

    def chunks(a):
        return np.ascontiguousarray(a.reshape(-1, P, a.shape[1]).transpose(1, 0, 2)).reshape(P, -1)

    e = np.arange(DH)
    third = [(np.arange(H)[:, None] * 3 * DH + n * DH + e[None, :]).ravel() for n in range(3)]
    f = np.arange(D)
    swap = (f // DH) * DH + (f % DH + DH // 2) % DH
    wqkv, bqkv = g["L0_attn_W_qkv"], g["L0_attn_b_qkv"]
    w1 = np.concatenate([g["L0_ffn_sW1"][None], g["L0_ffn_rW1"]])
    w2 = np.concatenate([g["L0_ffn_sW2"][None], g["L0_ffn_rW2"]])
    W1 = g["L1_attn_W"]
    mats = {"a_qk": np.concatenate([wqkv[:, third[0]], wqkv[:, third[1]]], 1), "a_v": wqkv[:, third[2]],
            "a_o": g["L0_attn_W_out"],
            "x0_q": g["L0_xattn_Wq"].T, "x0_k": g["L0_xattn_Wk"].T, "x0_v": g["L0_xattn_Wv"].T,
            "x0_o": g["L0_xattn_Wo"].T, "f0_r": g["L0_ffn_routing_W"].T,
            "f0_w1": w1.transpose(1, 0, 2).reshape(D, -1),
            "d_q": W1[0:D].T, "d_k": W1[D:2 * D].T, "d_v": W1[2 * D:].T,
            "x1_q": g["L1_xattn_q_w"].T, "x1_qs": g["L1_xattn_q_w"][swap].T,
            "x1_k": g["L1_xattn_k_w"].T, "x1_ks": g["L1_xattn_k_w"][swap].T,
            "x1_v": g["L1_xattn_v_w"].T, "x1_o": g["L1_xattn_o_w"].T, "f1_r": g["L1_ffn_w_router"]}
    packed = {n: chunks(a) for n, a in mats.items()}
    packed["f0_w2"] = w2.transpose(1, 0, 2).reshape(P, -1)
    weights = np.concatenate([packed[n] for n in W_COLS], 1)
    b1 = g["L1_attn_b"]
    row_of = {"a_v": bqkv[third[2]], "a_o": g["L0_attn_b_out"], "x0_v": g["L0_xattn_bv"], "x0_o": g["L0_xattn_bo"],
              "f0_o": g["L0_ffn_sb2"], "d_v": b1[2 * D:], "x1_v": g["L1_xattn_v_b"], "x1_o": g["L1_xattn_o_b"],
              "f0_r": g["L0_ffn_expert_bias"]}
    rows = np.concatenate([row_of[n] for n in ROW_COLS])
    col_of = {"a_qk": np.concatenate([bqkv[third[0]], bqkv[third[1]]]), "x0_q": g["L0_xattn_bq"],
              "x0_k": g["L0_xattn_bk"], "d_q": b1[0:D], "d_k": b1[D:2 * D],
              "x1_q": g["L1_xattn_q_b"], "x1_qs": g["L1_xattn_q_b"][swap],
              "x1_k": g["L1_xattn_k_b"], "x1_ks": g["L1_xattn_k_b"][swap],
              "f0_b1": np.concatenate([g["L0_ffn_sb1"][None], g["L0_ffn_rb1"]]).ravel()}
    cols = np.concatenate([col_of[n].reshape(-1, P).T for n in COL_COLS], 1)
    experts = np.stack([np.concatenate([chunks(a[:, u:u + P]), chunks(b[:, u:u + P]), c[u:u + P]], 1)
                        for a, b, c in
                        [(g["L1_ffn_sw1"], g["L1_ffn_sw3"], g["L1_ffn_sw2"])] +
                        [(g["L1_ffn_w1"][i], g["L1_ffn_w3"][i], g["L1_ffn_w2"][i]) for i in range(NE)]
                        for u in range(0, HID1, P)])

    p = np.arange(P)
    pos = (p % TR) * H + p // TR
    half = DH // 2
    freqs = (1.0 / 10000.0 ** (np.arange(half, dtype=np.float32) / half)).astype(np.float32)
    ang = np.arange(P, dtype=np.float32)[None, :] * freqs[p % half][:, None]
    sign = np.where(p % DH < half, -1.0, 1.0)[:, None]
    cos, sin = np.cos(ang), np.sin(ang) * sign
    keys = np.arange(SK)[None, :]
    const_of = {"ident": np.eye(P), "causal": np.where(pos[None, :] <= pos[:, None], 0.0, -2.0 ** 100),
                "window": np.where((keys <= p[:, None]) & (keys >= p[:, None] - 64), 0.0, -2.0 ** 100),
                "blk": p[:, None] // DH == np.arange(8)[None, :],
                "ropeq": np.concatenate([cos, sin], 1) * SCALE_X,
                "ropek": np.concatenate([cos[:, 0:SK], sin[:, 0:SK]], 1),
                "iota": np.tile(np.arange(8), (P, 1)), "expo": np.tile([-0.5] * 4 + [0.5] * 4, (P, 1))}
    consts = np.concatenate([np.asarray(const_of[n], np.float32) for n in CONST_COLS], 1)

    arrays = {"x": g["x"], "ctx": g["ctx_1024"], "mask": g["mask_Bx1xSxS2_bf0"].reshape(B, S, SK),
              "weights": weights, "rows": rows, "cols": cols, "consts": consts, "b2": g["L0_ffn_rb2"],
              "experts": experts}
    nc = bacc.Bacc("TRN2", target_bir_lowering=False, num_devices=1)
    feed, args = {}, []
    for name, a in arrays.items():
        a = np.ascontiguousarray(a)
        feed[f"in_{name}"] = a
        args.append(nc.dram_tensor(f"in_{name}", a.shape, mybir.dt.from_np(a.dtype), kind="ExternalInput").ap())
    args.append(nc.dram_tensor("result", (B, S, D), F32, kind="ExternalOutput").ap())
    args.append(nc.dram_tensor("v_scr", (S, D), F32, kind="Internal").ap())
    args.append(nc.dram_tensor("o_scr", (S, D), F32, kind="Internal").ap())
    args.append(nc.dram_tensor("p_scr", (3, 4, P, S), BF16, kind="Internal").ap())
    decoder(nc, *args)
    r = run_bass_kernel_spmd(nc, [feed], core_ids=[0])
    return r.results[0]["result"]
```

```python
from contextlib import ExitStack

import concourse.bass as bass
from concourse import mybir

F32 = mybir.dt.float32
F32R = mybir.dt.float32r
BF16 = mybir.dt.bfloat16
U8 = mybir.dt.uint8
U32 = mybir.dt.uint32
ALU = mybir.AluOpType
ACT = mybir.ActivationFunctionType
AX = mybir.AxisListType

P = 128
B, S, D = 4, 512, 256
NT, KC = S // P, D // P
H, DH = 16, 16
SK = 64
NE = 8
HID1 = 512
HB1 = HID1 // P
EPS = 1e-5
NJ = 4
HT = S // H
TR = HT // NJ
TERMS_Q = (0, 0, 1, 1, 0, 2)
TERMS_K = (0, 1, 0, 1, 2, 0)
NTERM = len(TERMS_Q)
ROWS6 = NTERM * DH
SCALE_A = float(2 * D) ** -0.5
SCALE_X = float(DH) ** -0.5
GONE = -3e38

W_COLS = {"a_qk": 1024, "a_v": 512, "a_o": 512,
          "x0_q": 512, "x0_k": 512, "x0_v": 512, "x0_o": 512,
          "f0_r": 16,
          "d_q": 512, "d_k": 512, "d_v": 512,
          "x1_q": 512, "x1_qs": 512, "x1_k": 512, "x1_ks": 512, "x1_v": 512, "x1_o": 512,
          "f1_r": 16}
ROW_COLS = {"a_v": 256, "a_o": 256, "x0_v": 256, "x0_o": 256, "f0_o": 256, "d_v": 256,
            "x1_v": 256, "x1_o": 256, "f0_r": 8}
COL_COLS = {"a_qk": 4, "x0_q": 2, "x0_k": 2, "d_q": 2, "d_k": 2, "x1_q": 2, "x1_qs": 2,
            "x1_k": 2, "x1_ks": 2, "f0_b1": 9}
CONST_COLS = {"ident": 128, "causal": 128, "window": 64, "blk": 8,
              "ropeq": 256, "ropek": 128, "iota": 8, "expo": 8}


def share(i, n, total):
    return (i + 1) * total // n - i * total // n


def offsets(cols):
    at, out = 0, {}
    for name, n in cols.items():
        out[name] = (at, at + n)
        at += n
    return out, at


WO, W_ALL = offsets(W_COLS)
RO, R_ALL = offsets(ROW_COLS)
CO, C_ALL = offsets(COL_COLS)
KO, K_ALL = offsets(CONST_COLS)

SEMS = """x_in ctx_in pen_in xt_ps xt_a xt_v x_bias
ln_sum ln_st ln_ag ln_ep ln_rs ln_done r_done
a_qk a_qkf a_hi a_r1 a_mid a_lo a_ps0 a_ps1 a_ps2 a_q6 a_v a_vt a_vd a_vre
a_qr a_kr a_k1 a_one a_s a_mx a_nt a_nh a_nr a_nm a_nl a_ns a_nd a_st a_ex a_pv a_on a_od0 a_od1 a_ot0 a_ot1 a_ot2 a_ri a_no
o_tp o_ta o_tv
c_tp c_ct c_k c_v c_kb0 c_ka c_kc c_kb1 c_vb pen
x_q x_qt x_qa x_s x_sm x_mx x_sub x_ex x_rs x_tp x_pt x_pv x_ri x_on
g_lg g_ls g_mx g_ix g_if g_oh g_sum g_a g_e g_b g_l g_c g_p g_cmb
e_h e_s e_y e_ev e_tp e_ct
e_w0 e_w1 e_w2 d_qk d_ev d_v d_s d_mx d_ex d_rz d_vn
q_tp q_ta q_tv q_lg q_ls q_mx q_ix q_if q_oh q_a q_e q_b q_cmb q_xh q_xl
f_w0 f_w1 f_wh f_wl f_v0 f_v1 f_vh f_vl f_h f_s f_u f_m f_hh f_hl f_y f_ev f_st f_ag f_ep f_rs f_ln f_out""".split()

CH = HB1 * (NE + 1)
FS = 2 * CH
SLOTS = FS + 6
HALF = S // 2
TILES = H * NJ
PARTS = ((0, S // 2, 52), (S // 2, 3 * S // 4, 66), (3 * S // 4, S, None))
NEG = 3
ROWS9 = ROWS6 + NEG
F_GATES, F_START, F_CTX, F_PREP, F_MAX, F_NEG, F_HEADS, F_OUT = 1, 2, 1, 11, 9, 4, 1, 3
F_CROSS, F_MOE, F_KEYS, F_ROPE, F_WINDOW, F_LN = 8, 6, 8, 8, 3, (2, 1)
NRAW = 2
NW13, NW2, NHM = 2, 3, 3
NF0 = 3



def decoder(nc, x, ctx_in, mask, weights, rows, cols, consts, b2rows, ones, f0, experts, out, v_scr, o_scr, p_scr, n_scr):
    with ExitStack() as ctx:
        def sb(name, shape, dt=F32):
            return ctx.enter_context(nc.sbuf_tensor(name, shape, dt))

        W = sb("W", [P, W_ALL])
        BR = sb("BR", [P, R_ALL])
        BC = sb("BC", [P, C_ALL])
        K = sb("K", [P, K_ALL])
        b2 = sb("b2", [NE, D])
        identb = sb("identb", [P, P], BF16)
        causalb = sb("causalb", [P, P], BF16)
        X = sb("X", [P, NT, D])
        XT = sb("XT", [P, KC, S])
        XF = sb("XF", [P, NT, D])
        XTFh = sb("XTFh", [P, KC, S], F32R)
        XTFl = sb("XTFl", [P, KC, S], F32R)
        w13 = sb("w13", [P, NRAW, 512])
        w13h = sb("w13h", [P, NW13, 512], F32R)
        w13l = sb("w13l", [P, NW13, 512], F32R)
        w2 = sb("w2", [P, NRAW, D])
        w2h = sb("w2h", [P, NW2, D], F32R)
        w2l = sb("w2l", [P, NW2, D], F32R)
        hsF = sb("hsF", [P, 2, HALF])
        hmF = sb("hmF", [P, 2, HALF])
        hmFh = sb("hmFh", [P, NHM, HALF], F32R)
        hmFl = sb("hmFl", [P, NHM, HALF], F32R)
        fbuf = sb("fbuf", [P, NF0, 512])
        cmbF = sb("cmbF", [P, NT, NE])
        stats = sb("stats", [P, 2, NT, 6])
        mv = sb("mv", [P, 2, NT, 2])
        veps = sb("veps", [P, 2, NT])
        rstd = sb("rstd", [P, 2, NT])

        r_q6 = sb("r_q6", [P, 4, 1024])
        q6 = r_q6[:].rearrange("p a b -> p (a b)").bitcast(BF16).rearrange("p (c s) -> p c s", c=H)
        kpos = r_q6[:].rearrange("p a b -> p (a b)").bitcast(BF16).rearrange("p (g c r) -> p g c r", c=H, r=TR)
        otok = r_q6[:, 0, :].rearrange("p (t d) -> p t d", t=NT)
        v_d = otok
        OT = r_q6[:, 1, :].rearrange("p (k s) -> p k s", k=KC)
        qT = r_q6[:, 2, :].rearrange("p (k s) -> p k s", k=KC)
        sc = r_q6[:, 3, :].rearrange("p (u h k) -> p u h k", u=2, k=SK)
        r_qpos = sb("r_qpos", [P, 4, 1024])
        qpos = r_qpos[:].rearrange("p a b -> p (a b)").bitcast(BF16).rearrange("p (g c r) -> p g c r", c=H, r=TR)
        v_a = r_qpos[:, 0, :].rearrange("p (t d) -> p t d", t=NT)
        kT = r_qpos[:, 0, :].rearrange("p (k s) -> p k s", k=KC)
        hs = r_qpos[:, 1, :].rearrange("p (u s) -> p u s", u=2)
        ex = r_qpos[:, 2:4, :].rearrange("p a (b s) -> p (a b) s", b=2)
        r_k6 = sb("r_k6", [P, 4096])
        k6 = r_k6[:].bitcast(BF16).rearrange("p (c s) -> p c s", c=H)
        vpos = r_k6[:, 0:TILES * 3 * DH].rearrange("p (g e) -> p g e", e=3 * DH)
        r_parts = sb("r_parts", [P, 3072])
        parts = r_parts[:].bitcast(BF16).rearrange("p (q b s) -> p q b s", q=3, b=4)
        pb = r_parts[:, 0:1024].rearrange("p (u s) -> p u s", u=2)
        pt = r_parts[:, 0:2048].rearrange("p (u s) -> p u s", u=4)
        sums = r_parts[:, 2048:3072].rearrange("p (k s) -> p k s", k=KC)
        negp = r_parts[0:TILES, 2048:2048 + NEG * P // 2].bitcast(BF16).rearrange("p (q n) -> p q n", q=NEG)
        negr = r_parts[0:TILES, 2304:2304 + P]
        ptb = r_parts[:, 1024:2048].rearrange("p (u s) -> p u s", u=2)
        qkf = sb("qkf", [P, 4, S])
        opos = qkf[0:3 * DH].rearrange("p a s -> p (a s)").rearrange("p (b c s) -> p b c s", b=2, c=H)
        nmax = sb("nmax", [P, H * NJ])
        rsum = sb("rsum", [P, H * NJ])
        rinv = sb("rinv", [P, H * NJ])
        ctok = sb("ctok", [SK, D])
        cT = sb("cT", [P, KC, 2, SK])
        kb = [sb(f"kb{i}", [P, KC, 8, SK]) for i in range(2)]
        kr = sb("kr", [P, 3, KC, SK])
        vb = [sb(f"vb{i}", [P, H // 2, 2, DH]) for i in range(2)]
        mask8 = sb("mask8", [P, NT, SK], U8)
        pen = sb("pen", [P, NT, SK])
        lg = sb("lg", [P, NT, NE])
        top = sb("top", [P, NT, 8])
        ix = sb("ix", [P, NT, 8], U32)
        ixf = sb("ixf", [P, NT, 8])
        oh = sb("oh", [P, 2, NT, NE])
        ga = sb("ga", [P, 8, NT, NE])
        cmb = sb("cmb", [P, NT, NE])
        cmbT = sb("cmbT", [NE, S])
        bank = [ctx.enter_context(nc.psum_tensor(f"bank{i}", [P, 512], F32)) for i in range(8)]
        M = bank[0:4]
        FH, FY = bank[4:6], bank[6:8]
        s = {n: ctx.enter_context(nc.semaphore(n)) for n in SEMS}
        w_in = [ctx.enter_context(nc.semaphore(f"w_in{i}")) for i in range(5)]
        setup = ctx.enter_context(nc.semaphore("setup"))
        cast = ctx.enter_context(nc.semaphore("cast"))

        def w(name):
            a, b = WO[name]
            return W[:, a:b].rearrange("p (k n) -> p k n", k=KC)

        def row(name):
            a, b = RO[name]
            return BR[:, a:b]

        def col(name):
            a, b = CO[name]
            return BC[:, a:b]

        def const(name):
            a, b = KO[name]
            return K[:, a:b]

        ident = const("ident")
        with nc.Block() as first:
            @first.sync
            def _(sp):
                sp.dma_start(K[:, :], consts).then_inc(w_in[0], 16)
                sp.dma_start(BC[:, :], cols).then_inc(w_in[0], 16)

            @first.vector
            def _(v):
                v.memset(vb[0][:], 0.0).then_inc(setup, 1)
                v.memset(vb[1][:], 0.0).then_inc(setup, 1)
                v.wait_ge(w_in[0], 32)
                v.tensor_copy(identb[:], ident).then_inc(cast, 1)
                v.tensor_copy(causalb[:], const("causal")).then_inc(cast, 1)
                v.tensor_scalar_mul(col("a_qk")[:, 0:2], col("a_qk")[:, 0:2], SCALE_A).then_inc(cast, 1)
                v.tensor_scalar_mul(col("x0_q"), col("x0_q"), SCALE_X).then_inc(cast, 1)
                v.tensor_scalar_mul(col("d_q"), col("d_q"), 1.0 / D).then_inc(cast, 1)
                v.wait_ge(cast, 5)
                v.wait_ge(setup, 2)

        def step(front, back):
            with nc.Block() as block:
                def slots(slot):
                    at = [0]

                    def run(n):
                        if back is not None:
                            for k in range(at[0], min(at[0] + n, SLOTS)):
                                slot(k)
                            at[0] = min(at[0] + n, SLOTS)
                    return run

                @block.sync
                def _(sp):
                    def load_w13(c):
                        if c >= NRAW:
                            sp.wait_ge(s["f_wl"], c - NRAW + 1)
                        sp.dma_start(w13[:, c % NRAW], experts[c, :, 0:512]).then_inc(s[f"f_w{c % NRAW}"], 16)

                    def load_w2(c):
                        if c >= NRAW:
                            sp.wait_ge(s["f_vl"], c - NRAW + 1)
                        sp.dma_start(w2[:, c % NRAW], experts[c, :, 512:768]).then_inc(s[f"f_v{c % NRAW}"], 16)

                    def load_f0(e):
                        if e >= NF0:
                            sp.wait_ge(s["e_y"], 2 * (e - NF0) + 2)
                        sp.dma_start(fbuf[:, e % NF0, :], f0[e]).then_inc(s[f"e_w{e % NF0}"], 16)

                    def slot(k):
                        if k % 2 and (k + 5) // 2 < CH:
                            load_w13((k + 5) // 2)
                        if k % 2 == 0 and k // 2 + 1 < CH:
                            load_w2(k // 2 + 1)
                        if k == SLOTS - 1:
                            sp.wait_ge(s["f_ln"], NT)
                            sp.dma_start(out[bass.ds(back, 1)].rearrange("a (t p) d -> (a p) t d", p=P), XF[:])\
                                .then_inc(s["f_out"], 16)

                    fill = slots(slot)
                    if back is not None:
                        load_w13(0)
                        load_w13(1)
                        load_w2(0)
                    if front is not None:
                        one = bass.ds(front, 1)
                        sp.dma_start(X[:], x[one].rearrange("a (t p) d -> (a p) t d", p=P)).then_inc(s["x_in"], 16)
                        sp.dma_start(ctok[:], ctx_in[one].rearrange("a p d -> (a p) d")).then_inc(s["ctx_in"], 16)
                        sp.dma_start(mask8[:], mask[one].rearrange("a (t p) k -> (a p) t k", p=P))\
                            .then_inc(s["pen_in"], 16)
                    if back is None:
                        cut = [0, WO["x0_q"][0], WO["d_q"][0], W_ALL]
                        for i in range(3):
                            sp.dma_start(W[:, cut[i]:cut[i + 1]], weights[:, cut[i]:cut[i + 1]])\
                                .then_inc(w_in[i + 1], 16)
                            if i == 0:
                                sp.dma_start(BR[:, :], rows.partition_broadcast(P)).then_inc(w_in[4], 16)
                                sp.dma_start(b2[:, :], b2rows).then_inc(w_in[4], 16)
                    if back is not None:
                        load_w13(2)
                        fill(F_GATES)
                    if front is not None:
                        sp.dma_start(kpos[ROWS6:ROWS9].rearrange("q g c r -> q (g c r)"), ones)\
                            .then_inc(s["a_k1"], 16)
                        for e in range(NF0):
                            load_f0(e)
                        fill(F_START)
                        for part, ready in ((0, "a_hi"), (1, "a_mid"), (2, "a_lo")):
                            sp.wait_ge(s[ready], 4)
                            sp.dma_start(p_scr[part].rearrange("b p s -> p b s"), parts[:, part])\
                                .then_inc(s[f"a_ps{part}"], 16)
                        fill(F_CTX)
                        for part in range(3):
                            sp.wait_ge(s[f"a_ps{part}"], 16)
                            for dst, base, terms in ((q6, 0, TERMS_Q), (k6, 2, TERMS_K)):
                                src = p_scr[part, base:base + 2].rearrange("b (c e) s -> e (b c) s", e=DH)
                                for n, term in enumerate(terms):
                                    if term == part:
                                        sp.dma_start(dst[DH * n:DH * n + DH], src).then_inc(s["a_q6"], 16)
                        sp.wait_ge(s["a_vt"], 2)
                        sp.dma_start(v_scr.rearrange("(t p) f -> p t f", p=P), v_a).then_inc(s["a_vd"], 16)
                        fill(F_PREP)
                        sp.wait_ge(s["a_vd"], 16)
                        sp.wait_ge(s["a_kr"], 4)
                        v_src = v_scr.rearrange("(g r) (c e) -> r c g e", r=TR, e=DH)
                        for r in range(TR):
                            sp.dma_start(vpos[r:P:TR, :, 0:DH], v_src[r]).then_inc(s["a_vre"], 16)
                        for i in range(TILES):
                            fill(share(i, TILES, F_MAX))
                        sp.wait_ge(s["a_ns"], 1)
                        sp.dma_start(n_scr.rearrange("q g n -> g q n"), negp[:]).then_inc(s["a_nd"], 16)
                        sp.wait_ge(s["a_nd"], 16)
                        sp.dma_start(qpos[ROWS6:ROWS9].rearrange("q g c r -> q g (c r)"), n_scr)\
                            .then_inc(s["a_nd"], 16)
                        fill(F_NEG)
                        o_dst = o_scr.rearrange("n (c e) t -> n e c t", e=DH)

                        def results_in(part):
                            first, end, _ = PARTS[part]
                            for b in range(2):
                                sp.wait_ge(s[f"a_od{b}"], 32 * (end // (4 * HT)))
                            for n, dst in enumerate((XT, sums)):
                                sp.dma_start(dst[:, :, first:end],
                                             o_scr[n].rearrange("(k p) t -> p k t", p=P)[:, :, first:end])\
                                    .then_inc(s[f"a_ot{part}"], 16)

                        for m in range(TILES + 3):
                            if m % 8 == 2 and m > 2:
                                g = m // 8 - 1
                                sp.wait_ge(s["a_on"], 2 * g + 2)
                                for n in range(2):
                                    sp.dma_start(o_dst[n, :, :, 2 * HT * g:2 * HT * (g + 1)],
                                                 opos[2 * DH * n:2 * DH * n + DH, g % 2])\
                                        .then_inc(s[f"a_od{g % 2}"], 16)
                                if g in (4, 6):
                                    results_in(g // 2 - 2)
                            fill(share(m, TILES + 3, F_HEADS))
                        results_in(2)
                        fill(F_OUT + sum(F_LN) + F_CROSS + sum(F_LN))
                        for e in range(1, NE + 1):
                            if e + NF0 - 1 <= NE:
                                load_f0(e + NF0 - 1)
                            fill(share(e - 1, NE, F_MOE))
                    fill(SLOTS)
                    if back is not None:
                        sp.wait_ge(s["f_out"], 16)

                @block.tensor
                def _(pe):
                    mm, tr = nc.tensor.matmul, nc.tensor.transpose

                    def feature_major(dst, wt, m0, rhs):
                        for k in range(KC):
                            last = mm(dst, wt[:, k, m0:m0 + P], rhs[:, k, :], start=(k == 0), stop=(k == KC - 1))
                        return last

                    def token_major(dst, src, t, wt):
                        for k in range(KC):
                            last = mm(dst, src[:, k, t * P:(t + 1) * P], wt[:, k, :],
                                      start=(k == 0), stop=(k == KC - 1))
                        return last

                    def three(dst, high, low, rhigh, rlow, start, stop):
                        mm(dst, high, rhigh, start=start, stop=False, skip_group_check=True)
                        mm(dst, high, rlow, start=False, stop=False, skip_group_check=True)
                        return mm(dst, low, rhigh, start=False, stop=stop, skip_group_check=True)

                    def slot(k):
                        if k < FS:
                            c, half = divmod(k, 2)
                            wh, wl = w13h[:, c % NW13], w13l[:, c % NW13]
                            if k == 0:
                                pe.wait_ge(s["q_xl"], 1)
                            if half == 0:
                                pe.wait_ge(s["f_wl"], c + 1)
                            if k >= 2:
                                pe.wait_ge(s["f_m"], k - 1)
                            toks = slice(half * HALF, (half + 1) * HALF)
                            for n in range(2):
                                for kc in range(KC):
                                    at = slice((2 * n + kc) * P, (2 * n + kc + 1) * P)
                                    last = three(FH[k % 2][:, n * HALF:(n + 1) * HALF], wh[:, at], wl[:, at],
                                                 XTFh[:, kc, toks], XTFl[:, kc, toks],
                                                 kc == 0, kc == KC - 1)
                            last.then_inc(s["f_h"], 1)
                        if 3 <= k < FS + 3:
                            j = k - 3
                            c, half = divmod(j, 2)
                            e, hb = divmod(c, HB1)
                            pe.wait_ge(s["f_hl"], j + 1)
                            if half == 0:
                                pe.wait_ge(s["f_vl"], c + 1)
                            if hb == 0 and e >= 1:
                                pe.wait_ge(s["f_ev"], 2 * (e - 1) + half + 1)
                            for t in range(2):
                                at = slice(t * P, (t + 1) * P)
                                last = three(FY[half][:, t * D:(t + 1) * D], hmFh[:, j % NHM, at],
                                             hmFl[:, j % NHM, at], w2h[:, c % NW2], w2l[:, c % NW2],
                                             hb == 0 and t == 0, hb == HB1 - 1)
                            last.then_inc(s["f_y"], 1)

                    def route(dst, name, xt, done):
                        for t in range(NT):
                            for k in range(KC):
                                last = mm(dst[:, t * NE:(t + 1) * NE], xt[:, k, t * P:(t + 1) * P],
                                          w(name)[:, k, :], start=(k == 0), stop=(k == KC - 1))
                        last.then_inc(s[done], 1)

                    if back is not None:
                        for t in range(NT):
                            for k in range(KC):
                                last = tr(M[k][:, t * P:(t + 1) * P], XF[:, t, k * P:(k + 1) * P], ident)
                        last.then_inc(s["q_tp"], 1)
                        pe.wait_ge(s["q_ta"], 1)
                        pe.wait_ge(s["q_tv"], 1)
                        route(M[2], "f1_r", XT, "q_lg")
                    fill = slots(slot)
                    fill(F_GATES)
                    if front is None:
                        fill(SLOTS)
                        return

                    def turn_x(st, src):
                        for t in range(NT):
                            if st == 0:
                                pe.wait_ge(s["x_in"], 16)
                            else:
                                pe.wait_ge(s["ln_done"], NT * (st - 1) + t + 1)
                            for k in range(KC):
                                last = tr(M[2 + k][:, t * P:(t + 1) * P], src[:, t, k * P:(k + 1) * P], ident)
                        last.then_inc(s["xt_ps"], 1)
                        pe.wait_ge(s["xt_a"], st + 1)
                        pe.wait_ge(s["xt_v"], st + 1)

                    def output(wt, src, tiles, parts=()):
                        for t in range(tiles):
                            for n, (first, _, _) in enumerate(parts):
                                if first == t * P:
                                    pe.wait_ge(s["a_no"], n + 1)
                            last = token_major(M[t // 2][:, (t % 2) * D:(t % 2 + 1) * D], src, t, wt)
                            if t % 2 == 1 or t == tiles - 1:
                                last.then_inc(s["r_done"], 1)

                    def project(n_o, wt, tiles):
                        for t in range(tiles):
                            for k in range(KC):
                                last = tr(M[2 + k][:, t * P:(t + 1) * P], otok[:, t, k * P:(k + 1) * P], ident)
                        last.then_inc(s["o_tp"], 1)
                        pe.wait_ge(s["o_ta"], n_o + 1)
                        pe.wait_ge(s["o_tv"], n_o + 1)
                        output(wt, OT, tiles)

                    fill(F_START)
                    pe.wait_ge(w_in[0], 32)
                    pe.wait_ge(w_in[1], 16)
                    if back is not None:
                        pe.wait_ge(s["q_ls"], 1)
                        pe.wait_ge(s["q_xh"], 2)
                    turn_x(0, X)
                    for blk in range(4):
                        feature_major(M[blk][:, :], w("a_qk"), blk * P, XT).then_inc(s["a_qk"], 1)
                    for t in range(NT):
                        if t % 2 == 0:
                            pe.wait_ge(s["a_qkf"], t // 2 + 1)
                        last = token_major(M[t // 2][:, (t % 2) * D:(t % 2 + 1) * D], XT, t, w("a_v"))
                        if t % 2:
                            last.then_inc(s["a_v"], 1)

                    fill(F_CTX)
                    pe.wait_ge(s["ctx_in"], 16)
                    pe.wait_ge(s["a_qkf"], 3)
                    for k in range(KC):
                        last = tr(M[2][:, k * SK:(k + 1) * SK], ctok[:, k * P:(k + 1) * P], ident[0:SK, 0:SK])
                    last.then_inc(s["c_tp"], 1)
                    pe.wait_ge(s["c_ct"], 1)
                    pe.wait_ge(s["a_qkf"], 4)
                    pe.wait_ge(w_in[2], 16)
                    pe.wait_ge(w_in[3], 16)
                    for n, name in enumerate(("x0_k", "x1_k", "x1_ks")):
                        for blk in range(KC):
                            at = (2 * n + blk) * SK
                            for k in range(KC):
                                last = mm(M[3][:, at:at + SK], w(name)[:, k, blk * P:(blk + 1) * P],
                                          cT[:, k, 0, :], start=(k == 0), stop=(k == KC - 1))
                    last.then_inc(s["c_k"], 1)
                    for n in range(2):
                        for k in range(KC):
                            last = mm(M[2][:, n * D:(n + 1) * D], cT[:, k, :, :], w(f"x{n}_v")[:, k, :],
                                      start=(k == 0), stop=(k == KC - 1))
                    last.then_inc(s["c_v"], 1)
                    fill(F_PREP)

                    for i in range(TILES):
                        h, j = divmod(i, NJ)
                        if i < 2:
                            pe.wait_ge(s["a_vt"], i + 1)
                        elif i == 2:
                            pe.wait_ge(s["c_vb"], 4)
                        elif i == 3:
                            pe.wait_ge(s["c_kb1"], 2)
                        else:
                            pe.wait_ge(s["a_mx"], i - 3)
                        if i % H == 0:
                            pe.wait_ge(s["a_qr"], i // H + 1)
                            pe.wait_ge(s["a_kr"], i // H + 1)
                        mm(M[i % 4][:, 0:P * (j + 1)], qpos[0:ROWS6, i, :, :],
                           kpos[0:ROWS6, NJ * h:i + 1, :, :].rearrange("p g c r -> p g (c r)"), start=True, stop=True)
                        mm(M[i % 4][:, P * j:P * (j + 1)], identb[:], causalb[:], start=False, stop=True,
                           skip_group_check=True).then_inc(s["a_s"], 1)
                        fill(share(i, TILES, F_MAX))
                    pe.wait_ge(s["a_mx"], TILES)
                    tr(M[2][0:TILES, 0:P], nmax[:, 0:TILES], ident).then_inc(s["a_nt"], 1)
                    fill(F_NEG)

                    pe.wait_ge(s["a_nd"], 32)
                    pe.wait_ge(s["a_k1"], 16)
                    for m in range(TILES + 3):
                        if m < TILES:
                            h, jj = divmod(m, NJ)
                            if m >= 2:
                                pe.wait_ge(s["a_ex"], m - 1)
                            mm(M[m % 2][:, 0:P * (NJ - jj)], kpos[0:ROWS9, m, :, :],
                               qpos[0:ROWS9, m:NJ * (h + 1), :, :].rearrange("p g c r -> p g (c r)"),
                               start=True, stop=True)
                            mm(M[m % 2][:, 0:P], causalb[:], identb[:], start=False, stop=True,
                               skip_group_check=True).then_inc(s["a_st"], 1)
                        if 2 <= m < TILES + 2:
                            n = m - 2
                            h, jj = divmod(n, NJ)
                            if n == 0:
                                pe.wait_ge(s["a_vre"], 16 * TR)
                                pe.wait_ge(s["a_one"], 1)
                                pe.wait_ge(s["a_nr"], 1)
                            if jj == 0 and h >= 2:
                                pe.wait_ge(s["a_on"], h - 1)
                            pe.wait_ge(s["a_ex"], n + 1)
                            mm(M[2 + h % 2][0:3 * DH, P * jj:S], vpos[:, n, :], pt[:, n % 4, 0:P * (NJ - jj)],
                               start=(jj == 0), stop=(jj == NJ - 1), skip_group_check=True).then_inc(s["a_pv"], 1)
                        fill(share(m, TILES + 3, F_HEADS))
                    fill(F_OUT)
                    pe.wait_ge(s["a_ex"], TILES)
                    output(w("a_o"), XT, NT, PARTS)
                    fill(sum(F_LN))

                    def cross(n, tiles, u0, t0, extra):
                        for u in range(2 * tiles + 2):
                            if u < 2 * tiles:
                                t, g = divmod(u, 2)
                                if u >= 2:
                                    pe.wait_ge(s["x_sm"], u0 + u - 1)
                                mm(M[u % 2][:, :], qT[:, g, t * P:(t + 1) * P], kb[n][:, g, :, :],
                                   start=True, stop=True).then_inc(s["x_s"], 1)
                            if 1 <= u <= 2 * tiles:
                                v_ = u - 1
                                pe.wait_ge(s["x_ex"], u0 + v_ + 1)
                                if u0 + v_:
                                    pe.wait_ge(s["x_pt"], u0 + v_)
                                for pr in range(4):
                                    last = tr(M[2][:, pr * P:(pr + 1) * P], pb[:, v_ % 2, pr * P:(pr + 1) * P], ident)
                                last.then_inc(s["x_tp"], 1)
                            if u >= 2:
                                v_ = u - 2
                                t, g = divmod(v_, 2)
                                pe.wait_ge(s["x_pt"], u0 + v_ + 1)
                                if g == 0 and t >= 1:
                                    pe.wait_ge(s["x_on"], t0 + t)
                                for pr in range(4):
                                    at = (4 * g + pr) * 2 * DH
                                    last = mm(M[3][:, at:at + 2 * DH], ptb[:, v_ % 2, pr * P:(pr + 1) * P],
                                              vb[n][:, 4 * g + pr, :, :], start=True, stop=True)
                                last.then_inc(s["x_pv"], 1)
                            if u < 2 * tiles:
                                fill(share(u, 2 * tiles, extra))
                        pe.wait_ge(s["x_on"], t0 + tiles)

                    turn_x(1, X)
                    for blk in range(KC):
                        feature_major(M[blk][:, :], w("x0_q"), blk * P, XT).then_inc(s["x_q"], 1)
                    pe.wait_ge(s["x_qt"], 2)
                    cross(0, NT, 0, 0, F_CROSS)
                    project(0, w("x0_o"), NT)
                    fill(sum(F_LN))

                    turn_x(2, X)
                    route(M[0], "f0_r", XT, "g_lg")
                    for e in range(NE + 2):
                        if e <= NE:
                            if e == 0:
                                pe.wait_ge(s["g_ls"], 1)
                            if e >= 2:
                                pe.wait_ge(s["e_s"], e - 1)
                            pe.wait_ge(s[f"e_w{e % NF0}"], 16 * (e // NF0 + 1))
                            feature_major(M[e % 2][:, :], fbuf[:, e % NF0, 0:D].rearrange("p (k n) -> p k n", k=KC),
                                          0, XT).then_inc(s["e_h"], 1)
                        if e >= 1:
                            n = e - 1
                            pe.wait_ge(s["e_s"], n + 1)
                            for t in range(NT):
                                if n >= 1 and t % 2 == 0:
                                    pe.wait_ge(s["e_ev"], 2 * (n - 1) + t // 2 + 1)
                                last = mm(M[2 + t // 2][:, (t % 2) * D:(t % 2 + 1) * D], hs[:, n % 2, t * P:(t + 1) * P],
                                          fbuf[:, n % NF0, D:2 * D], start=True, stop=True)
                                if t % 2:
                                    last.then_inc(s["e_y"], 1)
                        if 1 <= e <= NE:
                            fill(share(e - 1, NE, F_MOE))
                    pe.wait_ge(s["g_cmb"], 1)
                    for t in range(NT):
                        last = tr(M[1][0:NE, t * P:(t + 1) * P], cmb[:, t, :], ident)
                    last.then_inc(s["e_tp"], 1)
                    pe.wait_ge(s["e_ct"], 1)
                    for t in range(NT):
                        if t % 2 == 0:
                            pe.wait_ge(s["e_ev"], 2 * NE + t // 2 + 1)
                        last = mm(M[2 + t // 2][:, (t % 2) * D:(t % 2 + 1) * D], cmbT[:, t * P:(t + 1) * P], b2[:],
                                  start=True, stop=True)
                        if t % 2:
                            last.then_inc(s["e_y"], 1)
                    fill(sum(F_LN))

                    turn_x(3, X)
                    for blk in range(KC):
                        feature_major(M[blk][:, :], w("d_q"), blk * P, XT).then_inc(s["d_qk"], 1)
                    for blk in range(KC):
                        feature_major(M[2 + blk][:, :], w("d_k"), blk * P, XT).then_inc(s["d_qk"], 1)
                    for t in range(NT):
                        if t % 2 == 0:
                            pe.wait_ge(s["x_qt"], 3 + t // 2)
                        last = token_major(M[t // 2][:, (t % 2) * D:(t % 2 + 1) * D], XT, t, w("d_v"))
                        if t % 2:
                            last.then_inc(s["d_v"], 1)
                    pe.wait_ge(s["d_ev"], 2)
                    for j in range(NT):
                        if j >= 2:
                            pe.wait_ge(s["d_ev"], j + 1)
                        for k in range(KC):
                            last = mm(M[(2 + j) % 4][:, :], kT[:, k, j * P:(j + 1) * P], qT[:, k, :],
                                      start=(k == 0), stop=(k == KC - 1))
                        last.then_inc(s["d_s"], 1)
                    fill(F_KEYS)
                    pe.wait_ge(s["d_ex"], 2)
                    for j in range(NT):
                        pe.wait_ge(s["d_ex"], j + 1)
                        pe.wait_ge(s["d_vn"], j + 1)
                        for t in range(NT):
                            last = mm(M[2 + t // 2][:, (t % 2) * D:(t % 2 + 1) * D], ex[:, j, t * P:(t + 1) * P],
                                      v_d[:, j, :], start=(j == 0 and t % 2 == 0), stop=(j == NT - 1),
                                      skip_group_check=True)
                            if j == NT - 1 and t % 2:
                                last.then_inc(s["r_done"], 1)
                    fill(sum(F_LN))

                    turn_x(4, X)
                    for n, name in enumerate(("x1_q", "x1_qs")):
                        for blk in range(KC):
                            for k in range(KC):
                                last = mm(M[0][:, (2 * n + blk) * P:(2 * n + blk + 1) * P],
                                          w(name)[:, k, blk * P:(blk + 1) * P], XT[:, k, 0:P],
                                          start=(k == 0), stop=(k == KC - 1))
                    last.then_inc(s["x_q"], 1)
                    fill(F_ROPE)
                    pe.wait_ge(s["x_qt"], 6)
                    cross(1, 1, 2 * NT, NT, F_WINDOW)
                    project(1, w("x1_o"), 1)
                    fill(SLOTS)

                @block.scalar
                def _(act):
                    A = nc.scalar.activation

                    def w13_high(c):
                        act.wait_ge(s[f"f_w{c % NRAW}"], 16 * (c // NRAW + 1))
                        if c >= NW13:
                            act.wait_ge(s["f_h"], 2 * (c - NW13) + 2)
                        A(w13h[:, c % NW13], w13[:, c % NRAW], ACT.Copy).then_inc(s["f_wh"], 1)

                    def w2_high(c):
                        act.wait_ge(s[f"f_v{c % NRAW}"], 16 * (c // NRAW + 1))
                        if c >= NW2:
                            act.wait_ge(s["f_y"], 2 * (c - NW2) + 2)
                        A(w2h[:, c % NW2], w2[:, c % NRAW], ACT.Copy).then_inc(s["f_vh"], 1)

                    def slot(k):
                        if 1 <= k <= FS:
                            j = k - 1
                            act.wait_ge(s["f_h"], j + 1)
                            if j >= 2:
                                act.wait_ge(s["f_m"], j - 1)
                            A(hsF[:, j % 2, :], FH[j % 2][:, 0:HALF], ACT.Tanh, scale=0.5).then_inc(s["f_s"], 1)
                        if 2 <= k <= FS + 1:
                            j = k - 2
                            act.wait_ge(s["f_m"], j + 1)
                            if j >= NHM:
                                act.wait_ge(s["f_y"], j - NHM + 1)
                            A(hmFh[:, j % NHM, :], hmF[:, j % 2, :], ACT.Copy).then_inc(s["f_hh"], 1)
                        if k % 2 and (k + 3) // 2 < CH:
                            w13_high((k + 3) // 2)
                        if k % 2 == 0 and k // 2 < CH:
                            w2_high(k // 2)

                    if back is not None:
                        act.wait_ge(s["q_tp"], 1)
                        A(XT[:, 0, :], M[0][:, :], ACT.Copy).then_inc(s["q_ta"], 1)
                        A(XTFh[:, 0, :], M[0][:, :], ACT.Copy).then_inc(s["q_xh"], 1)
                        w13_high(0)
                        w13_high(1)
                    fill = slots(slot)
                    fill(F_GATES)
                    if back is not None:
                        act.wait_ge(s["q_a"], 1)
                        A(ga[:, 1, :, 0:1], ga[:, 0, :, 0:1], ACT.Exp).then_inc(s["q_e"], 1)
                    if front is None:
                        fill(SLOTS)
                        return

                    def xt_copy(st, dst):
                        act.wait_ge(s["xt_ps"], st + 1)
                        A(dst[:, 0, :], M[2][:, :], ACT.Copy).then_inc(s["xt_a"], 1)

                    def ot_copy(n, tiles):
                        act.wait_ge(s["o_tp"], n + 1)
                        A(OT[:, 0, 0:tiles * P], M[2][:, 0:tiles * P], ACT.Copy).then_inc(s["o_ta"], 1)

                    fill(F_START)
                    xt_copy(0, XT)
                    for blk in range(4):
                        act.wait_ge(s["a_qk"], blk + 1)
                        A(qkf[:, blk, :], M[blk][:, :], ACT.Identity, bias=col("a_qk")[:, blk:blk + 1],
                          scale=SCALE_A if blk < 2 else 1.0).then_inc(s["a_qkf"], 1)
                    for blk in range(4):
                        act.wait_ge(s["a_qkf"], blk + 1)
                        A(parts[:, 0, blk, :], qkf[:, blk, :], ACT.Copy).then_inc(s["a_hi"], 1)
                    for blk in range(4):
                        act.wait_ge(s["a_r1"], blk + 1)
                        A(parts[:, 1, blk, :], qkf[:, blk, :], ACT.Copy).then_inc(s["a_mid"], 1)
                    fill(F_CTX)
                    fill(F_PREP)

                    act.wait_ge(s["a_qr"], 4)
                    act.wait_ge(s["a_q6"], 16 * 2 * NTERM)
                    for g in range(4):
                        A(kpos[0:ROWS6, H * g:H * g + H],
                          k6[0:ROWS6, :, P * g:P * g + P].rearrange("p c (g r) -> p g c r", r=TR), ACT.Copy)\
                            .then_inc(s["a_kr"], 1)
                    for i in range(TILES):
                        fill(share(i, TILES, F_MAX))
                    fill(F_NEG)
                    for m in range(TILES + 3):
                        if m < TILES:
                            act.wait_ge(s["a_st"], m + 1)
                            if m >= 4:
                                act.wait_ge(s["a_pv"], m - 3)
                            n_q = P * (NJ - m % NJ)
                            A(pt[:, m % 4, 0:n_q], M[m % 2][:, 0:n_q], ACT.Exp).then_inc(s["a_ex"], 1)
                        if m % 4 == 2 and m > 2:
                            h = m // 4 - 1
                            act.wait_ge(s["a_pv"], NJ * (h + 1))
                            g, odd = divmod(h, 2)
                            if g >= 2 and not odd:
                                act.wait_ge(s[f"a_od{g % 2}"], 32 * (g // 2))
                            A(opos[:, g % 2, :, HT * odd:HT * odd + HT].rearrange("p c (j r) -> p j c r", r=TR),
                              M[2 + h % 2][0:3 * DH, :].rearrange("p (j c r) -> p j c r", j=NJ, c=H), ACT.Copy)\
                                .then_inc(s["a_on"], 1)
                        fill(share(m, TILES + 3, F_HEADS))
                    fill(F_OUT)
                    fill(sum(F_LN))

                    def cross(tiles, u0, extra):
                        for u in range(2 * tiles + 1):
                            if u < 2 * tiles:
                                act.wait_ge(s["x_sub"], u0 + u + 1)
                                if u >= 2:
                                    act.wait_ge(s["x_tp"], u0 + u - 1)
                                    act.wait_ge(s["x_rs"], u0 + u - 1)
                                A(pb[:, u % 2, :], sc[:, u % 2, :, :].rearrange("p a b -> p (a b)"), ACT.Exp)\
                                    .then_inc(s["x_ex"], 1)
                            if u >= 1:
                                v_ = u - 1
                                act.wait_ge(s["x_tp"], u0 + v_ + 1)
                                if v_ >= 2:
                                    act.wait_ge(s["x_pv"], u0 + v_ - 1)
                                A(ptb[:, v_ % 2, :], M[2][:, :], ACT.Copy).then_inc(s["x_pt"], 1)
                            if u < 2 * tiles:
                                fill(share(u, 2 * tiles, extra))

                    xt_copy(1, XT)
                    for blk in range(KC):
                        act.wait_ge(s["x_q"], blk + 1)
                        A(qT[:, blk, :], M[blk][:, :], ACT.Identity, bias=col("x0_q")[:, blk:blk + 1],
                          scale=SCALE_X).then_inc(s["x_qt"], 1)
                    cross(NT, 0, F_CROSS)
                    ot_copy(0, NT)
                    fill(sum(F_LN))

                    xt_copy(2, XT)
                    for e in range(NE + 1):
                        if e == 1:
                            act.wait_ge(s["g_a"], 1)
                            A(ga[:, 1], ga[:, 0], ACT.Exp).then_inc(s["g_e"], 1)
                            act.wait_ge(s["g_b"], 1)
                            A(ga[:, 4], ga[:, 2], ACT.Ln).then_inc(s["g_l"], 1)
                        act.wait_ge(s["e_h"], e + 1)
                        if e >= 2:
                            act.wait_ge(s["e_y"], 2 * (e - 1))
                        A(hs[:, e % 2, :], M[e % 2][:, :], ACT.Silu, bias=col("f0_b1")[:, e:e + 1])\
                            .then_inc(s["e_s"], 1)
                        if e >= 1:
                            fill(share(e - 1, NE, F_MOE))
                    fill(sum(F_LN))

                    xt_copy(3, XT)
                    for blk in range(KC):
                        act.wait_ge(s["d_qk"], blk + 1)
                        A(qT[:, blk, :], M[blk][:, :], ACT.Identity, bias=col("d_q")[:, blk:blk + 1],
                          scale=1.0 / D).then_inc(s["x_qt"], 1)
                    for j in range(NT):
                        act.wait_ge(s["d_mx"], j + 1)
                        A(ex[:, j, :], M[(2 + j) % 4][:, :], ACT.Exp, bias=nmax[:, j:j + 1],
                          accum_out=rsum[:, j:j + 1]).then_inc(s["d_ex"], 1)
                    fill(F_KEYS)
                    fill(sum(F_LN))

                    xt_copy(4, XT)
                    fill(F_ROPE)
                    cross(1, 2 * NT, F_WINDOW)
                    ot_copy(1, 1)
                    fill(SLOTS)

                @block.gpsimd
                def _(pool):
                    expo = const("expo")

                    def rsqrt(n, want, count, eps_done, rs_done, turn):
                        pool.wait_ge(s[want], count)
                        pool.tensor_scalar(veps[:, n], mv[:, n, :, 1], EPS, None, ALU.add).then_inc(s[eps_done], 1)
                        pool.wait_ge(s[eps_done], turn)
                        pool.tensor_tensor(rstd[:, n], veps[:, n], expo[:, 0:NT], ALU.pow).then_inc(s[rs_done], 1)

                    def w13_low(c):
                        pool.wait_ge(s["f_wh"], c + 1)
                        pool.tensor_tensor(w13l[:, c % NW13], w13[:, c % NRAW], w13h[:, c % NW13].bitcast(F32),
                                           ALU.subtract).then_inc(s["f_wl"], 1)

                    def w2_low(c):
                        pool.wait_ge(s["f_vh"], c + 1)
                        pool.tensor_tensor(w2l[:, c % NW2], w2[:, c % NRAW], w2h[:, c % NW2].bitcast(F32),
                                           ALU.subtract).then_inc(s["f_vl"], 1)

                    def slot(k):
                        if k % 2 and (k + 3) // 2 < CH:
                            w13_low((k + 3) // 2)
                        if k % 2 == 0 and k // 2 < CH:
                            w2_low(k // 2)
                        if k == SLOTS - 2:
                            rsqrt(1, "f_ag", NT, "f_ep", "f_rs", 1)

                    fill = slots(slot)
                    pool.wait_ge(w_in[0], 32)
                    pool.wait_ge(w_in[4], 32)
                    if back is not None:
                        w13_low(0)
                        w13_low(1)
                    if front is None:
                        fill(SLOTS)
                        return

                    def add_bias(st, name):
                        pool.wait_ge(s["xt_ps"], st + 1)
                        pool.tensor_tensor(X[:], X[:], row(name).unsqueeze(1).to_broadcast([P, NT, D]), ALU.add)\
                            .then_inc(s["x_bias"], 1)

                    def main_rsqrt(st):
                        rsqrt(0, "ln_ag", NT * (st + 1), "ln_ep", "ln_rs", st + 1)

                    fill(F_GATES + F_START)
                    add_bias(0, "a_o")
                    fill(F_CTX + F_PREP)
                    pool.wait_ge(s["a_kr"], 4)
                    pool.memset(vpos[:, :, DH:3 * DH], 1.0).then_inc(s["a_one"], 1)
                    fill(F_MAX + F_NEG + F_HEADS + F_OUT)
                    main_rsqrt(0)
                    fill(sum(F_LN))
                    add_bias(1, "x0_o")
                    fill(F_CROSS)
                    main_rsqrt(1)
                    fill(sum(F_LN))
                    add_bias(2, "f0_o")
                    pool.wait_ge(s["g_c"], 1)
                    pool.tensor_tensor(ga[:, 6], ga[:, 5], expo[:, 4:5].unsqueeze(1).to_broadcast([P, NT, NE]),
                                       ALU.pow).then_inc(s["g_p"], 1)
                    fill(F_MOE)
                    main_rsqrt(2)
                    fill(sum(F_LN))
                    fill(F_KEYS)
                    main_rsqrt(3)
                    fill(sum(F_LN))
                    add_bias(4, "x1_o")
                    fill(SLOTS)
                    main_rsqrt(4)

                @block.vector
                def _(v):
                    V = nc.vector

                    def evacuate(e, half):
                        v.wait_ge(s["f_y"], 2 * (HB1 * e + HB1 - 1) + half + 1)
                        if e >= 1:
                            v.wait_ge(s["f_ev"], 2 * (e - 1) + half + 1)
                        if e == 0:
                            last = V.scalar_tensor_tensor(XF[:, 2 * half:2 * half + 2, :],
                                                          FY[half][:, :].rearrange("p (t d) -> p t d", t=2), 0.5,
                                                          XF[:, 2 * half:2 * half + 2, :], ALU.mult, ALU.add)
                        else:
                            for t in (2 * half, 2 * half + 1):
                                last = V.scalar_tensor_tensor(XF[:, t, :], FY[half][:, (t % 2) * D:(t % 2 + 1) * D],
                                                              cmbF[:, t, e - 1:e], XF[:, t, :], ALU.mult, ALU.add)
                        last.then_inc(s["f_ev"], 1)

                    def statistics(n, src, ready, count, st_done, ag_done, base):
                        v.wait_ge(s[ready], count)
                        for t in range(NT):
                            V.bn_stats(stats[:, n, t, :], src[:, t, :]).then_inc(s[st_done], 1)
                        for t in range(NT):
                            v.wait_ge(s[st_done], base + t + 1)
                            V.bn_aggr(mv[:, n, t, :], stats[:, n, t, :]).then_inc(s[ag_done], 1)

                    def normalise(n, src, dst, rs_done, count, done):
                        v.wait_ge(s[rs_done], count)
                        for t in range(NT):
                            V.tensor_scalar(dst[:, t, :], src[:, t, :], mv[:, n, t, 0:1], rstd[:, n, t:t + 1],
                                            ALU.subtract, ALU.mult).then_inc(s[done], 1)

                    def slot(k):
                        if 1 <= k <= FS:
                            j = k - 1
                            v.wait_ge(s["f_s"], j + 1)
                            V.scalar_tensor_tensor(hsF[:, j % 2, :], hsF[:, j % 2, :], 1.0, FH[j % 2][:, 0:HALF],
                                                   ALU.add, ALU.mult).then_inc(s["f_u"], 1)
                            v.wait_ge(s["f_u"], j + 1)
                            if j >= 2:
                                v.wait_ge(s["f_hl"], j - 1)
                            V.tensor_tensor(hmF[:, j % 2, :], FH[j % 2][:, HALF:S], hsF[:, j % 2, :], ALU.mult)\
                                .then_inc(s["f_m"], 1)
                        if 2 <= k <= FS + 1:
                            j = k - 2
                            v.wait_ge(s["f_hh"], j + 1)
                            V.tensor_tensor(hmFl[:, j % NHM, :], hmF[:, j % 2, :],
                                            hmFh[:, j % NHM, :].bitcast(F32), ALU.subtract).then_inc(s["f_hl"], 1)
                        per = 2 * HB1
                        for half in range(2):
                            if k >= per + 2 + half and (k - per - 2 - half) % per == 0:
                                evacuate((k - per - 2 - half) // per, half)
                        if k == SLOTS - 3:
                            statistics(1, XF, "f_ev", 2 * (NE + 1), "f_st", "f_ag", 0)
                        if k == SLOTS - 2:
                            normalise(1, XF, XF, "f_rs", 1, "f_ln")

                    def pick(pre):
                        for t in range(NT):
                            V.max(top[:, t, :], lg[:, t, :]).then_inc(s[pre + "mx"], 1)
                        for t in range(NT):
                            v.wait_ge(s[pre + "mx"], t + 1)
                            V.max_index(ix[:, t, :], top[:, t, :], lg[:, t, :]).then_inc(s[pre + "ix"], 1)
                        v.wait_ge(s[pre + "ix"], NT)
                        V.tensor_copy(ixf[:], ix[:]).then_inc(s[pre + "if"], 1)
                        v.wait_ge(s[pre + "if"], 1)
                        for k in range(2):
                            V.tensor_tensor(oh[:, k], ixf[:, :, k:k + 1].to_broadcast([P, NT, NE]),
                                            const("iota").unsqueeze(1).to_broadcast([P, NT, NE]), ALU.is_equal)\
                                .then_inc(s[pre + "oh"], 1)
                        v.wait_ge(s[pre + "oh"], 2)

                    if back is not None:
                        v.wait_ge(s["q_tp"], 1)
                        V.tensor_copy(XT[:, 1, :], M[1][:, :]).then_inc(s["q_tv"], 1)
                        V.tensor_copy(XTFh[:, 1, :], M[1][:, :]).then_inc(s["q_xh"], 1)
                        v.wait_ge(s["q_xh"], 2)
                        v.wait_ge(s["q_ta"], 1)
                        V.tensor_tensor(XTFl[:], XT[:], XTFh[:].bitcast(F32), ALU.subtract).then_inc(s["q_xl"], 1)
                        v.wait_ge(s["q_lg"], 1)
                        V.tensor_copy(lg[:], M[2][:, 0:NT * NE].rearrange("p (t e) -> p t e", e=NE))\
                            .then_inc(s["q_ls"], 1)
                    fill = slots(slot)
                    fill(F_GATES)
                    if back is not None:
                        v.wait_ge(s["q_ls"], 1)
                        pick("q_")
                        V.tensor_tensor(ga[:, 0, :, 0:1], top[:, :, 1:2], top[:, :, 0:1], ALU.subtract)\
                            .then_inc(s["q_a"], 1)
                        v.wait_ge(s["q_e"], 1)
                        V.tensor_scalar(ga[:, 2, :, 0:1], ga[:, 1, :, 0:1], 1.0, None, ALU.add).then_inc(s["q_b"], 1)
                        v.wait_ge(s["q_b"], 1)
                        V.reciprocal(ga[:, 3, :, 0:1], ga[:, 2, :, 0:1]).then_inc(s["q_b"], 1)
                        v.wait_ge(s["q_b"], 2)
                        V.tensor_tensor(ga[:, 4, :, 0:1], ga[:, 3, :, 0:1], ga[:, 1, :, 0:1], ALU.mult)\
                            .then_inc(s["q_b"], 1)
                        V.tensor_tensor(ga[:, 5], oh[:, 0], ga[:, 3, :, 0:1].to_broadcast([P, NT, NE]), ALU.mult)\
                            .then_inc(s["q_b"], 1)
                        v.wait_ge(s["q_b"], 4)
                        V.tensor_tensor(ga[:, 6], oh[:, 1], ga[:, 4, :, 0:1].to_broadcast([P, NT, NE]), ALU.mult)\
                            .then_inc(s["q_b"], 1)
                        v.wait_ge(s["q_b"], 5)
                        V.tensor_tensor(ga[:, 7], ga[:, 5], ga[:, 6], ALU.add).then_inc(s["q_b"], 1)
                        v.wait_ge(s["q_b"], 6)
                        V.tensor_scalar(cmbF[:], ga[:, 7], 0.5, None, ALU.mult).then_inc(s["q_cmb"], 1)
                        v.wait_ge(s["q_cmb"], 1)

                    if front is None:
                        fill(SLOTS)
                        return

                    def xt_copy(st, dst):
                        v.wait_ge(s["xt_ps"], st + 1)
                        V.tensor_copy(dst[:, 1, :], M[3][:, :]).then_inc(s["xt_v"], 1)

                    def ot_copy(n, tiles):
                        v.wait_ge(s["o_tp"], n + 1)
                        V.tensor_copy(OT[:, 1, 0:tiles * P], M[3][:, 0:tiles * P]).then_inc(s["o_tv"], 1)

                    def add_result(banks, r0, sums):
                        for g, b in enumerate(banks):
                            v.wait_ge(s["r_done"], r0 + g + 1)
                            n = 2 if len(banks) == 2 else 1
                            V.tensor_tensor(X[:, 2 * g:2 * g + n, :],
                                            M[b][:, 0:n * D].rearrange("p (t d) -> p t d", t=n),
                                            X[:, 2 * g:2 * g + n, :], ALU.add).then_inc(s["ln_sum"], 1)

                    def layernorm(st, ready, count, dst):
                        statistics(0, X, ready, count, "ln_st", "ln_ag", NT * st)
                        if st < 4:
                            fill(F_LN[0])
                        normalise(0, X, dst, "ln_rs", st + 1, "ln_done")
                        if st < 4:
                            fill(F_LN[1])

                    fill(F_START)
                    v.wait_ge(w_in[4], 32)
                    v.wait_ge(s["pen_in"], 16)
                    V.tensor_scalar(pen[:], mask8[:], GONE, 10.0, ALU.mult, ALU.mult).then_inc(s["pen"], 1)
                    xt_copy(0, XT)
                    for blk in range(4):
                        v.wait_ge(s["a_hi"], blk + 1)
                        V.tensor_tensor(qkf[:, blk, :], qkf[:, blk, :], parts[:, 0, blk, :], ALU.subtract)\
                            .then_inc(s["a_r1"], 1)
                    for g in range(2):
                        v.wait_ge(s["a_v"], g + 1)
                        V.tensor_tensor(v_a[:, 2 * g:2 * g + 2, :],
                                        M[g][:, :].rearrange("p (t d) -> p t d", t=2),
                                        row("a_v").unsqueeze(1).to_broadcast([P, 2, D]), ALU.add)\
                            .then_inc(s["a_vt"], 1)
                    for blk in range(4):
                        v.wait_ge(s["a_mid"], blk + 1)
                        V.tensor_tensor(parts[:, 2, blk, :], qkf[:, blk, :], parts[:, 1, blk, :], ALU.subtract)\
                            .then_inc(s["a_lo"], 1)

                    fill(F_CTX)
                    v.wait_ge(s["c_tp"], 1)
                    V.tensor_copy(cT[:], M[2][:, 0:KC * SK].rearrange("p (k n) -> p k n", k=KC)
                                  .unsqueeze(2).to_broadcast([P, KC, 2, SK])).then_inc(s["c_ct"], 1)
                    v.wait_ge(s["c_k"], 1)
                    blkmask = const("blk").unsqueeze(2).to_broadcast([P, 8, SK])

                    def kbank(n, blk):
                        return M[3][:, (2 * n + blk) * SK:(2 * n + blk + 1) * SK]

                    for blk in range(KC):
                        V.scalar_tensor_tensor(kb[0][:, blk], kbank(0, blk).unsqueeze(1).to_broadcast([P, 8, SK]),
                                               col("x0_k")[:, blk:blk + 1], blkmask, ALU.add, ALU.mult)\
                            .then_inc(s["c_kb0"], 1)
                    rk = const("ropek")
                    for blk in range(KC):
                        V.scalar_tensor_tensor(kr[:, 0, blk], kbank(1, blk), col("x1_k")[:, blk:blk + 1], rk[:, 0:SK],
                                               ALU.add, ALU.mult).then_inc(s["c_ka"], 1)
                        V.scalar_tensor_tensor(kr[:, 1, blk], kbank(2, blk), col("x1_ks")[:, blk:blk + 1],
                                               rk[:, SK:2 * SK], ALU.add, ALU.mult).then_inc(s["c_ka"], 1)
                    v.wait_ge(s["c_ka"], 4)
                    V.tensor_tensor(kr[:, 2], kr[:, 0], kr[:, 1], ALU.add).then_inc(s["c_kc"], 1)
                    v.wait_ge(s["c_kc"], 1)
                    for blk in range(KC):
                        V.tensor_tensor(kb[1][:, blk], kr[:, 2, blk].unsqueeze(1).to_broadcast([P, 8, SK]), blkmask,
                                        ALU.mult).then_inc(s["c_kb1"], 1)
                    v.wait_ge(s["c_v"], 1)
                    for n in range(2):
                        for half in range(2):
                            rows_ = slice(SK * half, SK * half + SK)
                            src = M[2][rows_, n * D:(n + 1) * D].rearrange("p (a b e) -> p a b e", b=2, e=DH)
                            bias = row(f"x{n}_v")[rows_].rearrange("p (a b e) -> p a b e", b=2, e=DH)
                            V.tensor_tensor(vb[n][rows_, :, half, :], src[:, :, half, :], bias[:, :, half, :], ALU.add)\
                                .then_inc(s["c_vb"], 1)
                    fill(F_PREP)

                    v.wait_ge(s["a_q6"], 16 * 2 * NTERM)
                    v.wait_ge(s["a_vd"], 16)
                    for g in range(4):
                        V.tensor_copy(qpos[0:ROWS6, H * g:H * g + H],
                                      q6[0:ROWS6, :, P * g:P * g + P].rearrange("p c (g r) -> p g c r", r=TR))\
                            .then_inc(s["a_qr"], 1)

                    for i in range(TILES):
                        v.wait_ge(s["a_s"], i + 1)
                        V.tensor_reduce(nmax[:, i:i + 1], M[i % 4][:, 0:P * (i % NJ + 1)], AX.X, ALU.max,
                                        negate=True).then_inc(s["a_mx"], 1)
                        fill(share(i, TILES, F_MAX))
                    v.wait_ge(s["a_nt"], 1)
                    neg = M[2][0:TILES, 0:P]
                    V.tensor_copy(negp[:, 0, :], neg).then_inc(s["a_nh"], 1)
                    v.wait_ge(s["a_nh"], 1)
                    V.tensor_tensor(negr[:], neg, negp[:, 0, :], ALU.subtract).then_inc(s["a_nr"], 1)
                    v.wait_ge(s["a_nr"], 1)
                    V.tensor_copy(negp[:, 1, :], negr[:]).then_inc(s["a_nm"], 1)
                    v.wait_ge(s["a_nm"], 1)
                    V.tensor_tensor(negp[:, 2, :], negr[:], negp[:, 1, :], ALU.subtract).then_inc(s["a_ns"], 1)
                    fill(F_NEG)

                    def normalise_heads(part):
                        first, end, _ = PARTS[part]
                        v.wait_ge(s[f"a_ot{part}"], 32)
                        V.reciprocal(sums[:, :, first:end], sums[:, :, first:end]).then_inc(s["a_ri"], 1)
                        v.wait_ge(s["a_ri"], part + 1)
                        V.tensor_tensor(XT[:, :, first:end], XT[:, :, first:end], sums[:, :, first:end], ALU.mult)\
                            .then_inc(s["a_no"], 1)

                    for m in range(TILES + 3):
                        for n, (_, _, at) in enumerate(PARTS):
                            if m == at:
                                normalise_heads(n)
                        fill(share(m, TILES + 3, F_HEADS))
                    fill(F_OUT)
                    normalise_heads(2)
                    v.wait_ge(s["x_bias"], 1)
                    add_result((0, 1), 0, 0)
                    layernorm(0, "ln_sum", 2, X)

                    def cross(n, tiles, u0, t0, penalty, extra):
                        for u in range(2 * tiles + 2):
                            if u < 2 * tiles:
                                t, g = divmod(u, 2)
                                cur = sc[:, u % 2]
                                mx = nmax[:, 8 * (u % 2):8 * (u % 2) + 8]
                                v.wait_ge(s["x_s"], u0 + u + 1)
                                if u >= 2:
                                    v.wait_ge(s["x_ex"], u0 + u - 1)
                                V.tensor_tensor(cur, M[u % 2][:, :].rearrange("p (h k) -> p h k", k=SK),
                                                penalty(t).unsqueeze(1).to_broadcast([P, 8, SK]), ALU.add)\
                                    .then_inc(s["x_sm"], 1)
                                v.wait_ge(s["x_sm"], u0 + u + 1)
                                V.tensor_reduce(mx, cur, AX.X, ALU.max).then_inc(s["x_mx"], 1)
                                v.wait_ge(s["x_mx"], u0 + u + 1)
                                V.tensor_tensor(cur, cur, mx.unsqueeze(2).to_broadcast([P, 8, SK]), ALU.subtract)\
                                    .then_inc(s["x_sub"], 1)
                            if 1 <= u <= 2 * tiles:
                                v_ = u - 1
                                v.wait_ge(s["x_ex"], u0 + v_ + 1)
                                V.tensor_reduce(rsum[:, 8 * v_:8 * v_ + 8],
                                                pb[:, v_ % 2, :].rearrange("p (h k) -> p h k", k=SK),
                                                AX.X, ALU.add).then_inc(s["x_rs"], 1)
                            if u >= 2 and u % 2 == 1:
                                t = (u - 2) // 2
                                v.wait_ge(s["x_rs"], u0 + 2 * t + 2)
                                V.reciprocal(rinv[:, H * t:H * t + H], rsum[:, H * t:H * t + H]).then_inc(s["x_ri"], 1)
                                v.wait_ge(s["x_ri"], t0 + t + 1)
                                v.wait_ge(s["x_pv"], u0 + 2 * t + 2)
                                V.tensor_tensor(otok[:, t, :].rearrange("p (h e) -> p h e", e=DH),
                                                M[3][:, 0:D].rearrange("p (h e) -> p h e", e=DH),
                                                rinv[:, H * t:H * t + H].unsqueeze(2).to_broadcast([P, H, DH]), ALU.mult)\
                                    .then_inc(s["x_on"], 1)
                            if u < 2 * tiles:
                                fill(share(u, 2 * tiles, extra))

                    xt_copy(1, XT)
                    v.wait_ge(s["pen"], 1)
                    cross(0, NT, 0, 0, lambda t: pen[:, t, :], F_CROSS)
                    ot_copy(0, NT)
                    v.wait_ge(s["x_bias"], 2)
                    add_result((0, 1), 2, 2)
                    layernorm(1, "ln_sum", 4, X)

                    xt_copy(2, XT)
                    v.wait_ge(s["g_lg"], 1)
                    V.tensor_tensor(lg[:], M[0][:, 0:NT * NE].rearrange("p (t e) -> p t e", e=NE),
                                    row("f0_r").unsqueeze(1).to_broadcast([P, NT, NE]), ALU.add).then_inc(s["g_ls"], 1)
                    v.wait_ge(s["g_ls"], 1)
                    V.scalar_tensor_tensor(ga[:, 0], lg[:], -1.0, lg[:], ALU.mult, ALU.min).then_inc(s["g_a"], 1)
                    pick("g_")

                    def leave(n):
                        for half in range(2):
                            v.wait_ge(s["e_y"], 2 * n + half + 1)
                            if n >= 1:
                                v.wait_ge(s["e_ev"], 2 * (n - 1) + half + 1)
                            if n in (0, NE + 1):
                                last = V.tensor_tensor(X[:, 2 * half:2 * half + 2, :],
                                                       M[2 + half][:, :].rearrange("p (t d) -> p t d", t=2),
                                                       X[:, 2 * half:2 * half + 2, :], ALU.add)
                            else:
                                for t in (2 * half, 2 * half + 1):
                                    last = V.scalar_tensor_tensor(
                                        X[:, t, :], M[2 + half][:, (t % 2) * D:(t % 2 + 1) * D],
                                        cmb[:, t, n - 1:n], X[:, t, :], ALU.mult, ALU.add)
                            last.then_inc(s["e_ev"], 1)

                    for e in range(1, NE + 2):
                        if e == 1:
                            v.wait_ge(s["x_bias"], 3)
                            leave(0)
                            v.wait_ge(s["g_e"], 1)
                            V.tensor_scalar(ga[:, 2], ga[:, 1], 1.0, None, ALU.add).then_inc(s["g_b"], 1)
                            v.wait_ge(s["g_b"], 1)
                            V.tensor_scalar(ga[:, 3], ga[:, 2], -1.0, None, ALU.add).then_inc(s["g_b"], 1)
                            v.wait_ge(s["g_b"], 2)
                            V.tensor_scalar(ga[:, 5], ga[:, 3], 0.0, None, ALU.is_equal).then_inc(s["g_b"], 1)
                            V.tensor_scalar(ga[:, 6], ga[:, 3], 1e-30, None, ALU.max).then_inc(s["g_b"], 1)
                            v.wait_ge(s["g_b"], 4)
                            V.reciprocal(ga[:, 3], ga[:, 6]).then_inc(s["g_b"], 1)
                            V.tensor_tensor(ga[:, 7], ga[:, 5], ga[:, 1], ALU.mult).then_inc(s["g_b"], 1)
                            v.wait_ge(s["g_b"], 6)
                            V.tensor_tensor(ga[:, 5], ga[:, 3], ga[:, 1], ALU.mult).then_inc(s["g_b"], 1)
                            v.wait_ge(s["g_b"], 7)
                            v.wait_ge(s["g_l"], 1)
                            V.tensor_tensor(ga[:, 3], ga[:, 5], ga[:, 4], ALU.mult).then_inc(s["g_b"], 1)
                            v.wait_ge(s["g_b"], 8)
                            V.tensor_tensor(ga[:, 6], ga[:, 3], ga[:, 7], ALU.add).then_inc(s["g_b"], 1)
                            v.wait_ge(s["g_b"], 9)
                            V.scalar_tensor_tensor(ga[:, 5], lg[:], 0.0, ga[:, 6], ALU.max, ALU.add)\
                                .then_inc(s["g_c"], 1)
                            V.tensor_tensor(ga[:, 3], oh[:, 0], oh[:, 1], ALU.add).then_inc(s["g_sum"], 1)
                            v.wait_ge(s["g_sum"], 1)
                            v.wait_ge(s["g_p"], 1)
                            V.tensor_tensor(cmb[:], ga[:, 6], ga[:, 3], ALU.mult).then_inc(s["g_cmb"], 1)
                            v.wait_ge(s["g_cmb"], 1)
                        else:
                            leave(e - 1)
                        if 1 <= e <= NE:
                            fill(share(e - 1, NE, F_MOE))
                    v.wait_ge(s["e_tp"], 1)
                    V.tensor_copy(cmbT[:], M[1][0:NE, :]).then_inc(s["e_ct"], 1)
                    leave(NE + 1)
                    layernorm(2, "e_ev", 2 * (NE + 2), X)

                    xt_copy(3, XT)
                    for blk in range(KC):
                        v.wait_ge(s["d_qk"], 3 + blk)
                        V.tensor_scalar(kT[:, blk, :], M[2 + blk][:, :], col("d_k")[:, blk:blk + 1], None, ALU.add)\
                            .then_inc(s["d_ev"], 1)
                    for g in range(2):
                        v.wait_ge(s["d_v"], g + 1)
                        V.tensor_tensor(v_d[:, 2 * g:2 * g + 2, :],
                                        M[g][:, :].rearrange("p (t d) -> p t d", t=2),
                                        row("d_v").unsqueeze(1).to_broadcast([P, 2, D]), ALU.add)\
                            .then_inc(s["d_ev"], 1)
                    for j in range(NT):
                        v.wait_ge(s["d_s"], j + 1)
                        V.tensor_reduce(nmax[:, j:j + 1], M[(2 + j) % 4][:, :], AX.X, ALU.max, negate=True)\
                            .then_inc(s["d_mx"], 1)
                    v.wait_ge(s["d_ev"], 4)
                    for j in range(NT):
                        v.wait_ge(s["d_ex"], j + 1)
                        V.reciprocal(rinv[:, j:j + 1], rsum[:, j:j + 1]).then_inc(s["d_rz"], 1)
                        v.wait_ge(s["d_rz"], j + 1)
                        V.tensor_scalar(v_d[:, j, :], v_d[:, j, :], rinv[:, j:j + 1], None, ALU.mult)\
                            .then_inc(s["d_vn"], 1)
                    fill(F_KEYS)
                    v.wait_ge(s["xt_ps"], 4)
                    add_result((2, 3), 4, 4)
                    layernorm(3, "ln_sum", 6, X)

                    xt_copy(4, XT)
                    v.wait_ge(s["x_q"], 3)
                    rq = const("ropeq")
                    for n, name in enumerate(("x1_q", "x1_qs")):
                        for blk in range(KC):
                            V.scalar_tensor_tensor(hs[:, n, blk * P:(blk + 1) * P],
                                                   M[0][:, (2 * n + blk) * P:(2 * n + blk + 1) * P],
                                                   col(name)[:, blk:blk + 1], rq[:, n * P:(n + 1) * P],
                                                   ALU.add, ALU.mult).then_inc(s["x_qa"], 1)
                    v.wait_ge(s["x_qa"], 4)
                    for blk in range(KC):
                        V.tensor_tensor(qT[:, blk, 0:P], hs[:, 0, blk * P:(blk + 1) * P], hs[:, 1, blk * P:(blk + 1) * P],
                                        ALU.add).then_inc(s["x_qt"], 1)
                    fill(F_ROPE)
                    cross(1, 1, 2 * NT, NT, lambda t: const("window"), F_WINDOW)
                    ot_copy(1, 1)
                    v.wait_ge(s["x_bias"], 4)
                    add_result((0,), 6, 6)
                    fill(SLOTS)
                    if back is not None:
                        v.wait_ge(s["f_out"], 16)
                    layernorm(4, "ln_sum", 7, XF)
                    v.wait_ge(s["ln_done"], 5 * NT)

            nc.all_engine_barrier()
            engines = 7 * (nc.sync,) + 5 * (nc.scalar,) + 4 * (nc.gpsimd,) + 3 * (nc.vector,) + (nc.tensor,)
            for n, each in enumerate(s.values()):
                engines[n % 20].sem_clear(each)
            nc.all_engine_barrier()

        step(0, None)
        with nc.Fori(0, B - 1) as bi:
            step(bi + 1, bi)
        step(None, B - 1)


def kernel(**inputs):
    import numpy as np
    import concourse.bacc as bacc
    from concourse.bass_utils import run_bass_kernel_spmd

    g = {k: np.asarray(v) for k, v in inputs.items()}

    def chunks(a):
        return np.ascontiguousarray(a.reshape(-1, P, a.shape[1]).transpose(1, 0, 2)).reshape(P, -1)

    e = np.arange(DH)
    third = [(np.arange(H)[:, None] * 3 * DH + n * DH + e[None, :]).ravel() for n in range(3)]
    f = np.arange(D)
    swap = (f // DH) * DH + (f % DH + DH // 2) % DH
    wqkv, bqkv = g["L0_attn_W_qkv"], g["L0_attn_b_qkv"]
    w1 = np.concatenate([g["L0_ffn_sW1"][None], g["L0_ffn_rW1"]])
    w2 = np.concatenate([g["L0_ffn_sW2"][None], g["L0_ffn_rW2"]])
    W1 = g["L1_attn_W"]
    mats = {"a_qk": np.concatenate([wqkv[:, third[0]], wqkv[:, third[1]]], 1), "a_v": wqkv[:, third[2]],
            "a_o": g["L0_attn_W_out"],
            "x0_q": g["L0_xattn_Wq"].T, "x0_k": g["L0_xattn_Wk"].T, "x0_v": g["L0_xattn_Wv"].T,
            "x0_o": g["L0_xattn_Wo"].T, "f0_r": g["L0_ffn_routing_W"].T,
            "d_q": W1[0:D].T, "d_k": W1[D:2 * D].T, "d_v": W1[2 * D:].T,
            "x1_q": g["L1_xattn_q_w"].T, "x1_qs": g["L1_xattn_q_w"][swap].T,
            "x1_k": g["L1_xattn_k_w"].T, "x1_ks": g["L1_xattn_k_w"][swap].T,
            "x1_v": g["L1_xattn_v_w"].T, "x1_o": g["L1_xattn_o_w"].T, "f1_r": g["L1_ffn_w_router"]}
    packed = {n: chunks(a) for n, a in mats.items()}
    f0 = np.stack([np.concatenate([chunks(a), b], 1) for a, b in zip(w1, w2)])
    weights = np.concatenate([packed[n] for n in W_COLS], 1)
    b1 = g["L1_attn_b"]
    row_of = {"a_v": bqkv[third[2]], "a_o": g["L0_attn_b_out"], "x0_v": g["L0_xattn_bv"], "x0_o": g["L0_xattn_bo"],
              "f0_o": g["L0_ffn_sb2"], "d_v": b1[2 * D:], "x1_v": g["L1_xattn_v_b"], "x1_o": g["L1_xattn_o_b"],
              "f0_r": g["L0_ffn_expert_bias"]}
    rows = np.concatenate([row_of[n] for n in ROW_COLS])
    col_of = {"a_qk": np.concatenate([bqkv[third[0]], bqkv[third[1]]]), "x0_q": g["L0_xattn_bq"],
              "x0_k": g["L0_xattn_bk"], "d_q": b1[0:D], "d_k": b1[D:2 * D],
              "x1_q": g["L1_xattn_q_b"], "x1_qs": g["L1_xattn_q_b"][swap],
              "x1_k": g["L1_xattn_k_b"], "x1_ks": g["L1_xattn_k_b"][swap],
              "f0_b1": np.concatenate([g["L0_ffn_sb1"][None], g["L0_ffn_rb1"]]).ravel()}
    cols = np.concatenate([col_of[n].reshape(-1, P).T for n in COL_COLS], 1)
    experts = np.stack([np.concatenate([chunks(a[:, u:u + P]), chunks(b[:, u:u + P]), c[u:u + P]], 1)
                        for a, b, c in
                        [(g["L1_ffn_sw1"], g["L1_ffn_sw3"], g["L1_ffn_sw2"])] +
                        [(g["L1_ffn_w1"][i], g["L1_ffn_w3"][i], g["L1_ffn_w2"][i]) for i in range(NE)]
                        for u in range(0, HID1, P)])

    p = np.arange(P)
    pos = (p % TR) * H + p // TR
    half = DH // 2
    freqs = (1.0 / 10000.0 ** (np.arange(half, dtype=np.float32) / half)).astype(np.float32)
    ang = np.arange(P, dtype=np.float32)[None, :] * freqs[p % half][:, None]
    sign = np.where(p % DH < half, -1.0, 1.0)[:, None]
    cos, sin = np.cos(ang), np.sin(ang) * sign
    keys = np.arange(SK)[None, :]
    const_of = {"ident": np.eye(P), "causal": np.where(pos[None, :] <= pos[:, None], 0.0, -2.0 ** 100),
                "window": np.where((keys <= p[:, None]) & (keys >= p[:, None] - 64), 0.0, -2.0 ** 100),
                "blk": p[:, None] // DH == np.arange(8)[None, :],
                "ropeq": np.concatenate([cos, sin], 1) * SCALE_X,
                "ropek": np.concatenate([cos[:, 0:SK], sin[:, 0:SK]], 1),
                "iota": np.tile(np.arange(8), (P, 1)), "expo": np.tile([-0.5] * 4 + [0.5] * 4, (P, 1))}
    consts = np.concatenate([np.asarray(const_of[n], np.float32) for n in CONST_COLS], 1)

    arrays = {"x": g["x"], "ctx": g["ctx_1024"], "mask": g["mask_Bx1xSxS2_bf0"].reshape(B, S, SK),
              "weights": weights, "rows": rows, "cols": cols, "consts": consts, "b2": g["L0_ffn_rb2"],
              "ones": np.ones((NEG, TILES * P), mybir.dt.np(BF16)), "f0": f0, "experts": experts}
    nc = bacc.Bacc("TRN2", target_bir_lowering=False, num_devices=1)
    feed, args = {}, []
    for name, a in arrays.items():
        a = np.ascontiguousarray(a)
        feed[f"in_{name}"] = a
        args.append(nc.dram_tensor(f"in_{name}", a.shape, mybir.dt.from_np(a.dtype), kind="ExternalInput").ap())
    args.append(nc.dram_tensor("result", (B, S, D), F32, kind="ExternalOutput").ap())
    args.append(nc.dram_tensor("v_scr", (S, D), F32, kind="Internal").ap())
    args.append(nc.dram_tensor("o_scr", (2, D, S), F32, kind="Internal").ap())
    args.append(nc.dram_tensor("p_scr", (3, 4, P, S), BF16, kind="Internal").ap())
    args.append(nc.dram_tensor("n_scr", (NEG, TILES, P), BF16, kind="Internal").ap())
    decoder(nc, *args)
    r = run_bass_kernel_spmd(nc, [feed], core_ids=[0])
    return r.results[0]["result"]
```
